# Optimizing a Trainium2 kernel written in Bass

```python
import numpy as np
import jax
import jax.numpy as jnp

def _softmax(x, axis=-1):
    return jax.nn.softmax(x, axis=axis)

def _gelu(x):
    return jax.nn.gelu(x, approximate=True)

def _silu(x):
    return jax.nn.silu(x)

def _sigmoid(x):
    return jax.nn.sigmoid(x)

def _layernorm(x, axis=-1, eps=1e-05):
    m = jnp.mean(x, axis=axis, keepdims=True)
    v = jnp.var(x, axis=axis, keepdims=True)
    return (x - m) / jnp.sqrt(v + eps)

def _scatter_add(tgt, idx, src, axis=0):
    return tgt.at[idx].add(src)

def _segment_sum(src, seg, n):
    return jax.ops.segment_sum(src, seg, n)
kernel_name = 'mk_seq_preln_d2_jaxref_r8_ac7c82'

def setup_inputs(seed: int=0):
    np.random.seed(seed)
    _w = jnp.asarray

    def _L0_attn_setup():
        import jax, jax.numpy as jnp
        import numpy as np
        D_MODEL = 128
        N_HEADS = 16
        D_HEAD = D_MODEL // N_HEADS
        WIN = 32
        NEG_INF = -1e+30

        def _band_mask(nb: int):
            ti = jnp.arange(WIN)[:, None]
            tj = jnp.arange(2 * WIN)[None, :]
            base = (tj >= ti + 1) & (tj <= ti + WIN)
            first = base & (tj >= WIN)
            rest = jnp.broadcast_to(base, (nb - 1, WIN, 2 * WIN))
            return jnp.concatenate([first[None], rest], axis=0)
        key = jax.random.key(seed)
        k1, k2, k3 = jax.random.split(key, 3)
        B, L = (4, 512)
        x = jax.random.normal(k1, (B, L, D_MODEL), dtype=jnp.float32)
        w_qkv = jax.random.normal(k2, (D_MODEL, 3 * D_MODEL), dtype=jnp.float32) * (1.0 / np.sqrt(D_MODEL))
        w_out = jax.random.normal(k3, (D_MODEL, D_MODEL), dtype=jnp.float32) * (1.0 / np.sqrt(D_MODEL))
        return {'x': x, 'w_qkv': w_qkv, 'w_out': w_out}
    _L0_attn_in = _L0_attn_setup()

    def _L0_ffn_setup():
        import jax, jax.numpy as jnp
        import numpy as np
        D_MODEL = 128
        D_OUT = 128
        RANK = 16
        NUM_TRUE = 8
        NUM_NULL = 2
        TOP_K = 2
        SCALING = 32.0 / 16.0
        key = jax.random.key(seed)
        ks = jax.random.split(key, 6)
        x = jax.random.normal(ks[0], (4, 512, D_MODEL), dtype=jnp.float32)
        base_w = jax.random.normal(ks[1], (D_OUT, D_MODEL), dtype=jnp.float32) / np.sqrt(D_MODEL)
        base_b = jax.random.normal(ks[2], (D_OUT,), dtype=jnp.float32) * 0.01
        gate_w = jax.random.normal(ks[3], (NUM_TRUE + NUM_NULL, D_MODEL), dtype=jnp.float32) / np.sqrt(D_MODEL)
        lora_A = jax.random.normal(ks[4], (NUM_TRUE, RANK, D_MODEL), dtype=jnp.float32) / np.sqrt(D_MODEL)
        lora_B = jax.random.normal(ks[5], (NUM_TRUE, D_OUT, RANK), dtype=jnp.float32) * 0.01
        return {'x': x, 'base_w': base_w, 'base_b': base_b, 'gate_w': gate_w, 'lora_A': lora_A, 'lora_B': lora_B}
    _L0_ffn_in = _L0_ffn_setup()

    def _L1_attn_setup():
        import jax, jax.numpy as jnp
        import numpy as np
        DIM = 128
        DIM_HEAD = 64
        N_HEADS = 16
        INNER = DIM_HEAD * N_HEADS
        LN_EPS = 1e-05

        def layer_norm(x, gamma, beta):
            mu = jnp.mean(x, axis=-1, keepdims=True)
            var = jnp.var(x, axis=-1, keepdims=True)
            return (x - mu) * jax.lax.rsqrt(var + LN_EPS) * gamma + beta

        def alibi_bias(seq, n_heads):
            n_sequence = jnp.arange(n_heads, 0, -1).astype(jnp.float32)
            head_scalars = 2.0 ** (-8.0 / n_sequence)
            idx = jnp.arange(seq)
            dist = -jnp.abs(idx[:, None] - idx[None, :]).astype(jnp.float32)
            return head_scalars[:, None, None] * dist
        key = jax.random.key(seed)
        ks = jax.random.split(key, 6)
        B, S = (2, 256)
        scale = 0.02
        return {'x': jax.random.normal(ks[0], (B, S, DIM), dtype=jnp.float32), 'ln_gamma': jnp.ones((DIM,), dtype=jnp.float32), 'ln_beta': jnp.zeros((DIM,), dtype=jnp.float32), 'Wq': jax.random.normal(ks[1], (DIM, INNER), dtype=jnp.float32) * scale, 'Wk': jax.random.normal(ks[2], (DIM, INNER), dtype=jnp.float32) * scale, 'Wv': jax.random.normal(ks[3], (DIM, INNER), dtype=jnp.float32) * scale, 'Wo': jax.random.normal(ks[4], (INNER, DIM), dtype=jnp.float32) * scale}
    _L1_attn_in = _L1_attn_setup()

    def _L1_ffn_setup():
        import jax, jax.numpy as jnp
        import numpy as np
        DIM = 128
        HIDDEN = 384
        SCALE = 1.0 / 127.0

        def _dequant(w_int, dtype):
            return w_int.astype(dtype) * jnp.asarray(SCALE, dtype)
        key = jax.random.key(seed)
        k_x, k_g, k_u, k_d = jax.random.split(key, 4)
        x = jax.random.normal(k_x, (4, 256, DIM), dtype=jnp.float32)
        w_gate = jax.random.randint(k_g, (HIDDEN, DIM), -127, 128, dtype=jnp.int32)
        w_up = jax.random.randint(k_u, (HIDDEN, DIM), -127, 128, dtype=jnp.int32)
        w_down = jax.random.randint(k_d, (DIM, HIDDEN), -127, 128, dtype=jnp.int32)
        return {'x': x, 'w_gate': w_gate, 'w_up': w_up, 'w_down': w_down}
    _L1_ffn_in = _L1_ffn_setup()
    _d = {'L0_attn_x': _L0_attn_in['x'], 'L0_attn_w_qkv': _L0_attn_in['w_qkv'], 'L0_attn_w_out': _L0_attn_in['w_out'], 'L0_ffn_base_w': _L0_ffn_in['base_w'], 'L0_ffn_base_b': _L0_ffn_in['base_b'], 'L0_ffn_gate_w': _L0_ffn_in['gate_w'], 'L0_ffn_lora_A': _L0_ffn_in['lora_A'], 'L0_ffn_lora_B': _L0_ffn_in['lora_B'], 'L1_attn_ln_gamma': _L1_attn_in['ln_gamma'], 'L1_attn_ln_beta': _L1_attn_in['ln_beta'], 'L1_attn_Wq': _L1_attn_in['Wq'], 'L1_attn_Wk': _L1_attn_in['Wk'], 'L1_attn_Wv': _L1_attn_in['Wv'], 'L1_attn_Wo': _L1_attn_in['Wo'], 'L1_ffn_w_gate': _L1_ffn_in['w_gate'], 'L1_ffn_w_up': _L1_ffn_in['w_up'], 'L1_ffn_w_down': _L1_ffn_in['w_down']}
    _x0 = _d['L0_attn_x']
    _d['L0_attn_x'] = jax.random.normal(jax.random.fold_in(jax.random.key(seed), 1), (1, 2048, 128), dtype=_x0.dtype)
    del _x0
    return _d

def reference(L0_attn_x, L0_attn_w_qkv, L0_attn_w_out, L0_ffn_base_w, L0_ffn_base_b, L0_ffn_gate_w, L0_ffn_lora_A, L0_ffn_lora_B, L1_attn_ln_gamma, L1_attn_ln_beta, L1_attn_Wq, L1_attn_Wk, L1_attn_Wv, L1_attn_Wo, L1_ffn_w_gate, L1_ffn_w_up, L1_ffn_w_down):

    def _L0_attn_ref(x, w_qkv, w_out):
        import jax, jax.numpy as jnp
        import numpy as np
        D_MODEL = 128
        N_HEADS = 16
        D_HEAD = D_MODEL // N_HEADS
        WIN = 32
        NEG_INF = -1e+30

        def _band_mask(nb: int):
            ti = jnp.arange(WIN)[:, None]
            tj = jnp.arange(2 * WIN)[None, :]
            base = (tj >= ti + 1) & (tj <= ti + WIN)
            first = base & (tj >= WIN)
            rest = jnp.broadcast_to(base, (nb - 1, WIN, 2 * WIN))
            return jnp.concatenate([first[None], rest], axis=0)
        B, L, D = x.shape
        nb = L // WIN
        qkv = (x @ w_qkv).reshape(B, L, 3, N_HEADS, D_HEAD)
        q, k, v = (qkv[:, :, 0], qkv[:, :, 1], qkv[:, :, 2])

        def to_blocks(t):
            return t.transpose(0, 2, 1, 3).reshape(B, N_HEADS, nb, WIN, D_HEAD)
        qb, kb, vb = (to_blocks(q), to_blocks(k), to_blocks(v))
        zero_blk = jnp.zeros_like(kb[:, :, :1])
        k_kv = jnp.concatenate([jnp.concatenate([zero_blk, kb[:, :, :-1]], axis=2), kb], axis=3)
        v_kv = jnp.concatenate([jnp.concatenate([zero_blk, vb[:, :, :-1]], axis=2), vb], axis=3)
        scale = 1.0 / np.sqrt(D_HEAD)
        scores = jnp.einsum('bhnqd,bhnkd->bhnqk', qb, k_kv) * scale
        scores = jnp.where(_band_mask(nb), scores, NEG_INF)
        attn = jax.nn.softmax(scores, axis=-1)
        ob = jnp.einsum('bhnqk,bhnkd->bhnqd', attn, v_kv)
        out = ob.reshape(B, N_HEADS, L, D_HEAD).transpose(0, 2, 1, 3).reshape(B, L, D)
        return out @ w_out

    def _L0_ffn_ref(x, base_w, base_b, gate_w, lora_A, lora_B):
        import jax, jax.numpy as jnp
        import numpy as np
        D_MODEL = 128
        D_OUT = 128
        RANK = 16
        NUM_TRUE = 8
        NUM_NULL = 2
        TOP_K = 2
        SCALING = 32.0 / 16.0
        xf = x.reshape(-1, x.shape[-1])
        logits = jnp.einsum('td,ed->te', xf, gate_w)
        probs = jax.nn.softmax(logits, axis=-1)
        weights, selected = jax.lax.top_k(probs, TOP_K)
        true_mask = (selected < NUM_TRUE).astype(weights.dtype)
        tw = weights * true_mask
        denom = tw.sum(axis=-1, keepdims=True)
        denom = jnp.where(denom > 0, denom, jnp.ones_like(denom))
        nw = tw / denom
        onehot = jax.nn.one_hot(selected, NUM_TRUE, dtype=nw.dtype)
        ew = jnp.einsum('tk,tke->te', nw, onehot)
        z = jnp.einsum('td,erd->ter', xf, lora_A)
        moe = jnp.einsum('ter,te,eor->to', z, ew, lora_B) * SCALING
        base = jnp.einsum('td,od->to', xf, base_w) + base_b
        out = (base + moe).reshape(x.shape[:-1] + (D_OUT,))
        return out

    def _L1_attn_ref(x, ln_gamma, ln_beta, Wq, Wk, Wv, Wo):
        import jax, jax.numpy as jnp
        import numpy as np
        DIM = 128
        DIM_HEAD = 64
        N_HEADS = 16
        INNER = DIM_HEAD * N_HEADS
        LN_EPS = 1e-05

        def layer_norm(x, gamma, beta):
            mu = jnp.mean(x, axis=-1, keepdims=True)
            var = jnp.var(x, axis=-1, keepdims=True)
            return (x - mu) * jax.lax.rsqrt(var + LN_EPS) * gamma + beta

        def alibi_bias(seq, n_heads):
            n_sequence = jnp.arange(n_heads, 0, -1).astype(jnp.float32)
            head_scalars = 2.0 ** (-8.0 / n_sequence)
            idx = jnp.arange(seq)
            dist = -jnp.abs(idx[:, None] - idx[None, :]).astype(jnp.float32)
            return head_scalars[:, None, None] * dist
        B, S, _ = x.shape
        xn = layer_norm(x, ln_gamma, ln_beta)

        def heads(t):
            return t.reshape(B, S, N_HEADS, DIM_HEAD).transpose(0, 2, 1, 3)
        q = heads(xn @ Wq)
        k = heads(xn @ Wk)
        v = heads(xn @ Wv)
        att = jnp.einsum('bhid,bhjd->bhij', q, k) / DIM_HEAD ** 0.5
        att = att + alibi_bias(S, N_HEADS)[None]
        p = jax.nn.softmax(att, axis=-1)
        out = jnp.einsum('bhij,bhjd->bhid', p, v)
        out = out.transpose(0, 2, 1, 3).reshape(B, S, INNER)
        return out @ Wo

    def _L1_ffn_ref(x, w_gate, w_up, w_down):
        import jax, jax.numpy as jnp
        import numpy as np
        DIM = 128
        HIDDEN = 384
        SCALE = 1.0 / 127.0

        def _dequant(w_int, dtype):
            return w_int.astype(dtype) * jnp.asarray(SCALE, dtype)
        wg = _dequant(w_gate, x.dtype)
        wu = _dequant(w_up, x.dtype)
        wd = _dequant(w_down, x.dtype)
        gate = jnp.einsum('bsd,hd->bsh', x, wg)
        up = jnp.einsum('bsd,hd->bsh', x, wu)
        h = jax.nn.silu(gate) * up
        return jnp.einsum('bsh,dh->bsd', h, wd)
    x = L0_attn_x
    x = x + _L0_attn_ref(_layernorm(x, axis=-1), L0_attn_w_qkv, L0_attn_w_out)
    x = x + _L0_ffn_ref(_layernorm(x, axis=-1), L0_ffn_base_w, L0_ffn_base_b, L0_ffn_gate_w, L0_ffn_lora_A, L0_ffn_lora_B)
    x = x + _L1_attn_ref(_layernorm(x, axis=-1), L1_attn_ln_gamma, L1_attn_ln_beta, L1_attn_Wq, L1_attn_Wk, L1_attn_Wv, L1_attn_Wo)
    x = x + _L1_ffn_ref(_layernorm(x, axis=-1), L1_ffn_w_gate, L1_ffn_w_up, L1_ffn_w_down)
    return x

_drawn_inputs = setup_inputs


def setup_inputs(seed=0):
    import zlib

    import numpy as np

    out = dict(_drawn_inputs(seed))
    spreads = {'L1_attn_ln_gamma': (1.0, 0.6), 'L1_attn_ln_beta': (0.0, 0.57)}
    factors = {'L0_ffn_base_b': 5.589, 'L1_attn_Wq': 8.0, 'L1_attn_Wk': 8.0}
    for name, (base, spread) in spreads.items():
        noise = np.random.default_rng([zlib.crc32(name.encode()), seed]).standard_normal(out[name].shape)
        drawn = base * np.exp(spread * noise) if base else spread * noise
        out[name] = jnp.asarray(drawn.astype(out[name].dtype))
    for name, factor in factors.items():
        out[name] = (out[name] * factor).astype(out[name].dtype)
    return out
```

```python
from contextlib import ExitStack

import concourse.bass as bass
import numpy as np
from concourse import mybir

F32 = mybir.dt.float32
F16 = mybir.dt.float16
BF16 = mybir.dt.bfloat16
I32 = mybir.dt.int32
U16 = mybir.dt.uint16
ALU = mybir.AluOpType
ACT = mybir.ActivationFunctionType
AX = mybir.AxisListType

P = 128
T = 2048
NT = T // P
EPS = 1e-5

W0 = 32
H0 = 16
D0 = P // H0
G0 = 4
HG = H0 // G0
NB = T // (2 * W0)
SC0 = float(D0) ** -0.5
VW = HG * D0 + 1

NE, NTRUE, RANK = 10, 8, 16
NZ = NTRUE * RANK + NE
LORA_SCALE = 2.0

H1 = 16
D1 = 64
NP = H1 // 2
HALF = 1024
CENTRE = T // 2
TW = 2 * T - P
ROW_M = 64
ROW_A = 96
NA = 6
M_UNIT = 64.0

HID = 384
NH = HID // P
WSCALE = 1.0 / 127.0

POOL_SUMS = [1, 2, 4, 5, 6, 8, 9, 10, 12, 13, 14]
DVE_SUMS = [3, 7, 11, 15]


def bcast(ap, dim, n):
    a = ap.unsqueeze(dim)
    shape = list(a.shape)
    shape[dim] = n
    return a.broadcast_to(shape)


def prep_items():
    items = [("proj", i, c) for i in range(2) for c in range(2)]
    items += [("value", 0, 0), ("value", 1, 0)]
    for h in range(2):
        items += [("max", h, t, kh) for t in range(NT) for kh in range(2)]
        items.append(("mrow", h))
    return items


def main_schedule():
    prep = prep_items()
    steps = [[] for _ in range(2 * NT)]
    tail = {1: ("den",), 2: ("out",), NT + 1: ("den",), NT + 2: ("out",)}
    for s, k in ((1, 1), (2, 1), (3, 2), (4, 1), (5, 1)):
        steps[s] += prep[sum(map(len, steps)):][:k]
    rest = prep[6:]
    first = 7
    slots = 2 * NT - first
    at = 0
    for s in range(first, 2 * NT):
        to = (len(rest) * (s - first + 1) + slots - 1) // slots
        steps[s] += rest[at:to]
        at = to
    for s, item in tail.items():
        steps[s].append(item)
    return steps


PREP = prep_items()
SCHED = main_schedule()
NPREP = len(PREP)
NMAIN = sum(len(s) for s in SCHED)
LAST_VALUE = PREP.index(("value", 1, 0))
LAST_PROJ = PREP.index(("proj", 1, 1))


def place_in_main(item):
    flat = [x for s in SCHED for x in s]
    return flat.index(item)


def build(nc, io):
    ctx = ExitStack()
    with ctx:
        def sb(name, shape, dt):
            return ctx.enter_context(nc.sbuf_tensor(name, shape, dt))

        def sem(name):
            return ctx.enter_context(nc.semaphore(name))

        ps = ctx.enter_context(nc.psum_tensor("ps", [P, 8, 512], F32))

        x = sb("x", [P, NT, P], F32)
        ident = sb("ident", [P, P], F32)
        stat = sb("stat", [P, 8, NT], F32)
        xT_hi = sb("xT_hi", [P, W0 + T], F16)
        xT_lo = sb("xT_lo", [P, W0 + T], F16)
        wide = sb("wide", [P, T], F32)

        QA = sb("QA", [P, 2, 2, T], F16)
        KA = sb("KA", [P, 2, 2, T], F16)
        QB = sb("QB", [P, 2, 2, T], F16)
        KL = sb("KL", [P, 2, 2, T], F16)
        KR = sb("KR", [P, 2, 2, T], F16)
        arena = sb("arena", [P, 16384], F32)
        A16 = arena[:, :].bitcast(F16)

        HI = A16[:, 0:4096].rearrange("p (i t) -> p i t", i=2)
        LO = A16[:, 4096:8192].rearrange("p (i t) -> p i t", i=2)
        V1 = arena[:, 4096:8192].rearrange("p (a j d) -> p a j d", a=2, j=NT)
        Pr = arena[:, 8192:12288].rearrange("p (h a q) -> p h a q", h=2, a=2)
        accP = arena[:, 12288:14336].rearrange("p (h q) -> p h q", h=2)
        accD = arena[:, 14336:16384].rearrange("p (h q) -> p h q", h=2)
        o_raw = sb("o_raw", [P, HALF], F32)
        o_nrm = sb("o_nrm", [P, HALF], F32)
        dist = sb("dist", [P, TW], F16)
        dist_h = sb("dist_h", [P, TW], F16)
        junk = sb("junk", [P, HALF], F16)
        diag = sb("diag", [P, 2, 2, 2, P], F16)
        relu_w = sb("relu_w", [P, P], F16)
        w1 = sb("w1", [P, 3, P], F32)
        w1_hi = sb("w1_hi", [P, 3, P], F16)
        w1_lo = sb("w1_lo", [P, 3, P], F16)
        wo1 = sb("wo1", [P, 2, P], F32)
        slope = sb("slope", [P, 2, 2], F32)
        mx2 = sb("mx2", [P, 2, NT, 2], F32)
        nm = sb("nm", [P, 2, 2, NT], F32)
        bmask = sb("bmask", [P, NT], F32)
        tick = sb("tick", [P, 1], F32)
        ones1 = sb("ones1", [P, D1], F32)
        gb = sb("gb", [P, 2], F32)

        kT = A16[:, 0:2 * (W0 + T)].rearrange("p (a t) -> p a t", a=2)
        qT = A16[:, 4160:4160 + 2 * T].rearrange("p (a t) -> p a t", a=2)
        o1 = 8256
        nv = NB * G0 * 2 * VW
        v_hi = A16[:, o1:o1 + nv].rearrange("p (b g a w) -> p b g a w", b=NB, g=G0, a=2)
        v_lo = A16[:, o1 + nv:o1 + 2 * nv].rearrange("p (b g a w) -> p b g a w", b=NB, g=G0, a=2)
        R32 = QA[:, 0].rearrange("p h t -> p (h t)").bitcast(F32)
        R32b = QA[:, 1].rearrange("p h t -> p (h t)").bitcast(F32)
        RK = KA[:, 0].rearrange("p h t -> p (h t)")
        RK2 = KA[:, 1].rearrange("p h t -> p (h t)").bitcast(F32)
        sub_s = R32[:, 0:1024].rearrange("p (a n) -> p a n", a=2)
        exp_s = R32[:, 1024:2048].rearrange("p (a n) -> p a n", a=2)
        pT = RK[:, 0:2048].rearrange("p (a c n) -> p a c n", a=2, c=2)
        qm = RK[:, 2048:4096].rearrange("p (c n) -> p c n", c=2)
        qm_lo = R32b[:, 0:1024].bitcast(F16).rearrange("p (c n) -> p c n", c=2)
        qm_hi = R32b[:, 1024:2048].bitcast(F16).rearrange("p (c n) -> p c n", c=2)
        om1 = RK2[:, 0:256]
        om = RK2[:, 256:768].rearrange("p (a n) -> p a n", a=2)
        oT = RK2[:, 768:896]
        mx0 = RK2[:, 896:904]
        rc0 = RK2[:, 904:912]

        QBh = QB[:, :, :, :].rearrange("p a h t -> p (a h t)")
        QBf = QBh.bitcast(F32)
        mask0 = QBf[:, 0:512].bitcast(BF16).rearrange("p (v n) -> p v n", v=2)
        ident_b = QBf[:, 512:576].bitcast(BF16)
        hmask = QBh[:, 1152:1152 + H0 * W0]
        gmask = QBf[:, 832:864]
        sel = QBf[:, 864:896]
        w0 = QBf[:, 896:1280]
        w0_hi = QBh[:, 2560:2944]
        w0_lo = QBh[:, 2944:3328]
        wo0 = QBf[:, 1664:1792]
        wz = QBf[:, 1792:1792 + NZ]
        wbase = QBf[:, 1936:2064]
        wlb = QBf[:, 2064:2192]
        bias0 = QBf[:, 2192:2320]
        rank10 = QBf[:, 2320:2330]

        ffT = arena[:, 0:2048]
        z = arena[:, 2048:2048 + NT * NZ].rearrange("p (t n) -> p t n", t=NT)
        zw = arena[:, 4352:6400].rearrange("p (t n) -> p t n", t=NT)
        zwT = arena[:, 6400:8448]
        rt = arena[:, 8448:8448 + 8 * NT * NE].rearrange("p (k t e) -> p k t e", k=8, t=NT)
        rs = arena[:, 10240:10240 + 8 * NT].rearrange("p (k t) -> p k t", k=8)

        wgi = arena[:, 0:HID].bitcast(I32)
        wui = arena[:, HID:2 * HID].bitcast(I32)
        wdi = arena[:, 2 * HID:3 * HID].bitcast(I32)
        wg = A16[:, 4096:4096 + HID]
        wu = A16[:, 4096 + HID:4096 + 2 * HID]
        wd = arena[:, 2560:2560 + HID].rearrange("p (k d) -> p k d", k=NH)
        silu = arena[:, 4096:4096 + 2 * 512].rearrange("p (a n) -> p a n", a=2)
        hid = arena[:, 6144:6144 + NH * T].rearrange("p (k t) -> p k t", k=NH)

        ld0 = sem("ld0")
        ldc = sem("ldc")
        dv = sem("dv")
        ln_c, ln_sq, ln_v, ln_sd = sem("ln_c"), sem("ln_sq"), sem("ln_v"), sem("ln_sd")
        ln_x = sem("ln_x")
        tr = sem("tr")
        tr_ev = sem("tr_ev")
        gbt = sem("gbt")
        hi_ev = sem("hi_ev")
        w_split = sem("w_split")
        init = sem("init")
        qk0, qk0_hi, qk0_ev = sem("qk0"), sem("qk0_hi"), sem("qk0_ev")
        v0, v0_hi, v0_ev = sem("v0"), sem("v0_hi"), sem("v0_ev")
        qmh, qml, s0, m0, sub0, e0 = (sem(n) for n in ("qmh", "qml", "s0", "m0", "sub0", "e0"))
        t0, hi0, lo0, pv0, rc_s, om1_s, om0 = (sem(n) for n in ("t0", "hi0", "lo0", "pv0", "rc_s", "om1_s", "om0"))
        sel0, ot0, y0, x0 = (sem(n) for n in ("sel0", "ot0", "y0", "x0"))
        z_mm, z_ev, r_exp, r_exp_in, zw_s, zt_mm, zt_ev, f_mm, f_ev, xb_s = (
            sem(n) for n in ("z_mm", "z_ev", "r_exp", "r_exp_in", "zw_s", "zt_mm", "zt_ev", "f_mm", "f_ev", "xb_s"))
        ldrow = sem("ldrow")
        ldp = sem("ldp")
        ldt = sem("ldt")
        ldw = sem("ldw")
        w1s = sem("w1s")
        w1c = sem("w1c")
        mx_full, mx_free = sem("mx_full"), sem("mx_free")
        hi_done = sem("hi_done")
        asm = [sem("asm_a"), sem("asm_b")]
        asm_kq = sem("asm_kq")
        ts_done, nm1, nm_done = sem("ts_done"), sem("nm1"), sem("nm_done")
        qk_done, exp_done, pv_done, pv_evac = (sem(n) for n in ("qk_done", "exp_done", "pv_done", "pv_evac"))
        sum_pool, sum_dve, comb_done = sem("sum_pool"), sem("sum_dve"), sem("comb_done")
        den_rc, o_done = sem("den_rc"), sem("o_done")
        yt_mm, x3_s = sem("yt_mm"), sem("x3_s")
        wcv, gu_mm, silu_s, h_s, dn_mm, x4_s, st = (
            sem(n) for n in ("wcv", "gu_mm", "silu_s", "h_s", "dn_mm", "x4_s", "st"))

        LD0 = 12
        block = ctx.enter_context(nc.Block())

        MX = ps[:, 6:8, :].rearrange("p b n -> p (b n)")
        S1 = [ps[:, 2 * h:2 * h + 2, :].rearrange("p b n -> p (b n)") for h in range(2)]
        PV = ps[:, 4:6, :].rearrange("p b n -> p (b n)")

        @block.sync
        def _(sp):
            sp.dma_start(x[:, :, :], io["x"].rearrange("o (t p) d -> p (o t) d", p=P)).then_inc(ld0, 16)
            for dst, name in ((w0, "w_qkv"), (wo0, "w_out"), (ident, "ident"), (ident_b.bitcast(U16), "ident_b"),
                              (hmask, "hmask"), (gmask, "gmask"), (sel, "sel"), (wz, "wz"),
                              (wbase, "wbase"), (wlb, "wlb")):
                sp.dma_start(dst[:, :], io[name]).then_inc(ld0, 16)
            sp.dma_start(mask0.bitcast(U16), io["mask0"]).then_inc(ld0, 16)
            for dst, name in ((dist, "dist"), (relu_w, "relu_w"), (gb, "gb"), (bias0, "bias0"),
                              (rank10, "rank10"), (bmask, "bmask")):
                sp.dma_start(dst[:, :], io[name]).then_inc(ldc, 16)

            sp.wait_ge(init, 3)
            for a in range(2):
                for h in range(2):
                    sp.dma_start(QB[ROW_A:ROW_A + NA, a, h, :], io["pos_rows"]).then_inc(ldrow, 16)

            def load_pair(m, a):
                sp.wait_ge(w1c, m * 2 + 1)
                sp.wait_ge(init, 3)
                sp.dma_start(w1[:, :, :], io["w1"][m]).then_inc(ldp, 16)
                if not isinstance(m, int):
                    sp.wait_ge(qk_done, m * (4 * NT) + (2 - 4 * NT))
                    sp.wait_ge(ts_done, m * 2)
                sp.wait_ge(init, 3)
                for h in range(2):
                    sp.dma_start(KL[ROW_A:ROW_A + NA, a, h, :], io["alibi_l"][m, h]).then_inc(ldt, 16)
                    sp.dma_start(KR[ROW_A:ROW_A + NA, a, h, :], io["alibi_r"][m, h]).then_inc(ldt, 16)
                    sp.dma_start(diag[:, a, h, :, :], io["diag"][m, h]).then_inc(ldt, 16)
                sp.dma_start(slope[:, a, :], io["slope"][m]).then_inc(ldt, 16)

            def load_wo(m, a):
                sp.dma_start(wo1[:, a, :], io["wo1"][m]).then_inc(ldw, 16)

            def assemble(m, a, g0, g):
                parts = settled(sp, m * 4 + 4)
                consumed = settled(sp, g0 + 2 + g)
                sp.wait_ge(init, 3)
                sp.wait_ge(hi_done, parts)
                sp.wait_ge(mx_free, consumed)
                for h in range(2):
                    rows = slice(64 * h, 64 * h + 64)
                    sp.dma_start(QA[0:64, a, h, :], HI[rows, 0, :]).then_inc(asm[h], 16)
                    sp.dma_start(QA[64:128, a, h, :], LO[rows, 0, :]).then_inc(asm[h], 16)
                    sp.dma_start(KA[0:64, a, h, :], HI[rows, 1, :]).then_inc(asm[h], 16)
                    sp.dma_start(KA[64:128, a, h, :], HI[rows, 1, :]).then_inc(asm[h], 16)
                for h in range(2):
                    rows = slice(64 * h, 64 * h + 64)
                    sp.dma_start(QB[0:64, a, h, :], HI[rows, 0, :]).then_inc(asm_kq, 16)
                    sp.dma_start(KL[0:64, a, h, :], LO[rows, 1, :]).then_inc(asm_kq, 16)
                    sp.dma_start(KR[0:64, a, h, :], LO[rows, 1, :]).then_inc(asm_kq, 16)

            load_pair(0, 0)
            load_wo(0, 0)
            assemble(0, 0, 0, LAST_PROJ)
            with sp.Fori(0, NP // 2) as it:
                for a in range(2):
                    m = it * 2 + (a + 1)
                    load_pair(m, 1 - a)
                    sp.wait_ge(mx_free, (it * 2 + a) * NMAIN + (NPREP + 2 + place_in_main(("out",))))
                    sp.wait_ge(init, 3)
                    load_wo(m, 1 - a)
                    assemble(m, 1 - a, (it * 2 + a) * NMAIN + NPREP, place_in_main(("proj", 1, 1)))

            sp.wait_ge(yt_mm, 1)
            for sem_, per in ((asm[0], 64), (asm[1], 64), (asm_kq, 96)):
                sp.wait_ge(sem_, per * (NP + 1))
            for dst, name in ((wgi, "w_gate"), (wui, "w_up")):
                sp.dma_start(dst, io[name]).then_inc(wcv, 16)
            sp.dma_start(wdi.rearrange("p (k d) -> p k d", k=NH),
                         io["w_down"].rearrange("(k p) d -> p k d", p=P)).then_inc(wcv, 16)
            out_v = io["out"].rearrange("o (t p) d -> p (o t) d", p=P)
            for c in range(4):
                sp.wait_ge(x4_s, c + 1)
                sp.dma_start(out_v[:, 4 * c:4 * c + 4, :], x[:, 4 * c:4 * c + 4, :]).then_inc(st, 16)
            sp.wait_ge(st, 64)

        @block.tensor
        def _(pe):
            def transposes(k, src, bank0=0):
                for c in range(4):
                    for j in range(4):
                        last = nc.tensor.transpose(ps[:, bank0 + c, j * P:(j + 1) * P],
                                                   src[:, 4 * c + j, :], ident[:, :])
                    last.then_inc(tr, 1)

            def three_parts(out, a, b, start=True, stop=True):
                nc.tensor.matmul(out, a[0], b[0], start=start, stop=False)
                nc.tensor.matmul(out, a[1], b[0], start=False, stop=False)
                return nc.tensor.matmul(out, a[0], b[1], start=False, stop=stop)

            xn = wide[:, :].rearrange("p (t d) -> p t d", t=NT)
            pe.wait_ge(ld0, 16 * LD0)
            pe.wait_ge(ln_x, 1)
            transposes(0, xn)
            pe.wait_ge(w_split, 2)
            for i in range(2):
                for c in range(4):
                    if i == 0:
                        pe.wait_ge(tr_ev, c + 1)
                    if i == 1:
                        pe.wait_ge(qk0_ev, c + 1)
                    cols = slice(W0 + 512 * c, W0 + 512 * c + 512)
                    wc = slice(P * i, P * i + P)
                    three_parts(ps[:, 4 + c, :], (w0_hi[:, wc], w0_lo[:, wc]),
                                (xT_hi[:, cols], xT_lo[:, cols])).then_inc(qk0, 1)
            pe.wait_ge(init, 1)
            wc = slice(2 * P, 3 * P)
            for g in range(NB // 4):
                if g >= 4:
                    pe.wait_ge(v0_ev, g - 3)
                for j in range(4):
                    b = 4 * g + j
                    win = [xp[:, 2 * W0 * b:2 * W0 * b + 3 * W0] for xp in (xT_hi, xT_lo)]
                    out = ps[:, g % 4, j * P:(j + 1) * P]
                    for blk in range(2):
                        o = ps[64 * blk:64 * blk + 64, g % 4, j * P:(j + 1) * P]
                        w = [v[:, W0 * blk:W0 * blk + 2 * W0] for v in win]
                        last = three_parts(o, w, (w0_hi[:, wc], w0_lo[:, wc]))
                last.then_inc(v0, 1)

            def attn0(k, on, a, first):
                if on[0]:
                    b = k
                    pe.wait_ge(qmh, b + 1)
                    pe.wait_ge(qml, b + 1)
                    if not first or a >= 2:
                        pe.wait_ge(sub0, b - 1)
                    bank = a % 2
                    nc.tensor.matmul(ps[:, bank, :], ident_b[:, :], mask0[:, 1 if (first and a == 0) else 0, :],
                                     start=True, stop=False, skip_group_check=True)
                    for blk in range(2):
                        col = b * (2 * W0) + W0 * blk
                        kh = kT[:, 0, bass.ds(col, 2 * W0)]
                        kl = kT[:, 1, bass.ds(col, 2 * W0)]
                        for g in range(G0):
                            o = ps[:, bank, g * P + 64 * blk:g * P + 64 * blk + 64]
                            qs = slice(blk * 512 + g * P, blk * 512 + g * P + P)
                            end = blk == 1 and g == G0 - 1
                            nc.tensor.matmul(o, qm_hi[:, bank, qs], kh, start=False, stop=False, skip_group_check=True)
                            nc.tensor.matmul(o, qm_lo[:, bank, qs], kh, start=False, stop=False, skip_group_check=True)
                            last = nc.tensor.matmul(o, qm_hi[:, bank, qs], kl, start=False, stop=end,
                                                    skip_group_check=True)
                    last.then_inc(s0, 1)
                if on[1]:
                    b = k - 1
                    par = (a + 1) % 2
                    pe.wait_ge(e0, b + 1)
                    if not first or a >= 3:
                        pe.wait_ge(lo0, b - 1)
                    for g in range(G0):
                        last = nc.tensor.transpose(ps[:, 2 + par, g * P:(g + 1) * P],
                                                   exp_s[:, par, g * P:(g + 1) * P], ident[:, :])
                    last.then_inc(t0, 1)
                if on[2]:
                    b = k - 2
                    par = a % 2
                    pe.wait_ge(lo0, b + 1)
                    if not first or a >= 4:
                        pe.wait_ge(om0, b - 1)
                    for g in range(G0):
                        o = ps[:, 4 + par, g * 2 * VW:(g + 1) * 2 * VW]
                        pp = [pT[:, par, i, g * P:(g + 1) * P] for i in range(2)]
                        if isinstance(b, int):
                            vv = [v[:, b, g, :, :] for v in (v_hi, v_lo)]
                        else:
                            vv = [v[:, bass.ds(b, 1), g, :, :] for v in (v_hi, v_lo)]
                        vv = [v.rearrange("p a w -> p (a w)") if isinstance(b, int)
                              else v.rearrange("p b a w -> p (b a w)") for v in vv]
                        last = three_parts(o, pp, vv)
                    last.then_inc(pv0, 1)
                if on[3]:
                    b = k - 3
                    par = (a + 1) % 2
                    pe.wait_ge(om0, b + 1)
                    if not (first and a == 3):
                        pe.wait_ge(ot0, b)
                    for blk in range(2):
                        last = nc.tensor.matmul(ps[:, 6, blk * W0:(blk + 1) * W0],
                                                om[:, par, blk * P:(blk + 1) * P], sel[:, :], start=True, stop=True)
                    last.then_inc(sel0, 1)
                if on[4] and a % 2 == 0:
                    tile = on[4][0]
                    pe.wait_ge(ot0, tile * 2 + 2)
                    if not on[4][1]:
                        pe.wait_ge(x0, tile)
                    nc.tensor.matmul(ps[:, 7, 0:P], oT[:, :], wo0[:, :], start=True, stop=True).then_inc(y0, 1)

            run_attn0(pe, attn0)

            pe.wait_ge(ln_x, 2)
            transposes(1, xn)
            for c in range(8):
                pe.wait_ge(tr_ev, 4 + c // 2 + 1)
                if c >= 4:
                    pe.wait_ge(z_ev, c - 3)
                for j in range(2):
                    tt = 2 * c + j
                    last = nc.tensor.matmul(ps[:, 4 + c % 4, j * NZ:(j + 1) * NZ],
                                            ffT[:, tt * P:(tt + 1) * P], wz[:, :], start=True, stop=True)
                last.then_inc(z_mm, 1)
            pe.wait_ge(zw_s, 1)
            for c in range(4):
                for j in range(4):
                    last = nc.tensor.transpose(ps[:, c, j * P:(j + 1) * P], zw[:, 4 * c + j, :], ident[:, :])
                last.then_inc(zt_mm, 1)
            for c in range(4):
                pe.wait_ge(zt_ev, c + 1)
                for j in range(4):
                    tt = 4 * c + j
                    o = ps[:, 4 + c, j * P:(j + 1) * P]
                    nc.tensor.matmul(o, ffT[:, tt * P:(tt + 1) * P], wbase[:, :], start=True, stop=False)
                    last = nc.tensor.matmul(o, zwT[:, tt * P:(tt + 1) * P], wlb[:, :], start=False, stop=True)
                last.then_inc(f_mm, 1)

            pe.wait_ge(ln_x, 4)
            transposes(2, xn)
            pe.wait_ge(tr_ev, 12)

            def item(it_, a, g0, g, half):
                kind = it_[0]
                if kind == "proj":
                    if it_[1:] == (0, 0):
                        pe.wait_ge(w1s, half["m"] * 2 + 2)
                    pe.wait_ge(mx_free, g0 + 1 + g)
                    _, i, c = it_
                    for n in range(2):
                        cols = slice(W0 + HALF * c + 512 * n, W0 + HALF * c + 512 * n + 512)
                        last = three_parts(MX[:, 512 * n:512 * n + 512], (w1_hi[:, i, :], w1_lo[:, i, :]),
                                           (xT_hi[:, cols], xT_lo[:, cols]))
                elif kind == "value":
                    pe.wait_ge(mx_free, g0 + 1 + g)
                    for j in range(8):
                        tt = 8 * it_[1] + j
                        cols = slice(W0 + P * tt, W0 + P * tt + P)
                        last = three_parts(MX[:, P * j:P * j + P], (xT_hi[:, cols], xT_lo[:, cols]),
                                           (w1_hi[:, 2, :], w1_lo[:, 2, :]))
                elif kind == "max":
                    _, h, tt, kh = it_
                    if tt == 0 and kh == 0:
                        pe.wait_ge(asm[h], half["m"] * 64 + 64)
                    pe.wait_ge(mx_free, g0 + 1 + g)
                    for n in range(2):
                        c0 = HALF * kh + 512 * n
                        last = nc.tensor.matmul(MX[:, 512 * n:512 * n + 512], QA[:, a, h, tt * P:(tt + 1) * P],
                                                KA[:, a, h, c0:c0 + 512], start=True, stop=True)
                elif kind == "mrow":
                    pe.wait_ge(nm_done, half["m"] * 2 + (it_[1] + 1))
                    pe.wait_ge(mx_free, g0 + 1 + g)
                    last = nc.tensor.matmul(MX[ROW_M:ROW_M + NT, 0:P], nm[:, 1, it_[1], :], ident[:, :],
                                            start=True, stop=True)
                elif kind == "den":
                    pe.wait_ge(comb_done, half["H"] * 2 + 2)
                    pe.wait_ge(mx_free, g0 + 1 + g)
                    for n in range(2):
                        cs = slice(512 * n, 512 * n + 512)
                        nc.tensor.matmul(MX[0:64, cs], ones1[:, :], accD[:, 0, cs], start=True, stop=True)
                        last = nc.tensor.matmul(MX[64:128, cs], ones1[:, :], accD[:, 1, cs], start=True, stop=True)
                elif kind == "out":
                    if half["wo_load"] is not None:
                        pe.wait_ge(ldw, half["wo_load"] * 16 + 16)
                    pe.wait_ge(o_done, half["H"] + 1)
                    pe.wait_ge(mx_free, g0 + 1 + g)
                    for n in range(2):
                        cs = slice(512 * n, 512 * n + 512)
                        last = nc.tensor.matmul(MX[:, cs], wo1[:, half["wo"], :], o_nrm[:, cs], start=True, stop=True)
                last.then_inc(mx_full, 1)

            def scores(a, h, Q, J):
                key = slice(J * P, J * P + P)
                for n in range(2):
                    q0 = HALF * Q + 512 * n
                    S = S1[h]
                    right = min(max(J - q0 // P, 0), 4)
                    on_diag = 0 <= J - q0 // P < 4
                    nc.tensor.matmul(S[:, 512 * n:512 * n + 512], KA[:, a, h, key], QA[:, a, h, q0:q0 + 512],
                                     start=True, stop=False, skip_group_check=True)
                    if right:
                        last = nc.tensor.matmul(S[:, 512 * n:512 * n + right * P], KR[:, a, h, key],
                                                QB[:, a, h, q0:q0 + right * P], start=False,
                                                stop=right == 4, skip_group_check=True)
                    if right < 4:
                        last = nc.tensor.matmul(S[:, 512 * n + right * P:512 * n + 512], KL[:, a, h, key],
                                                QB[:, a, h, q0 + right * P:q0 + 512], start=False,
                                                stop=not on_diag, skip_group_check=True)
                    if on_diag:
                        d = 512 * n + right * P
                        for part in range(2):
                            last = nc.tensor.matmul(S[:, d:d + P], relu_w[:, :], diag[:, a, h, part, :],
                                                    start=False, stop=part == 1, skip_group_check=True)
                return last

            def values(a, J):
                for n in range(2):
                    cs = slice(512 * n, 512 * n + 512)
                    nc.tensor.matmul(PV[0:64, cs], V1[:, a, J, 0:64], Pr[:, 0, J % 2, cs],
                                     start=J == 0, stop=J == NT - 1)
                    last = nc.tensor.matmul(PV[64:128, cs], V1[:, a, J, 64:128], Pr[:, 1, J % 2, cs],
                                            start=J == 0, stop=J == NT - 1)
                last.then_inc(pv_done, 1)

            def tensor_main(it, a):
                n = it * 2 + a
                g0 = n * NMAIN + NPREP
                g = 0
                for s in range(2 * NT):
                    Q, J = divmod(s, NT)
                    H = it * 4 + (2 * a + Q)
                    G = H * NT + J
                    if s == 0:
                        pe.wait_ge(mx_free, g0 + 1)
                        pe.wait_ge(asm_kq, n * 96 + 96)
                        pe.wait_ge(ldt, n * 112 + 112)
                    for h in range(2):
                        pe.wait_ge(exp_done, G * 2 + (h + 1))
                        scores(a, h, Q, J).then_inc(qk_done, 1)
                    todo = list(SCHED[s])
                    info = {"m": n + 1, "H": H, "wo": (1 - a) if Q == 0 else a,
                            "wo_load": n if Q else None}
                    if J == NT - 1:
                        for i_ in todo:
                            item(i_, 1 - a, g0, g, info)
                            g += 1
                        todo = []
                    for JJ in ([J - 1] if J else []) + ([J] if J == NT - 1 else []):
                        if JJ == 0:
                            pe.wait_ge(pv_evac, H + 1)
                        pe.wait_ge(exp_done, (H * NT + JJ) * 2 + 4)
                        values(a, JJ)
                    for i_ in todo:
                        item(i_, 1 - a, g0, g, info)
                        g += 1

            for g, i_ in enumerate(PREP):
                item(i_, 0, 0, g, {"m": 0})
            pe.wait_ge(ldrow, 16 * 4)
            with pe.Fori(0, NP // 2) as it:
                for a in range(2):
                    tensor_main(it, a)
            g0 = NPREP + NP * NMAIN
            info = {"H": 2 * NP, "wo": 1, "wo_load": None}
            item(("den",), 0, g0, 0, info)
            item(("out",), 0, g0, 1, info)
            pe.wait_ge(mx_free, g0 + 3)
            for c in range(4):
                for j in range(4):
                    tt = 4 * c + j
                    last = nc.tensor.transpose(ps[:, c, j * P:(j + 1) * P], wide[:, tt * P:(tt + 1) * P], ident[:, :])
                last.then_inc(yt_mm, 1)

            pe.wait_ge(ln_x, 5)
            transposes(3, xn)
            pe.wait_ge(w_split, 5)
            for c in range(4):
                pe.wait_ge(tr_ev, 12 + c + 1)
                cols = slice(W0 + 512 * c, W0 + 512 * c + 512)
                for k in range(NH):
                    u = NH * c + k
                    if u >= 2:
                        pe.wait_ge(h_s, u - 1)
                    for i, w in enumerate((wg, wu)):
                        o = ps[:, 4 + 2 * (u % 2) + i, :]
                        nc.tensor.matmul(o, w[:, k * P:(k + 1) * P], xT_hi[:, cols], start=True, stop=False)
                        last = nc.tensor.matmul(o, w[:, k * P:(k + 1) * P], xT_lo[:, cols], start=False, stop=True)
                    last.then_inc(gu_mm, 1)
                if c:
                    down(pe, nc, c - 1, ps, hid, wd, h_s, dn_mm)
            down(pe, nc, 3, ps, hid, wd, h_s, dn_mm)

        @block.scalar
        def _(act):
            def norm(k):
                act.wait_ge(ln_c, k + 1)
                nc.scalar.activation(wide[:, :], xc_of(k), ACT.Square).then_inc(ln_sq, 1)
                act.wait_ge(ln_v, k + 1)
                nc.scalar.activation(stat[:, 4, :], stat[:, 3, :], ACT.Sqrt).then_inc(ln_sd, 1)

            def xc_of(k):
                return xc_view

            xc_view = KR[:, 0].rearrange("p h t -> p (h t)").bitcast(F32)

            norm(0)
            for c in range(4):
                act.wait_ge(tr, c + 1)
                nc.scalar.copy(xT_hi[:, W0 + 512 * c:W0 + 512 * c + 512], ps[:, c, :]).then_inc(hi_ev, 1)
            for i in range(2):
                dst = (qT[:, 0, :], kT[:, 0, W0:])[i]
                for c in range(4):
                    act.wait_ge(qk0, 4 * i + c + 1)
                    nc.scalar.copy(dst[:, 512 * c:512 * c + 512], ps[:, 4 + c, :]).then_inc(qk0_hi, 1)
            act.wait_ge(init, 2)
            for g in range(NB // 4):
                act.wait_ge(v0, g + 1)
                for blk in range(2):
                    rows = slice(64 * blk, 64 * blk + 64)
                    src = ps[rows, g % 4, :].rearrange("p (b g w) -> p (b g) w", b=4, g=G0)
                    dst = v_hi[rows, 4 * g:4 * g + 4, :, blk, 0:HG * D0].rearrange("p b g w -> p (b g) w")
                    last = nc.scalar.copy(dst, src)
                last.then_inc(v0_hi, 1)

            def attn0(k, on, a, first):
                if on[0]:
                    b = k
                    act.wait_ge(sub0, b + 1)
                    if not first or a >= 2:
                        act.wait_ge(t0, b - 1)
                    nc.scalar.activation(exp_s[:, a % 2, :], sub_s[:, a % 2, :], ACT.Exp, scale=SC0).then_inc(e0, 1)
                if on[1]:
                    b = k - 1
                    par = (a + 1) % 2
                    act.wait_ge(t0, b + 1)
                    if not first or a >= 3:
                        act.wait_ge(pv0, b - 1)
                    nc.scalar.copy(pT[:, par, 0, :], ps[:, 2 + par, :]).then_inc(hi0, 1)
                if on[3]:
                    b = k - 3
                    par = (a + 1) % 2
                    act.wait_ge(sel0, b + 1)
                    tile, is_first = on[3]
                    if par == 0 and not is_first:
                        act.wait_ge(y0, tile)
                    nc.scalar.copy(oT[:, 64 * par:64 * par + 64], ps[:, 6, 0:64]).then_inc(ot0, 1)

            run_attn0(act, attn0)

            norm(1)
            for c in range(4):
                act.wait_ge(tr, 4 + c + 1)
                nc.scalar.copy(ffT[:, 512 * c:512 * c + 512], ps[:, c, :]).then_inc(tr_ev, 1)
            for c in range(8):
                act.wait_ge(z_mm, c + 1)
                nc.scalar.copy(z[:, 2 * c:2 * c + 2, :].rearrange("p t n -> p (t n)"),
                               ps[:, 4 + c % 4, 0:2 * NZ]).then_inc(z_ev, 1)
            act.wait_ge(r_exp_in, 1)
            nc.scalar.activation(rt[:, 1].rearrange("p t e -> p (t e)"), rt[:, 0].rearrange("p t e -> p (t e)"),
                                 ACT.Exp).then_inc(r_exp, 1)
            for c in range(4):
                act.wait_ge(zt_mm, c + 1)
                nc.scalar.copy(zwT[:, 512 * c:512 * c + 512], ps[:, c, :]).then_inc(zt_ev, 1)

            norm(2)
            norm(3)
            for c in range(4):
                act.wait_ge(gbt, c + 1)
                nc.scalar.copy(xT_hi[:, W0 + 512 * c:W0 + 512 * c + 512],
                               ffT[:, 512 * c:512 * c + 512]).then_inc(hi_ev, 1)

            def item(it_, a, g0, g, m):
                kind = it_[0]
                if kind == "proj":
                    _, i, c = it_
                    act.wait_ge(mx_full, g0 + 1 + g)
                    if i == 0 and c == 0 and not (isinstance(m, int) and m == 0):
                        act.wait_ge(asm[0], m * 64)
                        act.wait_ge(asm[1], m * 64)
                        act.wait_ge(asm_kq, m * 96)
                    nc.scalar.mul(HI[:, i, HALF * c:HALF * c + HALF], MX[:, :],
                                  0.125 if i == 0 else 1.0).then_inc(hi_done, 1)
                elif kind == "value":
                    act.wait_ge(mx_full, g0 + 1 + g)
                    half = it_[1]
                    nc.scalar.copy(V1[:, a, 8 * half:8 * half + 8, :].rearrange("p j d -> p (j d)"),
                                   MX[:, :]).then_inc(mx_free, 1)

            def scalar_main(it, a):
                n = it * 2 + a
                g0 = n * NMAIN + NPREP
                g = 0
                for s in range(2 * NT):
                    Q, J = divmod(s, NT)
                    H = it * 4 + (2 * a + Q)
                    G = H * NT + J
                    for h in range(2):
                        act.wait_ge(qk_done, G * 2 + (h + 2))
                        act.wait_ge(pv_done, G + 1)
                        old = (J - 2) % NT
                        Ho = H if J >= 2 else H - 1
                        if old in DVE_SUMS:
                            act.wait_ge(sum_dve, Ho * (2 * len(DVE_SUMS)) + (2 * DVE_SUMS.index(old) + h + 3))
                        else:
                            k = POOL_SUMS.index(max(old, 1))
                            act.wait_ge(sum_pool, Ho * (2 * len(POOL_SUMS)) + (2 * k + h + 3))
                        nc.scalar.activation(Pr[:, h, J % 2, :], S1[h], ACT.Exp).then_inc(exp_done, 1)
                    for i_ in SCHED[s]:
                        item(i_, 1 - a, g0, g, n + 1)
                        g += 1
                    if J == NT - 1:
                        act.wait_ge(pv_done, G + 3)
                        act.wait_ge(o_done, H + 1)
                        nc.scalar.copy(o_raw[:, :], PV).then_inc(pv_evac, 1)

            for g, i_ in enumerate(PREP):
                item(i_, 0, 0, g, 0)
            with act.Fori(0, NP // 2) as it:
                for a in range(2):
                    scalar_main(it, a)

            norm(4)
            for c in range(4):
                act.wait_ge(tr, 12 + c + 1)
                nc.scalar.copy(xT_hi[:, W0 + 512 * c:W0 + 512 * c + 512], ps[:, c, :]).then_inc(hi_ev, 1)
            for u in range(4 * NH):
                act.wait_ge(gu_mm, u + 1)
                if u >= 2:
                    act.wait_ge(h_s, u - 1)
                nc.scalar.activation(silu[:, u % 2, :], ps[:, 4 + 2 * (u % 2), :], ACT.Silu,
                                     scale=WSCALE).then_inc(silu_s, 1)

        @block.vector
        def _(dve):
            chain = [0]

            def link(ins):
                chain[0] += 1
                ins.then_inc(dv, 1)
                dve.wait_ge(dv, chain[0])

            xcf = KR[:, 0].rearrange("p h t -> p (h t)").bitcast(F32)
            xc = xcf.rearrange("p (t d) -> p t d", t=NT)
            xn = wide[:, :].rearrange("p (t d) -> p t d", t=NT)

            def norm(k, src):
                link(nc.vector.reduce_sum(stat[:, 0, :], src, AX.X))
                link(nc.vector.tensor_scalar(stat[:, 1, :], stat[:, 0, :], -1.0 / P, None, ALU.mult))
                nc.vector.tensor_tensor(xc, src, bcast(stat[:, 1, :], 2, P), ALU.add).then_inc(ln_c, 1)
                dve.wait_ge(ln_sq, k + 1)
                link(nc.vector.reduce_sum(stat[:, 2, :], xn, AX.X))
                nc.vector.tensor_scalar(stat[:, 3, :], stat[:, 2, :], 1.0 / P, EPS, ALU.mult,
                                        ALU.add).then_inc(ln_v, 1)
                dve.wait_ge(ln_sd, k + 1)
                link(nc.vector.reciprocal(stat[:, 5, :], stat[:, 4, :]))
                nc.vector.tensor_tensor(xn, xc, bcast(stat[:, 5, :], 2, P), ALU.mult).then_inc(ln_x, 1)

            dve.wait_ge(ld0, 16 * LD0)
            norm(0, x[:, :, :])
            link(nc.vector.tensor_copy(w0_hi[:, :], w0[:, :]))
            nc.vector.tensor_tensor(w0_lo[:, :], w0[:, :], w0_hi[:, :], ALU.subtract).then_inc(w_split, 2)
            for c in range(4):
                dve.wait_ge(hi_ev, c + 1)
                cols = slice(W0 + 512 * c, W0 + 512 * c + 512)
                nc.vector.tensor_tensor(xT_lo[:, cols], ps[:, c, :], xT_hi[:, cols], ALU.subtract).then_inc(tr_ev, 1)
            for i in range(2):
                hi = (qT[:, 0, :], kT[:, 0, W0:])[i]
                lo = (qT[:, 1, :], kT[:, 1, W0:])[i]
                for c in range(4):
                    dve.wait_ge(qk0_hi, 4 * i + c + 1)
                    cs = slice(512 * c, 512 * c + 512)
                    nc.vector.tensor_tensor(lo[:, cs], ps[:, 4 + c, :], hi[:, cs], ALU.subtract).then_inc(qk0_ev, 1)
            for g in range(NB // 4):
                dve.wait_ge(v0_hi, g + 1)
                for blk in range(2):
                    rows = slice(64 * blk, 64 * blk + 64)
                    src = ps[rows, g % 4, :].rearrange("p (b g w) -> p (b g) w", b=4, g=G0)
                    cut = lambda v: v[rows, 4 * g:4 * g + 4, :, blk, 0:HG * D0].rearrange("p b g w -> p (b g) w")
                    last = nc.vector.tensor_tensor(cut(v_lo), src, cut(v_hi), ALU.subtract)
                last.then_inc(v0_ev, 1)
            dve.wait_ge(qk0_ev, 8)
            dve.wait_ge(v0_ev, NB // 4)

            hm = hmask[:, :].rearrange("p (h q) -> p h q", h=H0)

            def attn0(k, on, a, first):
                if on[0]:
                    b = k
                    par = a % 2
                    if not first or a >= 2:
                        dve.wait_ge(s0, b - 1)
                    for blk in range(2):
                        q = qT[:, 0, bass.ds(b * (2 * W0) + W0 * blk, W0)]
                        last = nc.vector.tensor_tensor(
                            qm_hi[:, par, blk * 512:blk * 512 + 512].rearrange("p (h q) -> p h q", h=H0),
                            bcast(q, 1, H0), hm, ALU.mult)
                    last.then_inc(qmh, 1)
                    dve.wait_ge(s0, b + 1)
                    sc = ps[:, par, :].rearrange("p (n k) -> p n k", k=2 * W0)
                    if not (first and a == 0):
                        dve.wait_ge(sub0, b)
                    nc.vector.reduce_max(mx0, sc, AX.X).then_inc(m0, 1)
                    dve.wait_ge(m0, b + 1)
                    if not first or a >= 2:
                        dve.wait_ge(e0, b - 1)
                    nc.vector.tensor_tensor(sub_s[:, par, :].rearrange("p (n k) -> p n k", k=2 * W0), sc,
                                            bcast(mx0, 2, 2 * W0), ALU.subtract).then_inc(sub0, 1)
                if on[1]:
                    b = k - 1
                    par = (a + 1) % 2
                    dve.wait_ge(hi0, b + 1)
                    if not first or a >= 3:
                        dve.wait_ge(pv0, b - 1)
                    nc.vector.tensor_tensor(pT[:, par, 1, :], ps[:, 2 + par, :], pT[:, par, 0, :],
                                            ALU.subtract).then_inc(lo0, 1)
                if on[2]:
                    b = k - 2
                    par = a % 2
                    dve.wait_ge(pv0, b + 1)
                    o = ps[:, 4 + par, 0:G0 * 2 * VW].rearrange("p (g a w) -> p a g w", g=G0, a=2)
                    if not (first and a == 2):
                        dve.wait_ge(om0, b)
                    rc = rc0.rearrange("p (a g) -> p a g", a=2)
                    nc.vector.reciprocal(rc, o[:, :, :, VW - 1]).then_inc(rc_s, 1)
                    t3 = om1.rearrange("p (a g w) -> p (a g) w", a=2, g=G0)
                    for blk in range(2):
                        last = nc.vector.tensor_tensor(t3[:, G0 * blk:G0 * blk + G0, :], o[:, blk, :, 0:VW - 1],
                                                       bcast(gmask[:, :], 1, G0), ALU.mult)
                    last.then_inc(om1_s, 1)
                    dve.wait_ge(rc_s, b + 1)
                    dve.wait_ge(om1_s, b + 1)
                    if not first or a >= 4:
                        dve.wait_ge(sel0, b - 1)
                    nc.vector.tensor_tensor(om[:, par, :].rearrange("p (n w) -> p n w", n=2 * G0), t3,
                                            bcast(rc0, 2, HG * D0), ALU.mult).then_inc(om0, 1)
                if on[4] and a % 2 == 0:
                    tile, _ = on[4]
                    dve.wait_ge(y0, tile + 1)
                    xt = x[:, bass.ds(tile, 1), :].rearrange("p a d -> p (a d)")
                    nc.vector.tensor_tensor(xt, ps[:, 7, 0:P], xt, ALU.add).then_inc(x0, 1)

            run_attn0(dve, attn0)
            dve.wait_ge(x0, NT)

            norm(1, x[:, :, :])
            dve.wait_ge(z_ev, 8)
            dve.wait_ge(ldc, 16 * 6)
            lg = z[:, :, NTRUE * RANK:NZ]
            link(nc.vector.reduce_max(rs[:, 0, :], lg, AX.X))
            nc.vector.tensor_tensor(rt[:, 0], lg, bcast(rs[:, 0, :], 2, NE), ALU.subtract).then_inc(r_exp_in, 1)
            dve.wait_ge(r_exp, 1)
            cur = rt[:, 1]
            for r in range(2):
                link(nc.vector.reduce_max(rs[:, 1, :], cur, AX.X))
                link(nc.vector.tensor_tensor(rt[:, 2], cur, bcast(rs[:, 1, :], 2, NE), ALU.is_equal))
                link(nc.vector.tensor_tensor(rt[:, 3], rt[:, 2], bcast(rank10[:, :], 1, NT), ALU.mult))
                link(nc.vector.reduce_max(rs[:, 2, :], rt[:, 3], AX.X))
                link(nc.vector.tensor_tensor(rt[:, 4 + r], rt[:, 3], bcast(rs[:, 2, :], 2, NE), ALU.is_equal))
                if r == 0:
                    link(nc.vector.tensor_tensor(rt[:, 6], cur, rt[:, 4], ALU.subtract))
                    link(nc.vector.tensor_tensor(rt[:, 7], rt[:, 6], rt[:, 4], ALU.subtract))
                    cur = rt[:, 7]
            link(nc.vector.tensor_tensor(rt[:, 2], rt[:, 4], rt[:, 5], ALU.add))
            link(nc.vector.tensor_tensor(rt[:, 3], rt[:, 2], rt[:, 1], ALU.mult))
            link(nc.vector.reduce_sum(rs[:, 3, :], rt[:, 3, :, 0:NTRUE], AX.X))
            link(nc.vector.tensor_scalar(rs[:, 4, :], rs[:, 3, :], 0.0, None, ALU.is_equal))
            link(nc.vector.tensor_tensor(rs[:, 5, :], rs[:, 3, :], rs[:, 4, :], ALU.add))
            link(nc.vector.reciprocal(rs[:, 6, :], rs[:, 5, :]))
            link(nc.vector.tensor_scalar(rs[:, 7, :], rs[:, 6, :], LORA_SCALE, None, ALU.mult))
            link(nc.vector.tensor_tensor(rt[:, 6], rt[:, 3], bcast(rs[:, 7, :], 2, NE), ALU.mult))
            for t8 in range(2):
                ts_ = slice(8 * t8, 8 * t8 + 8)
                last = nc.vector.tensor_tensor(
                    zw[:, ts_, :].rearrange("p t (e r) -> p t e r", e=NTRUE),
                    z[:, ts_, 0:NTRUE * RANK].rearrange("p t (e r) -> p t e r", e=NTRUE),
                    bcast(rt[:, 6, ts_, 0:NTRUE], 3, RANK), ALU.mult)
            link(last)
            nc.vector.tensor_tensor(xc, x[:, :, :], bcast(bias0[:, :], 1, NT), ALU.add).then_inc(zw_s, 1)
            dve.wait_ge(zw_s, 1)
            for c in range(4):
                dve.wait_ge(f_mm, c + 1)
                last = nc.vector.tensor_tensor(x[:, 4 * c:4 * c + 4, :].rearrange("p t d -> p (t d)"), ps[:, 4 + c, :],
                                               xc[:, 4 * c:4 * c + 4, :].rearrange("p t d -> p (t d)"), ALU.add)
            link(last)

            norm(2, x[:, :, :])
            dve.wait_ge(ln_x, 3)
            xn1 = ffT.rearrange("p (t d) -> p t d", t=NT)
            link(nc.vector.tensor_copy(xn1, xn))
            norm(3, xn1)
            for c in range(4):
                dve.wait_ge(tr, 8 + c + 1)
                cs = slice(512 * c, 512 * c + 512)
                nc.vector.tensor_scalar(ffT[:, cs], ps[:, c, :], gb[:, 0:1], gb[:, 1:2], ALU.mult,
                                        ALU.add).then_inc(gbt, 1)
                dve.wait_ge(hi_ev, 4 + c + 1)
                cols = slice(W0 + 512 * c, W0 + 512 * c + 512)
                nc.vector.tensor_tensor(xT_lo[:, cols], ffT[:, cs], xT_hi[:, cols], ALU.subtract).then_inc(tr_ev, 1)
            dve.wait_ge(tr_ev, 12)
            nc.vector.memset(QB[64:128, :, :, :].rearrange("p a h t -> p (a h t)").bitcast(F32), 0.0)
            for K in (KL, KR):
                nc.vector.memset(K[64:128, :, :, :].rearrange("p a h t -> p (a h t)").bitcast(F32), 0.0)
            nc.vector.memset(accD.rearrange("p h q -> p (h q)"), 1.0).then_inc(comb_done, 2)
            nc.vector.memset(wo1[:, :, :], 0.0)
            nc.vector.memset(ones1[:, :], 1.0)
            nc.vector.memset(o_raw[:, :], 0.0).then_inc(pv_evac, 1)
            link(nc.vector.memset(wide[:, :], 0.0))
            for K in (KL, KR):
                last = nc.vector.memset(K[ROW_M:ROW_M + NT, :, :, :].rearrange("p a h t -> p (a h t)"), M_UNIT)
            last.then_inc(init, 1)

            def item(it_, a, g0, g, m, H, yhalf):
                kind = it_[0]
                if kind == "proj":
                    _, i, c = it_
                    dve.wait_ge(hi_done, m * 4 + (2 * i + c + 1))
                    cs = slice(HALF * c, HALF * c + HALF)
                    nc.vector.scalar_tensor_tensor(out=LO[:, i, cs], in0=MX[:, :], scalar=0.125 if i == 0 else 1.0,
                                                   in1=HI[:, i, cs], op0=ALU.mult,
                                                   op1=ALU.subtract).then_inc(mx_free, 1)
                elif kind == "max":
                    _, h, tt, kh = it_
                    if tt == 0 and kh == 0:
                        dve.wait_ge(ldc, 16 * 6)
                        dve.wait_ge(ldt, m * 112 + 112)
                        dve.wait_ge(mx_free, g0 + 1 + g)
                        nc.vector.tensor_scalar(dist_h[:, :], dist[:, :], slope[:, a, h:h + 1], None,
                                                ALU.mult).then_inc(ts_done, 1)
                    ready = settled(dve, g0 + 1 + g)
                    scaled = settled(dve, m * 2 + (h + 1))
                    dve.wait_ge(ldc, 16 * 6)
                    if tt == 0 and kh == 0:
                        dve.wait_ge(ts_done, scaled)
                    dve.wait_ge(mx_full, ready)
                    c0 = T - P - P * tt + HALF * kh
                    nc.vector.tensor_tensor_reduce(
                        out=junk[:, :], in0=MX[:, :], in1=dist_h[:, c0:c0 + HALF], scale=1.0, scalar=-3.0e38,
                        op0=ALU.add, op1=ALU.max, accum_out=mx2[:, h, tt, kh:kh + 1]).then_inc(mx_free, 1)
                    if tt == NT - 1 and kh == 1:
                        dve.wait_ge(mx_free, g0 + 2 + g)
                        nc.vector.tensor_tensor(nm[:, 0, h, :], mx2[:, h, :, 0], mx2[:, h, :, 1],
                                                ALU.max).then_inc(nm1, 1)
                        dve.wait_ge(nm1, m * 2 + (h + 1))
                        nc.vector.tensor_scalar(nm[:, 1, h, :], nm[:, 0, h, :], -1.0 / M_UNIT, None,
                                                ALU.mult).then_inc(nm_done, 1)
                elif kind == "mrow":
                    h = it_[1]
                    rows = slice(ROW_M, ROW_M + NT)
                    dve.wait_ge(mx_full, g0 + 1 + g)
                    nc.vector.tensor_tensor(QB[rows, a, h, :].rearrange("p (t q) -> p t q", t=NT),
                                            bcast(MX[rows, 0:P], 1, NT), bcast(bmask[rows, :], 2, P),
                                            ALU.mult).then_inc(mx_free, 1)
                elif kind == "den":
                    dve.wait_ge(mx_full, g0 + 1 + g)
                    nc.vector.reciprocal(o_nrm[:, :], MX[:, :]).then_inc(mx_free, 1)
                    dve.wait_ge(mx_free, g0 + 2 + g)
                    dve.wait_ge(pv_evac, H + 1)
                    nc.vector.tensor_tensor(o_nrm[:, :], o_raw[:, :], o_nrm[:, :], ALU.mult).then_inc(o_done, 1)
                elif kind == "out":
                    dve.wait_ge(mx_full, g0 + 1 + g)
                    cs = slice(HALF * yhalf, HALF * yhalf + HALF)
                    nc.vector.tensor_tensor(wide[:, cs], MX[:, :], wide[:, cs], ALU.add).then_inc(mx_free, 1)

            def vector_sum(H, J):
                k = DVE_SUMS.index(J)
                for h in range(2):
                    dve.wait_ge(exp_done, (H * NT + J) * 2 + (h + 3))
                    if k == 0:
                        nc.vector.tensor_copy(accD[:, h, :], Pr[:, h, J % 2, :]).then_inc(sum_dve, 1)
                    else:
                        dve.wait_ge(sum_dve, H * (2 * len(DVE_SUMS)) + (2 * k + h + 1))
                        nc.vector.tensor_tensor(accD[:, h, :], accD[:, h, :], Pr[:, h, J % 2, :],
                                                ALU.add).then_inc(sum_dve, 1)

            def vector_main(it, a):
                n = it * 2 + a
                g0 = n * NMAIN + NPREP
                g = 0
                for s in range(2 * NT):
                    Q, J = divmod(s, NT)
                    H = it * 4 + (2 * a + Q)
                    if J - 1 in DVE_SUMS:
                        vector_sum(H, J - 1)
                    for i_ in SCHED[s]:
                        item(i_, 1 - a, g0, g, n + 1, H, 1 - Q)
                        g += 1
                    if J == NT - 1:
                        vector_sum(H, J)
                        for h in range(2):
                            dve.wait_ge(sum_pool, H * (2 * len(POOL_SUMS)) + (2 * len(POOL_SUMS) + 2))
                            dve.wait_ge(sum_dve, H * (2 * len(DVE_SUMS)) + (2 * len(DVE_SUMS) + 2))
                            nc.vector.tensor_tensor(accD[:, h, :], accD[:, h, :], accP[:, h, :],
                                                    ALU.add).then_inc(comb_done, 1)

            for g, i_ in enumerate(PREP):
                item(i_, 0, 0, g, 0, 0, 0)
            with dve.Fori(0, NP // 2) as it:
                for a in range(2):
                    vector_main(it, a)
            g0 = NPREP + NP * NMAIN
            item(("den",), 0, g0, 0, 0, 2 * NP, 1)
            item(("out",), 0, g0, 1, 0, 2 * NP, 1)
            for c in range(4):
                dve.wait_ge(yt_mm, c + 1)
                xs = x[:, 4 * c:4 * c + 4, :].rearrange("p t d -> p (t d)")
                last = nc.vector.tensor_tensor(xs, ps[:, c, :], xs, ALU.add)
            link(last)

            dve.wait_ge(asm_kq, 96 * (NP + 1))
            dve.wait_ge(ldt, 112 * (NP + 1))
            norm(4, x[:, :, :])
            dve.wait_ge(wcv, 48)
            for dst, src in ((wg, wgi), (wu, wui), (wd.rearrange("p k d -> p (k d)"), wdi)):
                nc.vector.tensor_copy(dst, src).then_inc(w_split, 1)
            for c in range(4):
                dve.wait_ge(hi_ev, 8 + c + 1)
                cols = slice(W0 + 512 * c, W0 + 512 * c + 512)
                nc.vector.tensor_tensor(xT_lo[:, cols], ps[:, c, :], xT_hi[:, cols], ALU.subtract).then_inc(tr_ev, 1)
            for c in range(4):
                for k in range(NH):
                    u = NH * c + k
                    dve.wait_ge(silu_s, u + 1)
                    nc.vector.scalar_tensor_tensor(out=hid[:, k, 512 * c:512 * c + 512],
                                                   in0=ps[:, 5 + 2 * (u % 2), :], scalar=WSCALE,
                                                   in1=silu[:, u % 2, :], op0=ALU.mult, op1=ALU.mult).then_inc(h_s, 1)
                if c:
                    residual(dve, nc, c - 1, ps, x, dn_mm, x4_s)
            residual(dve, nc, 3, ps, x, dn_mm, x4_s)

        @block.gpsimd
        def _(pool):
            nc.gpsimd.memset(xT_hi[:, 0:W0], 0.0)
            nc.gpsimd.memset(kT[:, :, 0:W0], 0.0)
            nc.gpsimd.memset(xT_lo[:, 0:W0], 0.0).then_inc(init, 1)
            pool.wait_ge(init, 1)
            nc.gpsimd.memset(v_hi.rearrange("p b g a w -> p (b g a w)"), 0.0)
            nc.gpsimd.memset(v_lo.rearrange("p b g a w -> p (b g a w)"), 0.0).then_inc(xb_s, 1)
            pool.wait_ge(xb_s, 1)
            nc.gpsimd.memset(v_hi[0:64, :, :, 0, VW - 1], 1.0).then_inc(xb_s, 1)
            pool.wait_ge(xb_s, 2)
            nc.gpsimd.memset(v_hi[64:128, :, :, 1, VW - 1], 1.0).then_inc(init, 1)
            pool.wait_ge(init, 2)

            hm = hmask[:, :].rearrange("p (h q) -> p h q", h=H0)
            pool.wait_ge(ld0, 16 * LD0)
            pool.wait_ge(qk0_ev, 4)

            def attn0(k, on, a, first):
                if on[0]:
                    b = k
                    par = a % 2
                    if not first or a >= 2:
                        pool.wait_ge(s0, b - 1)
                    for blk in range(2):
                        q = qT[:, 1, bass.ds(b * (2 * W0) + W0 * blk, W0)]
                        last = nc.gpsimd.tensor_tensor(
                            qm_lo[:, par, blk * 512:blk * 512 + 512].rearrange("p (h q) -> p h q", h=H0),
                            bcast(q, 1, H0), hm, ALU.mult)
                    last.then_inc(qml, 1)

            run_attn0(pool, attn0)

            def split(m):
                loaded = settled(pool, m * 16 + 16)
                pool.wait_ge(w1c, 1)
                pool.wait_ge(ldp, loaded)
                nc.gpsimd.tensor_copy(w1_hi[:, :, :], w1[:, :, :]).then_inc(w1s, 1)
                pool.wait_ge(w1s, m * 2 + 1)
                nc.gpsimd.tensor_tensor(w1_lo[:, :, :], w1[:, :, :], w1_hi[:, :, :], ALU.subtract).then_inc(w1s, 1)
                pool.wait_ge(w1s, m * 2 + 2)
                nc.gpsimd.memset(tick[:, :], 0.0).then_inc(w1c, 2)

            def pool_main(it, a):
                n = it * 2 + a
                pool.wait_ge(mx_free, n * NMAIN + (NPREP + 1))
                split(n + 1)
                for Q in range(2):
                    H = it * 4 + (2 * a + Q)
                    for k, J in enumerate(POOL_SUMS):
                        for h in range(2):
                            pool.wait_ge(exp_done, (H * NT + J) * 2 + (h + 3))
                            own = H * (2 * len(POOL_SUMS))
                            if k == 0:
                                pool.wait_ge(comb_done, H * 2 + (h + 1))
                                nc.gpsimd.tensor_tensor(accP[:, h, :], Pr[:, h, 0, :], Pr[:, h, 1, :],
                                                        ALU.add).then_inc(sum_pool, 1)
                            else:
                                pool.wait_ge(sum_pool, own + (2 * k + h + 1))
                                nc.gpsimd.tensor_tensor(accP[:, h, :], accP[:, h, :], Pr[:, h, J % 2, :],
                                                        ALU.add).then_inc(sum_pool, 1)

            nc.gpsimd.memset(tick[:, :], 0.0).then_inc(qk_done, 1)
            pool.wait_ge(qk_done, 1)
            for s_, v in ((exp_done, 2), (pv_done, 2), (sum_pool, 2), (sum_dve, 2), (mx_free, 1), (w1c, 1)):
                nc.gpsimd.memset(tick[:, :], 0.0).then_inc(s_, v)
                pool.wait_ge(s_, v)
            split(0)
            with pool.Fori(0, NP // 2) as it:
                for a in range(2):
                    pool_main(it, a)


def settled(eng, value):
    if not isinstance(value, int):
        eng.compute_val(value)
    return value


def down(pe, nc, c, ps, hid, wd, h_s, dn_mm):
    pe.wait_ge(h_s, NH * (c + 1))
    for j in range(4):
        t = 4 * c + j
        for k in range(NH):
            last = nc.tensor.matmul(ps[:, c, j * P:(j + 1) * P], hid[:, k, t * P:(t + 1) * P], wd[:, k, :],
                                    start=k == 0, stop=k == NH - 1)
    last.then_inc(dn_mm, 1)


def residual(dve, nc, c, ps, x, dn_mm, x4_s):
    dve.wait_ge(dn_mm, c + 1)
    xs = x[:, 4 * c:4 * c + 4, :].rearrange("p t d -> p (t d)")
    nc.vector.scalar_tensor_tensor(out=xs, in0=ps[:, c, :], scalar=WSCALE, in1=xs, op0=ALU.mult,
                                   op1=ALU.add).then_inc(x4_s, 1)


def run_attn0(eng, step):
    last = 3
    steady = 6

    def on(k, base=None):
        flags = []
        for j in range(5):
            b = k - min(j, 3)
            live = 0 <= b < NB
            if base is not None:
                live = True
            if live and j >= 3:
                tile = b // 2 if base is None else base + (b // 2)
                flags.append((tile, base is None and tile == 0))
            else:
                flags.append(live)
        return flags

    for k in range(steady):
        step(k, on(k), k, True)
    n = (NB - steady) // 2
    with eng.Fori(0, n) as i:
        for s in range(2):
            flags = on(steady + s, i)
            step(i * 2 + (steady + s), flags, (steady + s), False)
    for k in range(NB, NB + last):
        step(k, on(k), k, False)


def constants():
    c = {}
    c["ident"] = np.eye(P, dtype=np.float32)
    c["ident_b"] = bf16_bits(np.eye(P, dtype=np.float32))
    d = np.arange(P)
    c["hmask"] = np.repeat((d[:, None] // D0 == np.arange(H0)[None, :]), W0, axis=1).astype(np.float16)
    c["gmask"] = (d[:, None] // W0 == np.arange(HG * D0)[None, :] // D0).astype(np.float32)
    c["sel"] = (d[:, None] % W0 == np.arange(W0)[None, :]).astype(np.float32)
    ti, tj = (d % W0)[:, None], np.arange(2 * W0)[None, :]
    band = (tj >= ti + 1) & (tj <= ti + W0)
    first = band & (tj >= W0)
    mask = np.zeros((P, 2, G0, 2, 2 * W0), np.float32)
    mask[:, :] = np.where(band, 0.0, -1e30)[:, None, None, None, :]
    mask[:, 1, :, 0, :] = np.where(first, 0.0, -1e30)[:, None, :]
    c["mask0"] = bf16_bits(mask.reshape(P, 2, 512))
    c["rank10"] = np.tile(NE - np.arange(NE, dtype=np.float32), (P, 1))
    col = np.arange(TW)
    c["dist"] = (-np.abs(d[:, None] - col[None, :] + (T - P))).astype(np.float16)
    c["relu_w"] = np.maximum(d[None, :] - d[:, None], 0).astype(np.float16)
    bm = np.zeros((P, NT), np.float32)
    bm[ROW_M:ROW_M + NT] = np.eye(NT)
    c["bmask"] = bm
    n_seq = np.arange(H1, 0, -1).astype(np.float32)
    slopes = (np.float32(2.0) ** (np.float32(-8.0) / n_seq)).astype(np.float32).astype(np.float64)

    def parts(v, n):
        out = []
        for _ in range(n):
            p = v.astype(np.float16).astype(np.float64)
            out.append(p)
            v = v - p
        return np.stack(out)

    pos = np.arange(T) - CENTRE
    rows = np.zeros((NA, T))
    rows[0:3] = pos / 1024.0
    rows[3:6] = 1.0
    c["pos_rows"] = rows.astype(np.float16)
    left = np.zeros((H1, NA, T))
    for h in range(H1):
        left[h, 0:3] = parts(-slopes[h:h + 1] * 1024.0, 3)
        left[h, 3:6] = parts(slopes[h] * pos, 3)
    pad = lambda a: np.concatenate([a, a[:1]])
    c["alibi_l"] = pad(left.reshape(NP, 2, NA, T)).astype(np.float16)
    c["alibi_r"] = pad(-left.reshape(NP, 2, NA, T)).astype(np.float16)
    dg = np.zeros((H1, P, 2, P))
    for h in range(H1):
        for i, p in enumerate(parts(-2.0 * slopes[h:h + 1], 2)):
            dg[h, :, i, :] = np.eye(P) * p
    c["diag"] = pad(dg.reshape(NP, 2, P, 2, P)).astype(np.float16)
    c["slope"] = pad(np.tile(slopes.astype(np.float32).reshape(NP, 1, 2), (1, P, 1)))
    return c


def bf16_bits(a):
    return (np.ascontiguousarray(a, np.float32).view(np.uint32) >> 16).astype(np.uint16)


def layout(v):
    pairs = lambda w: w.reshape(P, NP, P).transpose(1, 0, 2)
    pad = lambda a: np.concatenate([a, a[:1]])
    out = {
        "x": v["L0_attn_x"], "w_qkv": v["L0_attn_w_qkv"], "w_out": v["L0_attn_w_out"],
        "wz": np.concatenate([v["L0_ffn_lora_A"].reshape(NTRUE * RANK, P), v["L0_ffn_gate_w"]]).T,
        "wbase": v["L0_ffn_base_w"].T,
        "wlb": v["L0_ffn_lora_B"].transpose(0, 2, 1).reshape(NTRUE * RANK, P),
        "bias0": np.broadcast_to(v["L0_ffn_base_b"], (P, P)),
        "gb": np.stack([v["L1_attn_ln_gamma"], v["L1_attn_ln_beta"]], axis=1),
        "w1": pad(np.stack([pairs(v["L1_attn_Wq"]), pairs(v["L1_attn_Wk"]), pairs(v["L1_attn_Wv"])], axis=2)),
        "wo1": pad(v["L1_attn_Wo"].reshape(NP, P, P)),
        "w_gate": v["L1_ffn_w_gate"].T, "w_up": v["L1_ffn_w_up"].T, "w_down": v["L1_ffn_w_down"].T,
    }
    return {k: np.ascontiguousarray(a) for k, a in out.items()}


def kernel(**inputs):
    import concourse.bacc as _bacc
    from concourse.bass_utils import run_bass_kernel_spmd as _run

    nc = _bacc.Bacc("TRN2", target_bir_lowering=False, num_devices=1)
    arrays = layout({k: np.asarray(a) for k, a in inputs.items()})
    arrays.update(constants())
    io = {n: nc.dram_tensor(f"in_{n}", a.shape, mybir.dt.from_np(a.dtype), kind="ExternalInput").ap()
          for n, a in arrays.items()}
    io["out"] = nc.dram_tensor("out", (1, T, P), F32, kind="ExternalOutput").ap()
    build(nc, io)
    r = _run(nc, [{f"in_{n}": a for n, a in arrays.items()}], core_ids=[0])
    return r.results[0]["out"]
```

```python
from contextlib import ExitStack

import concourse.bass as bass
import numpy as np
from concourse import mybir

F32 = mybir.dt.float32
F16 = mybir.dt.float16
BF16 = mybir.dt.bfloat16
I32 = mybir.dt.int32
U16 = mybir.dt.uint16
ALU = mybir.AluOpType
ACT = mybir.ActivationFunctionType
AX = mybir.AxisListType

P = 128
T = 2048
NT = T // P
EPS = 1e-5

W0 = 32
H0 = 16
D0 = P // H0
G0 = 4
HG = H0 // G0
NB = T // (2 * W0)
SC0 = float(D0) ** -0.5
VW = HG * D0 + 1

NE, NTRUE, RANK = 10, 8, 16
NZ = NTRUE * RANK + NE
LORA_SCALE = 2.0

H1 = 16
D1 = 64
NP = H1 // 2
HALF = 1024
CENTRE = T // 2
TW = 2 * T - P
ROW_M = 64
ROW_A = 96
NA = 6
M_UNIT = 64.0

HID = 384
NH = HID // P
WSCALE = 1.0 / 127.0

POOL_SUMS = [1, 2, 4, 5, 6, 8, 9, 10, 12, 13, 14]
DVE_SUMS = [3, 7, 11, 15]


def bcast(ap, dim, n):
    a = ap.unsqueeze(dim)
    shape = list(a.shape)
    shape[dim] = n
    return a.broadcast_to(shape)


def prep_items():
    items = [("proj", i, c) for i in range(2) for c in range(T // 512)]
    items += [("value", c) for c in range(T // 512)]
    for h in range(2):
        items += [("max", h, t, c) for t in range(NT) for c in range(T // 512)]
        items.append(("mrow", h))
    return items


SLOTS = 4


def main_schedule():
    prep = prep_items()
    slots = [[] for _ in range(2 * NT * SLOTS)]
    for i in range(12):
        slots[SLOTS + i].append(prep[i])
    rest = prep[12:]
    first = 7 * SLOTS
    free = [k for k in range(first, len(slots)) if k % (NT * SLOTS) not in (2, 3)]
    at = 0
    for n, k in enumerate(free):
        to = (len(rest) * (n + 1) + len(free) - 1) // len(free)
        slots[k] += rest[at:to]
        at = to
    for q in range(2):
        base = q * NT * SLOTS
        for k, item in ((SLOTS, ("den", 0)), (SLOTS + 1, ("den", 1)), (3 * SLOTS, ("recip",)),
                        (5 * SLOTS + 2, ("scale",)), (6 * SLOTS, ("out", 0)), (6 * SLOTS + 1, ("out", 1))):
            slots[base + k].append(item)
    return slots


def banked(item):
    return item[0] not in ("recip", "scale")


PREP = prep_items()
SCHED = main_schedule()
FLAT = [x for s in SCHED for x in s if banked(x)]
NPREP = len(PREP)
NMAIN = len(FLAT)
assert NPREP % 2 == 0 and NMAIN % 2 == 0


def numbered(s):
    g = sum(banked(x) for k in SCHED[:SLOTS * s] for x in k)
    out = []
    for k in SCHED[SLOTS * s:SLOTS * s + SLOTS]:
        out.append([])
        for x in k:
            out[-1].append((x, g))
            g += banked(x)
    return out


def build(nc, io):
    ctx = ExitStack()
    with ctx:
        def sb(name, shape, dt):
            return ctx.enter_context(nc.sbuf_tensor(name, shape, dt))

        def sem(name):
            return ctx.enter_context(nc.semaphore(name))

        ps = ctx.enter_context(nc.psum_tensor("ps", [P, 8, 512], F32))

        x = sb("x", [P, NT, P], F32)
        ident = sb("ident", [P, P], F32)
        stat = sb("stat", [P, 8, NT], F32)
        xT_hi = sb("xT_hi", [P, W0 + T], F16)
        xT_lo = sb("xT_lo", [P, W0 + T], F16)
        wide = sb("wide", [P, T], F32)

        QA = sb("QA", [P, 2, 2, T], F16)
        KA = sb("KA", [P, 2, 2, T], F16)
        QB = sb("QB", [P, 2, 2, T], F16)
        KL = sb("KL", [P, 2, 2, T], F16)
        KR = sb("KR", [P, 2, 2, T], F16)
        arena = sb("arena", [P, 16384], F32)
        A16 = arena[:, :].bitcast(F16)

        HI = A16[:, 0:4096].rearrange("p (i t) -> p i t", i=2)
        LO = A16[:, 4096:8192].rearrange("p (i t) -> p i t", i=2)
        V1 = arena[:, 4096:8192].rearrange("p (a j d) -> p a j d", a=2, j=NT)
        Pr = arena[:, 8192:12288].rearrange("p (h a q) -> p h a q", h=2, a=2)
        accP = arena[:, 12288:14336].rearrange("p (h q) -> p h q", h=2)
        accD = arena[:, 14336:16384].rearrange("p (h q) -> p h q", h=2)
        o_raw = sb("o_raw", [P, HALF], F32)
        o_nrm = sb("o_nrm", [P, HALF], F32)
        dist = sb("dist", [P, TW], F16)
        dist_h = sb("dist_h", [P, TW], F16)
        junk = sb("junk", [P, 2, 512], F16)
        diag = sb("diag", [P, 2, 2, 2, P], F16)
        relu_w = sb("relu_w", [P, P], F16)
        w1 = sb("w1", [P, 3, P], F32)
        w1_hi = sb("w1_hi", [P, 3, P], F16)
        w1_lo = sb("w1_lo", [P, 3, P], F16)
        wo1 = sb("wo1", [P, 2, P], F32)
        slope = sb("slope", [P, 2, 2], F32)
        mx2 = sb("mx2", [P, 2, NT, 4], F32)
        den_c = sb("den_c", [P, 2, HALF // P], F32)
        rec_c = sb("rec_c", [P, 2, HALF // P], F32)
        den_sb = rec_b = o_nrm
        rec_row = nc.dram_tensor("rec_row", (2, HALF), F32, kind="Internal").ap()
        nm = sb("nm", [P, 2, 2, NT], F32)
        bmask = sb("bmask", [P, NT], F32)
        tick = sb("tick", [P, 1], F32)
        ones1 = sb("ones1", [P, D1], F32)
        gb = sb("gb", [P, 2], F32)

        kT = A16[:, 0:2 * (W0 + T)].rearrange("p (a t) -> p a t", a=2)
        qT = A16[:, 4160:4160 + 2 * T].rearrange("p (a t) -> p a t", a=2)
        o1 = 8256
        nv = NB * G0 * 2 * VW
        v_hi = A16[:, o1:o1 + nv].rearrange("p (b g a w) -> p b g a w", b=NB, g=G0, a=2)
        v_lo = A16[:, o1 + nv:o1 + 2 * nv].rearrange("p (b g a w) -> p b g a w", b=NB, g=G0, a=2)
        R32 = QA[:, 0].rearrange("p h t -> p (h t)").bitcast(F32)
        R32b = QA[:, 1].rearrange("p h t -> p (h t)").bitcast(F32)
        RK = KA[:, 0].rearrange("p h t -> p (h t)")
        RK2 = KA[:, 1].rearrange("p h t -> p (h t)").bitcast(F32)
        sub_s = R32[:, 0:1024].rearrange("p (a n) -> p a n", a=2)
        exp_s = R32[:, 1024:2048].rearrange("p (a n) -> p a n", a=2)
        pT = RK[:, 0:2048].rearrange("p (a c n) -> p a c n", a=2, c=2)
        qm = RK[:, 2048:4096].rearrange("p (c n) -> p c n", c=2)
        qm_lo = R32b[:, 0:1024].bitcast(F16).rearrange("p (c n) -> p c n", c=2)
        qm_hi = R32b[:, 1024:2048].bitcast(F16).rearrange("p (c n) -> p c n", c=2)
        om1 = RK2[:, 0:256]
        om = RK2[:, 256:768].rearrange("p (a n) -> p a n", a=2)
        oT = RK2[:, 768:896]
        mx0 = RK2[:, 896:904]
        rc0 = RK2[:, 904:912]

        QBh = QB[:, :, :, :].rearrange("p a h t -> p (a h t)")
        QBf = QBh.bitcast(F32)
        mask0 = QBf[:, 0:512].bitcast(BF16).rearrange("p (v n) -> p v n", v=2)
        ident_b = QBf[:, 512:576].bitcast(BF16)
        hmask = QBh[:, 1152:1152 + H0 * W0]
        gmask = QBf[:, 832:864]
        sel = QBf[:, 864:896]
        w0 = QBf[:, 896:1280]
        w0_hi = QBh[:, 2560:2944]
        w0_lo = QBh[:, 2944:3328]
        wo0 = QBf[:, 1664:1792]
        wz = QBf[:, 1792:1792 + NZ]
        wbase = QBf[:, 1936:2064]
        wlb = QBf[:, 2064:2192]
        bias0 = QBf[:, 2192:2320]
        rank10 = QBf[:, 2320:2330]

        ffT = arena[:, 0:2048]
        z = arena[:, 2048:2048 + NT * NZ].rearrange("p (t n) -> p t n", t=NT)
        zw = arena[:, 4352:6400].rearrange("p (t n) -> p t n", t=NT)
        zwT = arena[:, 6400:8448]
        rt = arena[:, 8448:8448 + 8 * NT * NE].rearrange("p (k t e) -> p k t e", k=8, t=NT)
        rs = arena[:, 10240:10240 + 8 * NT].rearrange("p (k t) -> p k t", k=8)

        wgi = arena[:, 0:HID].bitcast(I32)
        wui = arena[:, HID:2 * HID].bitcast(I32)
        wdi = arena[:, 2 * HID:3 * HID].bitcast(I32)
        wg = A16[:, 4096:4096 + HID]
        wu = A16[:, 4096 + HID:4096 + 2 * HID]
        wd = arena[:, 2560:2560 + HID].rearrange("p (k d) -> p k d", k=NH)
        silu = arena[:, 4096:4096 + 2 * 512].rearrange("p (a n) -> p a n", a=2)
        hid = arena[:, 6144:6144 + NH * T].rearrange("p (k t) -> p k t", k=NH)

        ld0 = sem("ld0")
        ldc = sem("ldc")
        dv = sem("dv")
        ln_c, ln_sq, ln_v, ln_sd = sem("ln_c"), sem("ln_sq"), sem("ln_v"), sem("ln_sd")
        ln_x = sem("ln_x")
        tr = sem("tr")
        tr_ev = sem("tr_ev")
        gbt = sem("gbt")
        hi_ev = sem("hi_ev")
        w_split = sem("w_split")
        init = sem("init")
        qk0, qk0_hi, qk0_ev = sem("qk0"), sem("qk0_hi"), sem("qk0_ev")
        v0, v0_hi, v0_ev = sem("v0"), sem("v0_hi"), sem("v0_ev")
        qmh, qml, s0, m0, sub0, e0 = (sem(n) for n in ("qmh", "qml", "s0", "m0", "sub0", "e0"))
        t0, hi0, lo0, pv0, rc_s, om1_s, om0 = (sem(n) for n in ("t0", "hi0", "lo0", "pv0", "rc_s", "om1_s", "om0"))
        sel0, ot0, y0, x0 = (sem(n) for n in ("sel0", "ot0", "y0", "x0"))
        z_mm, z_ev, r_exp, r_exp_in, zw_s, zt_mm, zt_ev, f_mm, f_ev, xb_s = (
            sem(n) for n in ("z_mm", "z_ev", "r_exp", "r_exp_in", "zw_s", "zt_mm", "zt_ev", "f_mm", "f_ev", "xb_s"))
        ldrow = sem("ldrow")
        ldp = sem("ldp")
        ldt = sem("ldt")
        ldw = sem("ldw")
        w1s = sem("w1s")
        w1c = sem("w1c")
        mx_full = sem("mx_full")
        mx_free = [sem("mx_free0"), sem("mx_free1")]
        hi_done = sem("hi_done")
        asm = [sem("asm_a"), sem("asm_b")]
        asm_kq = sem("asm_kq")
        ts_done, nm1, nm_done = sem("ts_done"), sem("nm1"), sem("nm_done")
        qk_done, exp_done, pv_done, pv_evac = (sem(n) for n in ("qk_done", "exp_done", "pv_done", "pv_evac"))
        sum_pool, sum_dve, comb_done = sem("sum_pool"), sem("sum_dve"), sem("comb_done")
        o_done = sem("o_done")
        den_dma, rec_done, row_dma, rb_dma = (
            sem(n) for n in ("den_dma", "rec_done", "row_dma", "rb_dma"))
        yt_mm, x3_s = sem("yt_mm"), sem("x3_s")
        wcv, gu_mm, silu_s, h_s, dn_mm, x4_s, st = (
            sem(n) for n in ("wcv", "gu_mm", "silu_s", "h_s", "dn_mm", "x4_s", "st"))

        LD0 = 12
        block = ctx.enter_context(nc.Block())

        MX = [ps[:, 6, :], ps[:, 7, :]]
        S1 = [ps[:, 2 * h:2 * h + 2, :].rearrange("p b n -> p (b n)") for h in range(2)]
        PV = ps[:, 4:6, :].rearrange("p b n -> p (b n)")

        def await_bank(eng, b0, g):
            eng.wait_ge(mx_free[g % 2], b0 + (g // 2 + 1))

        def await_items(eng, b0, g):
            eng.wait_ge(mx_free[0], b0 + (g // 2 + 2))
            eng.wait_ge(mx_free[1], b0 + ((g + 1) // 2 + 1))

        @block.sync
        def _(sp):
            def await_values(*pairs):
                counts = [settled(sp, v) for _, v in pairs]
                sp.wait_ge(init, 3)
                for (s_, _), v in zip(pairs, counts):
                    sp.wait_ge(s_, v)

            def items(b0, g):
                return (mx_free[0], b0 + (g // 2 + 2)), (mx_free[1], b0 + ((g + 1) // 2 + 1))

            sp.dma_start(x[:, :, :], io["x"].rearrange("o (t p) d -> p (o t) d", p=P)).then_inc(ld0, 16)
            for dst, name in ((w0, "w_qkv"), (wo0, "w_out"), (ident, "ident"), (ident_b.bitcast(U16), "ident_b"),
                              (hmask, "hmask"), (gmask, "gmask"), (sel, "sel"), (wz, "wz"),
                              (wbase, "wbase"), (wlb, "wlb")):
                sp.dma_start(dst[:, :], io[name]).then_inc(ld0, 16)
            sp.dma_start(mask0.bitcast(U16), io["mask0"]).then_inc(ld0, 16)
            for dst, name in ((dist, "dist"), (relu_w, "relu_w"), (gb, "gb"), (bias0, "bias0"),
                              (rank10, "rank10"), (bmask, "bmask")):
                sp.dma_start(dst[:, :], io[name]).then_inc(ldc, 16)

            sp.wait_ge(init, 3)
            for a in range(2):
                for h in range(2):
                    sp.dma_start(QB[ROW_A:ROW_A + NA, a, h, :], io["pos_rows"]).then_inc(ldrow, 16)

            def load_w1(m):
                await_values((w1c, m * 2 + 1))
                sp.dma_start(w1[:, :, :], io["w1"][m]).then_inc(ldp, 16)

            def load_tables(m, a):
                if not isinstance(m, int):
                    await_values((qk_done, m * (4 * NT) + (2 - 4 * NT)), (ts_done, m * 2))
                for h in range(2):
                    sp.dma_start(KL[ROW_A:ROW_A + NA, a, h, :], io["alibi_l"][m, h]).then_inc(ldt, 16)
                    sp.dma_start(KR[ROW_A:ROW_A + NA, a, h, :], io["alibi_r"][m, h]).then_inc(ldt, 16)
                    sp.dma_start(diag[:, a, h, :, :], io["diag"][m, h]).then_inc(ldt, 16)
                sp.dma_start(slope[:, a, :], io["slope"][m]).then_inc(ldt, 16)

            def load_wo(m, a):
                sp.dma_start(wo1[:, a, :], io["wo1"][m]).then_inc(ldw, 16)

            def assemble(m, a, b0, g):
                await_values((hi_done, m * 8 + 8), *items(b0, g))
                for h in range(2):
                    rows = slice(64 * h, 64 * h + 64)
                    sp.dma_start(QA[0:64, a, h, :], HI[rows, 0, :]).then_inc(asm[h], 16)
                    sp.dma_start(QA[64:128, a, h, :], LO[rows, 0, :]).then_inc(asm[h], 16)
                    sp.dma_start(KA[0:64, a, h, :], HI[rows, 1, :]).then_inc(asm[h], 16)
                    sp.dma_start(KA[64:128, a, h, :], HI[rows, 1, :]).then_inc(asm[h], 16)
                for h in range(2):
                    rows = slice(64 * h, 64 * h + 64)
                    sp.dma_start(QB[0:64, a, h, :], HI[rows, 0, :]).then_inc(asm_kq, 16)
                    sp.dma_start(KL[0:64, a, h, :], LO[rows, 1, :]).then_inc(asm_kq, 16)
                    sp.dma_start(KR[0:64, a, h, :], LO[rows, 1, :]).then_inc(asm_kq, 16)

            def tail(H, b0, g):
                await_values(*items(b0, g))
                for h in range(2):
                    sp.dma_start(den_c[:, h, :], den_sb[64 * h:64 * h + 1, :]).then_inc(den_dma, 16)
                await_values((rec_done, H + 1))
                for h in range(2):
                    sp.dma_start(rec_row[h].rearrange("(p i) -> p i", p=P), rec_c[:, h, :]).then_inc(row_dma, 16)
                await_values((row_dma, H * 32 + 32))
                for h in range(2):
                    sp.dma_start(rec_b[64 * h:64 * h + 64, :],
                                 rec_row[h:h + 1, :].broadcast_to([64, HALF])).then_inc(rb_dma, 16)

            load_w1(0)
            load_tables(0, 0)
            load_wo(0, 0)
            assemble(0, 0, 0, 7)
            load_w1(1)
            with sp.Fori(0, NP // 2) as it:
                for a in range(2):
                    n = it * 2 + a
                    b0 = n * (NMAIN // 2) + NPREP // 2
                    load_tables(n + 1, 1 - a)
                    tail(n * 2, b0, FLAT.index(("den", 1)))
                    assemble(n + 1, 1 - a, b0, FLAT.index(("proj", 1, 3)))
                    await_values(*items(b0, FLAT.index(("out", 1))))
                    load_wo(n + 1, 1 - a)
                    tail(n * 2 + 1, b0, len(FLAT) - 1 - FLAT[::-1].index(("den", 1)))
                    load_w1(n + 2)
            tail(2 * NP, (NPREP + NP * NMAIN) // 2, 1)
            sp.wait_ge(ldp, 16 * (NP + 2))

            sp.wait_ge(yt_mm, 1)
            for sem_, per in ((asm[0], 64), (asm[1], 64), (asm_kq, 96)):
                sp.wait_ge(sem_, per * (NP + 1))
            for dst, name in ((wgi, "w_gate"), (wui, "w_up")):
                sp.dma_start(dst, io[name]).then_inc(wcv, 16)
            sp.dma_start(wdi.rearrange("p (k d) -> p k d", k=NH),
                         io["w_down"].rearrange("(k p) d -> p k d", p=P)).then_inc(wcv, 16)
            out_v = io["out"].rearrange("o (t p) d -> p (o t) d", p=P)
            for c in range(4):
                sp.wait_ge(x4_s, c + 1)
                sp.dma_start(out_v[:, 4 * c:4 * c + 4, :], x[:, 4 * c:4 * c + 4, :]).then_inc(st, 16)
            sp.wait_ge(st, 64)

        @block.tensor
        def _(pe):
            def transposes(k, src, bank0=0):
                for c in range(4):
                    for j in range(4):
                        last = nc.tensor.transpose(ps[:, bank0 + c, j * P:(j + 1) * P],
                                                   src[:, 4 * c + j, :], ident[:, :])
                    last.then_inc(tr, 1)

            def three_parts(out, a, b, start=True, stop=True):
                nc.tensor.matmul(out, a[0], b[0], start=start, stop=False)
                nc.tensor.matmul(out, a[1], b[0], start=False, stop=False)
                return nc.tensor.matmul(out, a[0], b[1], start=False, stop=stop)

            xn = wide[:, :].rearrange("p (t d) -> p t d", t=NT)
            pe.wait_ge(ld0, 16 * LD0)
            pe.wait_ge(ln_x, 1)
            transposes(0, xn)
            pe.wait_ge(w_split, 2)
            for i in range(2):
                for c in range(4):
                    if i == 0:
                        pe.wait_ge(tr_ev, c + 1)
                    if i == 1:
                        pe.wait_ge(qk0_ev, c + 1)
                    cols = slice(W0 + 512 * c, W0 + 512 * c + 512)
                    wc = slice(P * i, P * i + P)
                    three_parts(ps[:, 4 + c, :], (w0_hi[:, wc], w0_lo[:, wc]),
                                (xT_hi[:, cols], xT_lo[:, cols])).then_inc(qk0, 1)
            pe.wait_ge(init, 1)
            wc = slice(2 * P, 3 * P)
            for g in range(NB // 4):
                if g >= 4:
                    pe.wait_ge(v0_ev, g - 3)
                for j in range(4):
                    b = 4 * g + j
                    win = [xp[:, 2 * W0 * b:2 * W0 * b + 3 * W0] for xp in (xT_hi, xT_lo)]
                    out = ps[:, g % 4, j * P:(j + 1) * P]
                    for blk in range(2):
                        o = ps[64 * blk:64 * blk + 64, g % 4, j * P:(j + 1) * P]
                        w = [v[:, W0 * blk:W0 * blk + 2 * W0] for v in win]
                        last = three_parts(o, w, (w0_hi[:, wc], w0_lo[:, wc]))
                last.then_inc(v0, 1)

            def attn0(k, on, a, first):
                if on[0]:
                    b = k
                    pe.wait_ge(qmh, b + 1)
                    pe.wait_ge(qml, b + 1)
                    if not first or a >= 2:
                        pe.wait_ge(sub0, b - 1)
                    bank = a % 2
                    nc.tensor.matmul(ps[:, bank, :], ident_b[:, :], mask0[:, 1 if (first and a == 0) else 0, :],
                                     start=True, stop=False, skip_group_check=True)
                    for blk in range(2):
                        col = b * (2 * W0) + W0 * blk
                        kh = kT[:, 0, bass.ds(col, 2 * W0)]
                        kl = kT[:, 1, bass.ds(col, 2 * W0)]
                        for g in range(G0):
                            o = ps[:, bank, g * P + 64 * blk:g * P + 64 * blk + 64]
                            qs = slice(blk * 512 + g * P, blk * 512 + g * P + P)
                            end = blk == 1 and g == G0 - 1
                            nc.tensor.matmul(o, qm_hi[:, bank, qs], kh, start=False, stop=False, skip_group_check=True)
                            nc.tensor.matmul(o, qm_lo[:, bank, qs], kh, start=False, stop=False, skip_group_check=True)
                            last = nc.tensor.matmul(o, qm_hi[:, bank, qs], kl, start=False, stop=end,
                                                    skip_group_check=True)
                    last.then_inc(s0, 1)
                if on[1]:
                    b = k - 1
                    par = (a + 1) % 2
                    pe.wait_ge(e0, b + 1)
                    if not first or a >= 3:
                        pe.wait_ge(lo0, b - 1)
                    for g in range(G0):
                        last = nc.tensor.transpose(ps[:, 2 + par, g * P:(g + 1) * P],
                                                   exp_s[:, par, g * P:(g + 1) * P], ident[:, :])
                    last.then_inc(t0, 1)
                if on[2]:
                    b = k - 2
                    par = a % 2
                    pe.wait_ge(lo0, b + 1)
                    if not first or a >= 4:
                        pe.wait_ge(om0, b - 1)
                    for g in range(G0):
                        o = ps[:, 4 + par, g * 2 * VW:(g + 1) * 2 * VW]
                        pp = [pT[:, par, i, g * P:(g + 1) * P] for i in range(2)]
                        if isinstance(b, int):
                            vv = [v[:, b, g, :, :] for v in (v_hi, v_lo)]
                        else:
                            vv = [v[:, bass.ds(b, 1), g, :, :] for v in (v_hi, v_lo)]
                        vv = [v.rearrange("p a w -> p (a w)") if isinstance(b, int)
                              else v.rearrange("p b a w -> p (b a w)") for v in vv]
                        last = three_parts(o, pp, vv)
                    last.then_inc(pv0, 1)
                if on[3]:
                    b = k - 3
                    par = (a + 1) % 2
                    pe.wait_ge(om0, b + 1)
                    if not (first and a == 3):
                        pe.wait_ge(ot0, b)
                    for blk in range(2):
                        last = nc.tensor.matmul(ps[:, 6, blk * W0:(blk + 1) * W0],
                                                om[:, par, blk * P:(blk + 1) * P], sel[:, :], start=True, stop=True)
                    last.then_inc(sel0, 1)
                if on[4] and a % 2 == 0:
                    tile = on[4][0]
                    pe.wait_ge(ot0, tile * 2 + 2)
                    if not on[4][1]:
                        pe.wait_ge(x0, tile)
                    nc.tensor.matmul(ps[:, 7, 0:P], oT[:, :], wo0[:, :], start=True, stop=True).then_inc(y0, 1)

            run_attn0(pe, attn0)

            pe.wait_ge(ln_x, 2)
            transposes(1, xn)
            for c in range(8):
                pe.wait_ge(tr_ev, 4 + c // 2 + 1)
                if c >= 4:
                    pe.wait_ge(z_ev, c - 3)
                for j in range(2):
                    tt = 2 * c + j
                    last = nc.tensor.matmul(ps[:, 4 + c % 4, j * NZ:(j + 1) * NZ],
                                            ffT[:, tt * P:(tt + 1) * P], wz[:, :], start=True, stop=True)
                last.then_inc(z_mm, 1)
            pe.wait_ge(zw_s, 1)
            for c in range(4):
                for j in range(4):
                    last = nc.tensor.transpose(ps[:, c, j * P:(j + 1) * P], zw[:, 4 * c + j, :], ident[:, :])
                last.then_inc(zt_mm, 1)
            for c in range(4):
                pe.wait_ge(zt_ev, c + 1)
                for j in range(4):
                    tt = 4 * c + j
                    o = ps[:, 4 + c, j * P:(j + 1) * P]
                    nc.tensor.matmul(o, ffT[:, tt * P:(tt + 1) * P], wbase[:, :], start=True, stop=False)
                    last = nc.tensor.matmul(o, zwT[:, tt * P:(tt + 1) * P], wlb[:, :], start=False, stop=True)
                last.then_inc(f_mm, 1)

            pe.wait_ge(ln_x, 4)
            transposes(2, xn)
            pe.wait_ge(tr_ev, 12)

            def item(it_, a, b0, g, info):
                kind = it_[0]
                bank = MX[g % 2]
                if not banked(it_):
                    return
                if kind == "proj":
                    if it_[1:] == (0, 0):
                        pe.wait_ge(w1s, info["m"] * 2 + 2)
                    await_bank(pe, b0, g)
                    _, i, c = it_
                    cols = slice(W0 + 512 * c, W0 + 512 * c + 512)
                    last = three_parts(bank, (w1_hi[:, i, :], w1_lo[:, i, :]), (xT_hi[:, cols], xT_lo[:, cols]))
                elif kind == "value":
                    await_bank(pe, b0, g)
                    for j in range(4):
                        cols = slice(W0 + P * (4 * it_[1] + j), W0 + P * (4 * it_[1] + j) + P)
                        last = three_parts(bank[:, P * j:P * j + P], (xT_hi[:, cols], xT_lo[:, cols]),
                                           (w1_hi[:, 2, :], w1_lo[:, 2, :]))
                elif kind == "max":
                    _, h, tt, c = it_
                    if tt == 0 and c == 0:
                        pe.wait_ge(asm[h], info["m"] * 64 + 64)
                    await_bank(pe, b0, g)
                    last = nc.tensor.matmul(bank, QA[:, a, h, tt * P:(tt + 1) * P],
                                            KA[:, a, h, 512 * c:512 * c + 512], start=True, stop=True)
                elif kind == "mrow":
                    pe.wait_ge(nm_done, info["m"] * 2 + (it_[1] + 1))
                    await_bank(pe, b0, g)
                    last = nc.tensor.matmul(bank[ROW_M:ROW_M + NT, 0:P], nm[:, 1, it_[1], :], ident[:, :],
                                            start=True, stop=True)
                elif kind == "den":
                    pe.wait_ge(comb_done, info["H"] * 2 + 2)
                    await_bank(pe, b0, g)
                    cs = slice(512 * it_[1], 512 * it_[1] + 512)
                    nc.tensor.matmul(bank[0:64, :], ones1[:, :], accD[:, 0, cs], start=True, stop=True)
                    last = nc.tensor.matmul(bank[64:128, :], ones1[:, :], accD[:, 1, cs], start=True, stop=True)
                elif kind == "out":
                    if info["wo_load"] is not None:
                        pe.wait_ge(ldw, info["wo_load"] * 16 + 16)
                    pe.wait_ge(o_done, info["H"] + 1)
                    await_bank(pe, b0, g)
                    cs = slice(512 * it_[1], 512 * it_[1] + 512)
                    last = nc.tensor.matmul(bank, wo1[:, info["wo"], :], o_nrm[:, cs], start=True, stop=True)
                last.then_inc(mx_full, 1)

            def scores(a, h, Q, J):
                key = slice(J * P, J * P + P)
                for n in range(2):
                    q0 = HALF * Q + 512 * n
                    S = S1[h]
                    right = min(max(J - q0 // P, 0), 4)
                    on_diag = 0 <= J - q0 // P < 4
                    nc.tensor.matmul(S[:, 512 * n:512 * n + 512], KA[:, a, h, key], QA[:, a, h, q0:q0 + 512],
                                     start=True, stop=False, skip_group_check=True)
                    if right:
                        last = nc.tensor.matmul(S[:, 512 * n:512 * n + right * P], KR[:, a, h, key],
                                                QB[:, a, h, q0:q0 + right * P], start=False,
                                                stop=right == 4, skip_group_check=True)
                    if right < 4:
                        last = nc.tensor.matmul(S[:, 512 * n + right * P:512 * n + 512], KL[:, a, h, key],
                                                QB[:, a, h, q0 + right * P:q0 + 512], start=False,
                                                stop=not on_diag, skip_group_check=True)
                    if on_diag:
                        d = 512 * n + right * P
                        for part in range(2):
                            last = nc.tensor.matmul(S[:, d:d + P], relu_w[:, :], diag[:, a, h, part, :],
                                                    start=False, stop=part == 1, skip_group_check=True)
                return last

            def values(a, J, n):
                cs = slice(512 * n, 512 * n + 512)
                nc.tensor.matmul(PV[0:64, cs], V1[:, a, J, 0:64], Pr[:, 0, J % 2, cs],
                                 start=J == 0, stop=J == NT - 1)
                last = nc.tensor.matmul(PV[64:128, cs], V1[:, a, J, 64:128], Pr[:, 1, J % 2, cs],
                                        start=J == 0, stop=J == NT - 1)
                if n == 1:
                    last.then_inc(pv_done, 1)

            def tensor_main(it, a):
                n = it * 2 + a
                b0 = n * (NMAIN // 2) + NPREP // 2
                for s in range(2 * NT):
                    Q, J = divmod(s, NT)
                    H = it * 4 + (2 * a + Q)
                    G = H * NT + J
                    if s == 0:
                        await_items(pe, b0, -1)
                        pe.wait_ge(asm_kq, n * 96 + 96)
                        pe.wait_ge(ldt, n * 112 + 112)
                    todo = numbered(s)
                    info = {"m": n + 1, "H": H, "wo": (1 - a) if Q == 0 else a,
                            "wo_load": n if Q else None}
                    for h in range(2):
                        pe.wait_ge(exp_done, G * 2 + (h + 1))
                        scores(a, h, Q, J).then_inc(qk_done, 1)
                        for i_, g in todo[h]:
                            item(i_, 1 - a, b0, g, info)
                    for JJ in ([J - 1] if J else []) + ([J] if J == NT - 1 else []):
                        if JJ == 0:
                            pe.wait_ge(pv_evac, H + 1)
                        pe.wait_ge(exp_done, (H * NT + JJ) * 2 + 4)
                        for x_ in range(2):
                            values(a, JJ, x_)
                            if JJ < J:
                                for i_, g in todo[2 + x_]:
                                    item(i_, 1 - a, b0, g, info)

            for g, i_ in enumerate(PREP):
                item(i_, 0, 0, g, {"m": 0})
            pe.wait_ge(ldrow, 16 * 4)
            with pe.Fori(0, NP // 2) as it:
                for a in range(2):
                    tensor_main(it, a)
            b0 = (NPREP + NP * NMAIN) // 2
            info = {"H": 2 * NP, "wo": 1, "wo_load": None}
            for g, i_ in enumerate((("den", 0), ("den", 1), ("out", 0), ("out", 1))):
                item(i_, 0, b0, g, info)
            await_items(pe, b0, 3)
            for c in range(4):
                for j in range(4):
                    tt = 4 * c + j
                    last = nc.tensor.transpose(ps[:, c, j * P:(j + 1) * P], wide[:, tt * P:(tt + 1) * P], ident[:, :])
                last.then_inc(yt_mm, 1)

            pe.wait_ge(ln_x, 5)
            transposes(3, xn)
            pe.wait_ge(w_split, 5)
            for c in range(4):
                pe.wait_ge(tr_ev, 12 + c + 1)
                cols = slice(W0 + 512 * c, W0 + 512 * c + 512)
                for k in range(NH):
                    u = NH * c + k
                    if u >= 2:
                        pe.wait_ge(h_s, u - 1)
                    for i, w in enumerate((wg, wu)):
                        o = ps[:, 4 + 2 * (u % 2) + i, :]
                        nc.tensor.matmul(o, w[:, k * P:(k + 1) * P], xT_hi[:, cols], start=True, stop=False)
                        last = nc.tensor.matmul(o, w[:, k * P:(k + 1) * P], xT_lo[:, cols], start=False, stop=True)
                    last.then_inc(gu_mm, 1)
                if c:
                    down(pe, nc, c - 1, ps, hid, wd, h_s, dn_mm)
            down(pe, nc, 3, ps, hid, wd, h_s, dn_mm)

        @block.scalar
        def _(act):
            def norm(k):
                act.wait_ge(ln_c, k + 1)
                nc.scalar.activation(wide[:, :], xc_of(k), ACT.Square).then_inc(ln_sq, 1)
                act.wait_ge(ln_v, k + 1)
                nc.scalar.activation(stat[:, 4, :], stat[:, 3, :], ACT.Sqrt).then_inc(ln_sd, 1)

            def xc_of(k):
                return xc_view

            xc_view = KR[:, 0].rearrange("p h t -> p (h t)").bitcast(F32)

            norm(0)
            for c in range(4):
                act.wait_ge(tr, c + 1)
                nc.scalar.copy(xT_hi[:, W0 + 512 * c:W0 + 512 * c + 512], ps[:, c, :]).then_inc(hi_ev, 1)
            for i in range(2):
                dst = (qT[:, 0, :], kT[:, 0, W0:])[i]
                for c in range(4):
                    act.wait_ge(qk0, 4 * i + c + 1)
                    nc.scalar.copy(dst[:, 512 * c:512 * c + 512], ps[:, 4 + c, :]).then_inc(qk0_hi, 1)
            act.wait_ge(init, 2)
            for g in range(NB // 4):
                act.wait_ge(v0, g + 1)
                for blk in range(2):
                    rows = slice(64 * blk, 64 * blk + 64)
                    src = ps[rows, g % 4, :].rearrange("p (b g w) -> p (b g) w", b=4, g=G0)
                    dst = v_hi[rows, 4 * g:4 * g + 4, :, blk, 0:HG * D0].rearrange("p b g w -> p (b g) w")
                    last = nc.scalar.copy(dst, src)
                last.then_inc(v0_hi, 1)

            def attn0(k, on, a, first):
                if on[0]:
                    b = k
                    act.wait_ge(sub0, b + 1)
                    if not first or a >= 2:
                        act.wait_ge(t0, b - 1)
                    nc.scalar.activation(exp_s[:, a % 2, :], sub_s[:, a % 2, :], ACT.Exp, scale=SC0).then_inc(e0, 1)
                if on[1]:
                    b = k - 1
                    par = (a + 1) % 2
                    act.wait_ge(t0, b + 1)
                    if not first or a >= 3:
                        act.wait_ge(pv0, b - 1)
                    nc.scalar.copy(pT[:, par, 0, :], ps[:, 2 + par, :]).then_inc(hi0, 1)
                if on[3]:
                    b = k - 3
                    par = (a + 1) % 2
                    act.wait_ge(sel0, b + 1)
                    tile, is_first = on[3]
                    if par == 0 and not is_first:
                        act.wait_ge(y0, tile)
                    nc.scalar.copy(oT[:, 64 * par:64 * par + 64], ps[:, 6, 0:64]).then_inc(ot0, 1)

            run_attn0(act, attn0)

            norm(1)
            for c in range(4):
                act.wait_ge(tr, 4 + c + 1)
                nc.scalar.copy(ffT[:, 512 * c:512 * c + 512], ps[:, c, :]).then_inc(tr_ev, 1)
            for c in range(8):
                act.wait_ge(z_mm, c + 1)
                nc.scalar.copy(z[:, 2 * c:2 * c + 2, :].rearrange("p t n -> p (t n)"),
                               ps[:, 4 + c % 4, 0:2 * NZ]).then_inc(z_ev, 1)
            act.wait_ge(r_exp_in, 1)
            nc.scalar.activation(rt[:, 1].rearrange("p t e -> p (t e)"), rt[:, 0].rearrange("p t e -> p (t e)"),
                                 ACT.Exp).then_inc(r_exp, 1)
            for c in range(4):
                act.wait_ge(zt_mm, c + 1)
                nc.scalar.copy(zwT[:, 512 * c:512 * c + 512], ps[:, c, :]).then_inc(zt_ev, 1)

            norm(2)
            norm(3)
            for c in range(4):
                act.wait_ge(gbt, c + 1)
                nc.scalar.copy(xT_hi[:, W0 + 512 * c:W0 + 512 * c + 512],
                               ffT[:, 512 * c:512 * c + 512]).then_inc(hi_ev, 1)

            def item(it_, a, g0, g, m):
                kind = it_[0]
                bank = MX[g % 2]
                if kind == "proj":
                    _, i, c = it_
                    act.wait_ge(mx_full, g0 + 1 + g)
                    if i == 0 and c == 0 and not (isinstance(m, int) and m == 0):
                        act.wait_ge(asm[0], m * 64)
                        act.wait_ge(asm[1], m * 64)
                        act.wait_ge(asm_kq, m * 96)
                    nc.scalar.mul(HI[:, i, 512 * c:512 * c + 512], bank,
                                  0.125 if i == 0 else 1.0).then_inc(hi_done, 1)
                elif kind == "value":
                    act.wait_ge(mx_full, g0 + 1 + g)
                    c = it_[1]
                    nc.scalar.copy(V1[:, a, 4 * c:4 * c + 4, :].rearrange("p j d -> p (j d)"),
                                   bank).then_inc(mx_free[g % 2], 1)
                elif kind == "den":
                    act.wait_ge(mx_full, g0 + 1 + g)
                    cs = slice(512 * it_[1], 512 * it_[1] + 512)
                    nc.scalar.copy(den_sb[:, cs], bank).then_inc(mx_free[g % 2], 1)

            def scalar_main(it, a):
                n = it * 2 + a
                g0 = n * NMAIN + NPREP
                for s in range(2 * NT):
                    Q, J = divmod(s, NT)
                    H = it * 4 + (2 * a + Q)
                    G = H * NT + J
                    todo = numbered(s)
                    for h in range(2):
                        act.wait_ge(qk_done, G * 2 + (h + 2))
                        act.wait_ge(pv_done, G + 1)
                        old = (J - 2) % NT
                        Ho = H if J >= 2 else H - 1
                        if old in DVE_SUMS:
                            act.wait_ge(sum_dve, Ho * (2 * len(DVE_SUMS)) + (2 * DVE_SUMS.index(old) + h + 3))
                        else:
                            k = POOL_SUMS.index(max(old, 1))
                            act.wait_ge(sum_pool, Ho * (2 * len(POOL_SUMS)) + (2 * k + h + 3))
                        nc.scalar.activation(Pr[:, h, J % 2, :], S1[h], ACT.Exp).then_inc(exp_done, 1)
                        for i_, g in (todo[h] if h == 0 else todo[1] + todo[2] + todo[3]):
                            item(i_, 1 - a, g0, g, n + 1)
                    if J == NT - 1:
                        act.wait_ge(pv_done, G + 3)
                        act.wait_ge(o_done, H + 1)
                        nc.scalar.copy(o_raw[:, :], PV).then_inc(pv_evac, 1)

            for g, i_ in enumerate(PREP):
                item(i_, 0, 0, g, 0)
            with act.Fori(0, NP // 2) as it:
                for a in range(2):
                    scalar_main(it, a)
            for g in range(2):
                item(("den", g), 0, NPREP + NP * NMAIN, g, NP)

            norm(4)
            for c in range(4):
                act.wait_ge(tr, 12 + c + 1)
                nc.scalar.copy(xT_hi[:, W0 + 512 * c:W0 + 512 * c + 512], ps[:, c, :]).then_inc(hi_ev, 1)
            for u in range(4 * NH):
                act.wait_ge(gu_mm, u + 1)
                if u >= 2:
                    act.wait_ge(h_s, u - 1)
                nc.scalar.activation(silu[:, u % 2, :], ps[:, 4 + 2 * (u % 2), :], ACT.Silu,
                                     scale=WSCALE).then_inc(silu_s, 1)

        @block.vector
        def _(dve):
            chain = [0]

            def link(ins):
                chain[0] += 1
                ins.then_inc(dv, 1)
                dve.wait_ge(dv, chain[0])

            xcf = KR[:, 0].rearrange("p h t -> p (h t)").bitcast(F32)
            xc = xcf.rearrange("p (t d) -> p t d", t=NT)
            xn = wide[:, :].rearrange("p (t d) -> p t d", t=NT)

            def norm(k, src):
                link(nc.vector.reduce_sum(stat[:, 0, :], src, AX.X))
                link(nc.vector.tensor_scalar(stat[:, 1, :], stat[:, 0, :], -1.0 / P, None, ALU.mult))
                nc.vector.tensor_tensor(xc, src, bcast(stat[:, 1, :], 2, P), ALU.add).then_inc(ln_c, 1)
                dve.wait_ge(ln_sq, k + 1)
                link(nc.vector.reduce_sum(stat[:, 2, :], xn, AX.X))
                nc.vector.tensor_scalar(stat[:, 3, :], stat[:, 2, :], 1.0 / P, EPS, ALU.mult,
                                        ALU.add).then_inc(ln_v, 1)
                dve.wait_ge(ln_sd, k + 1)
                link(nc.vector.reciprocal(stat[:, 5, :], stat[:, 4, :]))
                nc.vector.tensor_tensor(xn, xc, bcast(stat[:, 5, :], 2, P), ALU.mult).then_inc(ln_x, 1)

            dve.wait_ge(ld0, 16 * LD0)
            norm(0, x[:, :, :])
            link(nc.vector.tensor_copy(w0_hi[:, :], w0[:, :]))
            nc.vector.tensor_tensor(w0_lo[:, :], w0[:, :], w0_hi[:, :], ALU.subtract).then_inc(w_split, 2)
            for c in range(4):
                dve.wait_ge(hi_ev, c + 1)
                cols = slice(W0 + 512 * c, W0 + 512 * c + 512)
                nc.vector.tensor_tensor(xT_lo[:, cols], ps[:, c, :], xT_hi[:, cols], ALU.subtract).then_inc(tr_ev, 1)
            for i in range(2):
                hi = (qT[:, 0, :], kT[:, 0, W0:])[i]
                lo = (qT[:, 1, :], kT[:, 1, W0:])[i]
                for c in range(4):
                    dve.wait_ge(qk0_hi, 4 * i + c + 1)
                    cs = slice(512 * c, 512 * c + 512)
                    nc.vector.tensor_tensor(lo[:, cs], ps[:, 4 + c, :], hi[:, cs], ALU.subtract).then_inc(qk0_ev, 1)
            for g in range(NB // 4):
                dve.wait_ge(v0_hi, g + 1)
                for blk in range(2):
                    rows = slice(64 * blk, 64 * blk + 64)
                    src = ps[rows, g % 4, :].rearrange("p (b g w) -> p (b g) w", b=4, g=G0)
                    cut = lambda v: v[rows, 4 * g:4 * g + 4, :, blk, 0:HG * D0].rearrange("p b g w -> p (b g) w")
                    last = nc.vector.tensor_tensor(cut(v_lo), src, cut(v_hi), ALU.subtract)
                last.then_inc(v0_ev, 1)
            dve.wait_ge(qk0_ev, 8)
            dve.wait_ge(v0_ev, NB // 4)

            hm = hmask[:, :].rearrange("p (h q) -> p h q", h=H0)

            def attn0(k, on, a, first):
                if on[0]:
                    b = k
                    par = a % 2
                    if not first or a >= 2:
                        dve.wait_ge(s0, b - 1)
                    for blk in range(2):
                        q = qT[:, 0, bass.ds(b * (2 * W0) + W0 * blk, W0)]
                        last = nc.vector.tensor_tensor(
                            qm_hi[:, par, blk * 512:blk * 512 + 512].rearrange("p (h q) -> p h q", h=H0),
                            bcast(q, 1, H0), hm, ALU.mult)
                    last.then_inc(qmh, 1)
                    dve.wait_ge(s0, b + 1)
                    sc = ps[:, par, :].rearrange("p (n k) -> p n k", k=2 * W0)
                    if not (first and a == 0):
                        dve.wait_ge(sub0, b)
                    nc.vector.reduce_max(mx0, sc, AX.X).then_inc(m0, 1)
                    dve.wait_ge(m0, b + 1)
                    if not first or a >= 2:
                        dve.wait_ge(e0, b - 1)
                    nc.vector.tensor_tensor(sub_s[:, par, :].rearrange("p (n k) -> p n k", k=2 * W0), sc,
                                            bcast(mx0, 2, 2 * W0), ALU.subtract).then_inc(sub0, 1)
                if on[1]:
                    b = k - 1
                    par = (a + 1) % 2
                    dve.wait_ge(hi0, b + 1)
                    if not first or a >= 3:
                        dve.wait_ge(pv0, b - 1)
                    nc.vector.tensor_tensor(pT[:, par, 1, :], ps[:, 2 + par, :], pT[:, par, 0, :],
                                            ALU.subtract).then_inc(lo0, 1)
                if on[2]:
                    b = k - 2
                    par = a % 2
                    dve.wait_ge(pv0, b + 1)
                    o = ps[:, 4 + par, 0:G0 * 2 * VW].rearrange("p (g a w) -> p a g w", g=G0, a=2)
                    if not (first and a == 2):
                        dve.wait_ge(om0, b)
                    rc = rc0.rearrange("p (a g) -> p a g", a=2)
                    nc.vector.reciprocal(rc, o[:, :, :, VW - 1]).then_inc(rc_s, 1)
                    t3 = om1.rearrange("p (a g w) -> p (a g) w", a=2, g=G0)
                    for blk in range(2):
                        last = nc.vector.tensor_tensor(t3[:, G0 * blk:G0 * blk + G0, :], o[:, blk, :, 0:VW - 1],
                                                       bcast(gmask[:, :], 1, G0), ALU.mult)
                    last.then_inc(om1_s, 1)
                    dve.wait_ge(rc_s, b + 1)
                    dve.wait_ge(om1_s, b + 1)
                    if not first or a >= 4:
                        dve.wait_ge(sel0, b - 1)
                    nc.vector.tensor_tensor(om[:, par, :].rearrange("p (n w) -> p n w", n=2 * G0), t3,
                                            bcast(rc0, 2, HG * D0), ALU.mult).then_inc(om0, 1)
                if on[4] and a % 2 == 0:
                    tile, _ = on[4]
                    dve.wait_ge(y0, tile + 1)
                    xt = x[:, bass.ds(tile, 1), :].rearrange("p a d -> p (a d)")
                    nc.vector.tensor_tensor(xt, ps[:, 7, 0:P], xt, ALU.add).then_inc(x0, 1)

            run_attn0(dve, attn0)
            dve.wait_ge(x0, NT)

            norm(1, x[:, :, :])
            dve.wait_ge(z_ev, 8)
            dve.wait_ge(ldc, 16 * 6)
            lg = z[:, :, NTRUE * RANK:NZ]
            link(nc.vector.reduce_max(rs[:, 0, :], lg, AX.X))
            nc.vector.tensor_tensor(rt[:, 0], lg, bcast(rs[:, 0, :], 2, NE), ALU.subtract).then_inc(r_exp_in, 1)
            dve.wait_ge(r_exp, 1)
            cur = rt[:, 1]
            for r in range(2):
                link(nc.vector.reduce_max(rs[:, 1, :], cur, AX.X))
                link(nc.vector.tensor_tensor(rt[:, 2], cur, bcast(rs[:, 1, :], 2, NE), ALU.is_equal))
                link(nc.vector.tensor_tensor(rt[:, 3], rt[:, 2], bcast(rank10[:, :], 1, NT), ALU.mult))
                link(nc.vector.reduce_max(rs[:, 2, :], rt[:, 3], AX.X))
                link(nc.vector.tensor_tensor(rt[:, 4 + r], rt[:, 3], bcast(rs[:, 2, :], 2, NE), ALU.is_equal))
                if r == 0:
                    link(nc.vector.tensor_tensor(rt[:, 6], cur, rt[:, 4], ALU.subtract))
                    link(nc.vector.tensor_tensor(rt[:, 7], rt[:, 6], rt[:, 4], ALU.subtract))
                    cur = rt[:, 7]
            link(nc.vector.tensor_tensor(rt[:, 2], rt[:, 4], rt[:, 5], ALU.add))
            link(nc.vector.tensor_tensor(rt[:, 3], rt[:, 2], rt[:, 1], ALU.mult))
            link(nc.vector.reduce_sum(rs[:, 3, :], rt[:, 3, :, 0:NTRUE], AX.X))
            link(nc.vector.tensor_scalar(rs[:, 4, :], rs[:, 3, :], 0.0, None, ALU.is_equal))
            link(nc.vector.tensor_tensor(rs[:, 5, :], rs[:, 3, :], rs[:, 4, :], ALU.add))
            link(nc.vector.reciprocal(rs[:, 6, :], rs[:, 5, :]))
            link(nc.vector.tensor_scalar(rs[:, 7, :], rs[:, 6, :], LORA_SCALE, None, ALU.mult))
            link(nc.vector.tensor_tensor(rt[:, 6], rt[:, 3], bcast(rs[:, 7, :], 2, NE), ALU.mult))
            for t8 in range(2):
                ts_ = slice(8 * t8, 8 * t8 + 8)
                last = nc.vector.tensor_tensor(
                    zw[:, ts_, :].rearrange("p t (e r) -> p t e r", e=NTRUE),
                    z[:, ts_, 0:NTRUE * RANK].rearrange("p t (e r) -> p t e r", e=NTRUE),
                    bcast(rt[:, 6, ts_, 0:NTRUE], 3, RANK), ALU.mult)
            link(last)
            nc.vector.tensor_tensor(xc, x[:, :, :], bcast(bias0[:, :], 1, NT), ALU.add).then_inc(zw_s, 1)
            dve.wait_ge(zw_s, 1)
            for c in range(4):
                dve.wait_ge(f_mm, c + 1)
                last = nc.vector.tensor_tensor(x[:, 4 * c:4 * c + 4, :].rearrange("p t d -> p (t d)"), ps[:, 4 + c, :],
                                               xc[:, 4 * c:4 * c + 4, :].rearrange("p t d -> p (t d)"), ALU.add)
            link(last)

            norm(2, x[:, :, :])
            dve.wait_ge(ln_x, 3)
            xn1 = ffT.rearrange("p (t d) -> p t d", t=NT)
            link(nc.vector.tensor_copy(xn1, xn))
            norm(3, xn1)
            for c in range(4):
                dve.wait_ge(tr, 8 + c + 1)
                cs = slice(512 * c, 512 * c + 512)
                nc.vector.tensor_scalar(ffT[:, cs], ps[:, c, :], gb[:, 0:1], gb[:, 1:2], ALU.mult,
                                        ALU.add).then_inc(gbt, 1)
                dve.wait_ge(hi_ev, 4 + c + 1)
                cols = slice(W0 + 512 * c, W0 + 512 * c + 512)
                nc.vector.tensor_tensor(xT_lo[:, cols], ffT[:, cs], xT_hi[:, cols], ALU.subtract).then_inc(tr_ev, 1)
            dve.wait_ge(tr_ev, 12)
            nc.vector.memset(QB[64:128, :, :, :].rearrange("p a h t -> p (a h t)").bitcast(F32), 0.0)
            for K in (KL, KR):
                nc.vector.memset(K[64:128, :, :, :].rearrange("p a h t -> p (a h t)").bitcast(F32), 0.0)
            nc.vector.memset(accD.rearrange("p h q -> p (h q)"), 1.0).then_inc(comb_done, 2)
            nc.vector.memset(wo1[:, :, :], 0.0)
            nc.vector.memset(ones1[:, :], 1.0)
            nc.vector.memset(o_raw[:, :], 0.0).then_inc(pv_evac, 1)
            link(nc.vector.memset(wide[:, :], 0.0))
            for K in (KL, KR):
                last = nc.vector.memset(K[ROW_M:ROW_M + NT, :, :, :].rearrange("p a h t -> p (a h t)"), M_UNIT)
            last.then_inc(init, 1)

            def item(it_, a, g0, b0, g, m, H, yhalf):
                kind = it_[0]
                bank = MX[g % 2]
                if kind == "proj":
                    _, i, c = it_
                    dve.wait_ge(hi_done, m * 8 + (4 * i + c + 1))
                    cs = slice(512 * c, 512 * c + 512)
                    nc.vector.scalar_tensor_tensor(out=LO[:, i, cs], in0=bank, scalar=0.125 if i == 0 else 1.0,
                                                   in1=HI[:, i, cs], op0=ALU.mult,
                                                   op1=ALU.subtract).then_inc(mx_free[g % 2], 1)
                elif kind == "max":
                    _, h, tt, c = it_
                    if tt == 0 and c == 0:
                        await_items(dve, b0, g - 1)
                        dve.wait_ge(ldc, 16 * 6)
                        dve.wait_ge(ldt, m * 112 + 112)
                        nc.vector.tensor_scalar(dist_h[:, :], dist[:, :], slope[:, a, h:h + 1], None,
                                                ALU.mult).then_inc(ts_done, 1)
                    ready = settled(dve, g0 + 1 + g)
                    scaled = settled(dve, m * 2 + (h + 1))
                    dve.wait_ge(ldc, 16 * 6)
                    if tt == 0 and c == 0:
                        dve.wait_ge(ts_done, scaled)
                    dve.wait_ge(mx_full, ready)
                    c0 = T - P - P * tt + 512 * c
                    nc.vector.tensor_tensor_reduce(
                        out=junk[:, g % 2, :], in0=bank, in1=dist_h[:, c0:c0 + 512], scale=1.0, scalar=-3.0e38,
                        op0=ALU.add, op1=ALU.max, accum_out=mx2[:, h, tt, c:c + 1]).then_inc(mx_free[g % 2], 1)
                    if tt == NT - 1 and c == 3:
                        await_items(dve, b0, g)
                        nc.vector.reduce_max(nm[:, 0, h, :], mx2[:, h, :, :], AX.X).then_inc(nm1, 1)
                        dve.wait_ge(nm1, m * 2 + (h + 1))
                        nc.vector.tensor_scalar(nm[:, 1, h, :], nm[:, 0, h, :], -1.0 / M_UNIT, None,
                                                ALU.mult).then_inc(nm_done, 1)
                elif kind == "mrow":
                    h = it_[1]
                    rows = slice(ROW_M, ROW_M + NT)
                    dve.wait_ge(mx_full, g0 + 1 + g)
                    nc.vector.tensor_tensor(QB[rows, a, h, :].rearrange("p (t q) -> p t q", t=NT),
                                            bcast(bank[rows, 0:P], 1, NT), bcast(bmask[rows, :], 2, P),
                                            ALU.mult).then_inc(mx_free[g % 2], 1)
                elif kind == "recip":
                    dve.wait_ge(den_dma, H * 32 + 32)
                    nc.vector.reciprocal(rec_c[:, :, :], den_c[:, :, :]).then_inc(rec_done, 1)
                elif kind == "scale":
                    dve.wait_ge(rb_dma, H * 32 + 32)
                    dve.wait_ge(pv_evac, H + 1)
                    nc.vector.tensor_tensor(o_nrm[:, :], o_raw[:, :], rec_b[:, :], ALU.mult).then_inc(o_done, 1)
                elif kind == "out":
                    dve.wait_ge(mx_full, g0 + 1 + g)
                    cs = slice(HALF * yhalf + 512 * it_[1], HALF * yhalf + 512 * it_[1] + 512)
                    nc.vector.tensor_tensor(wide[:, cs], bank, wide[:, cs], ALU.add).then_inc(mx_free[g % 2], 1)

            def vector_sum(H, J):
                k = DVE_SUMS.index(J)
                for h in range(2):
                    dve.wait_ge(exp_done, (H * NT + J) * 2 + (h + 3))
                    if k == 0:
                        nc.vector.tensor_copy(accD[:, h, :], Pr[:, h, J % 2, :]).then_inc(sum_dve, 1)
                    else:
                        dve.wait_ge(sum_dve, H * (2 * len(DVE_SUMS)) + (2 * k + h + 1))
                        nc.vector.tensor_tensor(accD[:, h, :], accD[:, h, :], Pr[:, h, J % 2, :],
                                                ALU.add).then_inc(sum_dve, 1)

            def vector_main(it, a):
                n = it * 2 + a
                g0 = n * NMAIN + NPREP
                b0 = n * (NMAIN // 2) + NPREP // 2
                for s in range(2 * NT):
                    Q, J = divmod(s, NT)
                    H = it * 4 + (2 * a + Q)
                    for k, todo in enumerate(numbered(s)):
                        for i_, g in todo:
                            item(i_, 1 - a, g0, b0, g, n + 1, H, 1 - Q)
                        if k == 1 and J - 1 in DVE_SUMS:
                            vector_sum(H, J - 1)
                    if J == NT - 1:
                        vector_sum(H, J)
                        for h in range(2):
                            dve.wait_ge(sum_pool, H * (2 * len(POOL_SUMS)) + (2 * len(POOL_SUMS) + 2))
                            dve.wait_ge(sum_dve, H * (2 * len(DVE_SUMS)) + (2 * len(DVE_SUMS) + 2))
                            nc.vector.tensor_tensor(accD[:, h, :], accD[:, h, :], accP[:, h, :],
                                                    ALU.add).then_inc(comb_done, 1)

            for g, i_ in enumerate(PREP):
                item(i_, 0, 0, 0, g, 0, 0, 0)
            with dve.Fori(0, NP // 2) as it:
                for a in range(2):
                    vector_main(it, a)
            g0 = NPREP + NP * NMAIN
            for i_, g in ((("recip",), 0), (("scale",), 0), (("out", 0), 2), (("out", 1), 3)):
                item(i_, 0, g0, g0 // 2, g, 0, 2 * NP, 1)
            for c in range(4):
                dve.wait_ge(yt_mm, c + 1)
                xs = x[:, 4 * c:4 * c + 4, :].rearrange("p t d -> p (t d)")
                last = nc.vector.tensor_tensor(xs, ps[:, c, :], xs, ALU.add)
            link(last)

            dve.wait_ge(asm_kq, 96 * (NP + 1))
            dve.wait_ge(ldt, 112 * (NP + 1))
            norm(4, x[:, :, :])
            dve.wait_ge(wcv, 48)
            for dst, src in ((wg, wgi), (wu, wui), (wd.rearrange("p k d -> p (k d)"), wdi)):
                nc.vector.tensor_copy(dst, src).then_inc(w_split, 1)
            for c in range(4):
                dve.wait_ge(hi_ev, 8 + c + 1)
                cols = slice(W0 + 512 * c, W0 + 512 * c + 512)
                nc.vector.tensor_tensor(xT_lo[:, cols], ps[:, c, :], xT_hi[:, cols], ALU.subtract).then_inc(tr_ev, 1)
            for c in range(4):
                for k in range(NH):
                    u = NH * c + k
                    dve.wait_ge(silu_s, u + 1)
                    nc.vector.scalar_tensor_tensor(out=hid[:, k, 512 * c:512 * c + 512],
                                                   in0=ps[:, 5 + 2 * (u % 2), :], scalar=WSCALE,
                                                   in1=silu[:, u % 2, :], op0=ALU.mult, op1=ALU.mult).then_inc(h_s, 1)
                if c:
                    residual(dve, nc, c - 1, ps, x, dn_mm, x4_s)
            residual(dve, nc, 3, ps, x, dn_mm, x4_s)

        @block.gpsimd
        def _(pool):
            nc.gpsimd.memset(xT_hi[:, 0:W0], 0.0)
            nc.gpsimd.memset(kT[:, :, 0:W0], 0.0)
            nc.gpsimd.memset(xT_lo[:, 0:W0], 0.0).then_inc(init, 1)
            pool.wait_ge(init, 1)
            nc.gpsimd.memset(v_hi.rearrange("p b g a w -> p (b g a w)"), 0.0)
            nc.gpsimd.memset(v_lo.rearrange("p b g a w -> p (b g a w)"), 0.0).then_inc(xb_s, 1)
            pool.wait_ge(xb_s, 1)
            nc.gpsimd.memset(v_hi[0:64, :, :, 0, VW - 1], 1.0).then_inc(xb_s, 1)
            pool.wait_ge(xb_s, 2)
            nc.gpsimd.memset(v_hi[64:128, :, :, 1, VW - 1], 1.0).then_inc(init, 1)
            pool.wait_ge(init, 2)

            hm = hmask[:, :].rearrange("p (h q) -> p h q", h=H0)
            pool.wait_ge(ld0, 16 * LD0)
            pool.wait_ge(qk0_ev, 4)

            def attn0(k, on, a, first):
                if on[0]:
                    b = k
                    par = a % 2
                    if not first or a >= 2:
                        pool.wait_ge(s0, b - 1)
                    for blk in range(2):
                        q = qT[:, 1, bass.ds(b * (2 * W0) + W0 * blk, W0)]
                        last = nc.gpsimd.tensor_tensor(
                            qm_lo[:, par, blk * 512:blk * 512 + 512].rearrange("p (h q) -> p h q", h=H0),
                            bcast(q, 1, H0), hm, ALU.mult)
                    last.then_inc(qml, 1)

            run_attn0(pool, attn0)

            def split(m):
                loaded = settled(pool, m * 16 + 16)
                pool.wait_ge(w1c, 1)
                pool.wait_ge(ldp, loaded)
                nc.gpsimd.tensor_copy(w1_hi[:, :, :], w1[:, :, :]).then_inc(w1s, 1)
                pool.wait_ge(w1s, m * 2 + 1)
                nc.gpsimd.tensor_tensor(w1_lo[:, :, :], w1[:, :, :], w1_hi[:, :, :], ALU.subtract).then_inc(w1s, 1)
                pool.wait_ge(w1s, m * 2 + 2)
                nc.gpsimd.memset(tick[:, :], 0.0).then_inc(w1c, 2)

            def pool_main(it, a):
                n = it * 2 + a
                await_items(pool, n * (NMAIN // 2) + NPREP // 2, -1)
                split(n + 1)
                for Q in range(2):
                    H = it * 4 + (2 * a + Q)
                    for k, J in enumerate(POOL_SUMS):
                        for h in range(2):
                            pool.wait_ge(exp_done, (H * NT + J) * 2 + (h + 3))
                            own = H * (2 * len(POOL_SUMS))
                            if k == 0:
                                pool.wait_ge(comb_done, H * 2 + (h + 1))
                                nc.gpsimd.tensor_tensor(accP[:, h, :], Pr[:, h, 0, :], Pr[:, h, 1, :],
                                                        ALU.add).then_inc(sum_pool, 1)
                            else:
                                pool.wait_ge(sum_pool, own + (2 * k + h + 1))
                                nc.gpsimd.tensor_tensor(accP[:, h, :], accP[:, h, :], Pr[:, h, J % 2, :],
                                                        ALU.add).then_inc(sum_pool, 1)

            nc.gpsimd.memset(tick[:, :], 0.0).then_inc(qk_done, 1)
            pool.wait_ge(qk_done, 1)
            for s_, v in ((exp_done, 2), (pv_done, 2), (sum_pool, 2), (sum_dve, 2), (mx_free[0], 1), (mx_free[1], 1),
                          (w1c, 1)):
                nc.gpsimd.memset(tick[:, :], 0.0).then_inc(s_, v)
                pool.wait_ge(s_, v)
            split(0)
            with pool.Fori(0, NP // 2) as it:
                for a in range(2):
                    pool_main(it, a)


def settled(eng, value):
    if not isinstance(value, int):
        eng.compute_val(value)
    return value


def down(pe, nc, c, ps, hid, wd, h_s, dn_mm):
    pe.wait_ge(h_s, NH * (c + 1))
    for j in range(4):
        t = 4 * c + j
        for k in range(NH):
            last = nc.tensor.matmul(ps[:, c, j * P:(j + 1) * P], hid[:, k, t * P:(t + 1) * P], wd[:, k, :],
                                    start=k == 0, stop=k == NH - 1)
    last.then_inc(dn_mm, 1)


def residual(dve, nc, c, ps, x, dn_mm, x4_s):
    dve.wait_ge(dn_mm, c + 1)
    xs = x[:, 4 * c:4 * c + 4, :].rearrange("p t d -> p (t d)")
    nc.vector.scalar_tensor_tensor(out=xs, in0=ps[:, c, :], scalar=WSCALE, in1=xs, op0=ALU.mult,
                                   op1=ALU.add).then_inc(x4_s, 1)


def run_attn0(eng, step):
    last = 3
    steady = 6

    def on(k, base=None):
        flags = []
        for j in range(5):
            b = k - min(j, 3)
            live = 0 <= b < NB
            if base is not None:
                live = True
            if live and j >= 3:
                tile = b // 2 if base is None else base + (b // 2)
                flags.append((tile, base is None and tile == 0))
            else:
                flags.append(live)
        return flags

    for k in range(steady):
        step(k, on(k), k, True)
    n = (NB - steady) // 2
    with eng.Fori(0, n) as i:
        for s in range(2):
            flags = on(steady + s, i)
            step(i * 2 + (steady + s), flags, (steady + s), False)
    for k in range(NB, NB + last):
        step(k, on(k), k, False)


def constants():
    c = {}
    c["ident"] = np.eye(P, dtype=np.float32)
    c["ident_b"] = bf16_bits(np.eye(P, dtype=np.float32))
    d = np.arange(P)
    c["hmask"] = np.repeat((d[:, None] // D0 == np.arange(H0)[None, :]), W0, axis=1).astype(np.float16)
    c["gmask"] = (d[:, None] // W0 == np.arange(HG * D0)[None, :] // D0).astype(np.float32)
    c["sel"] = (d[:, None] % W0 == np.arange(W0)[None, :]).astype(np.float32)
    ti, tj = (d % W0)[:, None], np.arange(2 * W0)[None, :]
    band = (tj >= ti + 1) & (tj <= ti + W0)
    first = band & (tj >= W0)
    mask = np.zeros((P, 2, G0, 2, 2 * W0), np.float32)
    mask[:, :] = np.where(band, 0.0, -1e30)[:, None, None, None, :]
    mask[:, 1, :, 0, :] = np.where(first, 0.0, -1e30)[:, None, :]
    c["mask0"] = bf16_bits(mask.reshape(P, 2, 512))
    c["rank10"] = np.tile(NE - np.arange(NE, dtype=np.float32), (P, 1))
    col = np.arange(TW)
    c["dist"] = (-np.abs(d[:, None] - col[None, :] + (T - P))).astype(np.float16)
    c["relu_w"] = np.maximum(d[None, :] - d[:, None], 0).astype(np.float16)
    bm = np.zeros((P, NT), np.float32)
    bm[ROW_M:ROW_M + NT] = np.eye(NT)
    c["bmask"] = bm
    n_seq = np.arange(H1, 0, -1).astype(np.float32)
    slopes = (np.float32(2.0) ** (np.float32(-8.0) / n_seq)).astype(np.float32).astype(np.float64)

    def parts(v, n):
        out = []
        for _ in range(n):
            p = v.astype(np.float16).astype(np.float64)
            out.append(p)
            v = v - p
        return np.stack(out)

    pos = np.arange(T) - CENTRE
    rows = np.zeros((NA, T))
    rows[0:3] = pos / 1024.0
    rows[3:6] = 1.0
    c["pos_rows"] = rows.astype(np.float16)
    left = np.zeros((H1, NA, T))
    for h in range(H1):
        left[h, 0:3] = parts(-slopes[h:h + 1] * 1024.0, 3)
        left[h, 3:6] = parts(slopes[h] * pos, 3)
    pad = lambda a: np.concatenate([a, a[:1]])
    c["alibi_l"] = pad(left.reshape(NP, 2, NA, T)).astype(np.float16)
    c["alibi_r"] = pad(-left.reshape(NP, 2, NA, T)).astype(np.float16)
    dg = np.zeros((H1, P, 2, P))
    for h in range(H1):
        for i, p in enumerate(parts(-2.0 * slopes[h:h + 1], 2)):
            dg[h, :, i, :] = np.eye(P) * p
    c["diag"] = pad(dg.reshape(NP, 2, P, 2, P)).astype(np.float16)
    c["slope"] = pad(np.tile(slopes.astype(np.float32).reshape(NP, 1, 2), (1, P, 1)))
    return c


def bf16_bits(a):
    return (np.ascontiguousarray(a, np.float32).view(np.uint32) >> 16).astype(np.uint16)


def layout(v):
    pairs = lambda w: w.reshape(P, NP, P).transpose(1, 0, 2)
    pad = lambda a: np.concatenate([a, a[:1]])
    out = {
        "x": v["L0_attn_x"], "w_qkv": v["L0_attn_w_qkv"], "w_out": v["L0_attn_w_out"],
        "wz": np.concatenate([v["L0_ffn_lora_A"].reshape(NTRUE * RANK, P), v["L0_ffn_gate_w"]]).T,
        "wbase": v["L0_ffn_base_w"].T,
        "wlb": v["L0_ffn_lora_B"].transpose(0, 2, 1).reshape(NTRUE * RANK, P),
        "bias0": np.broadcast_to(v["L0_ffn_base_b"], (P, P)),
        "gb": np.stack([v["L1_attn_ln_gamma"], v["L1_attn_ln_beta"]], axis=1),
        "w1": pad(pad(np.stack([pairs(v["L1_attn_Wq"]), pairs(v["L1_attn_Wk"]), pairs(v["L1_attn_Wv"])], axis=2))),
        "wo1": pad(v["L1_attn_Wo"].reshape(NP, P, P)),
        "w_gate": v["L1_ffn_w_gate"].T, "w_up": v["L1_ffn_w_up"].T, "w_down": v["L1_ffn_w_down"].T,
    }
    return {k: np.ascontiguousarray(a) for k, a in out.items()}


def kernel(**inputs):
    import concourse.bacc as _bacc
    from concourse.bass_utils import run_bass_kernel_spmd as _run

    nc = _bacc.Bacc("TRN2", target_bir_lowering=False, num_devices=1)
    arrays = layout({k: np.asarray(a) for k, a in inputs.items()})
    arrays.update(constants())
    io = {n: nc.dram_tensor(f"in_{n}", a.shape, mybir.dt.from_np(a.dtype), kind="ExternalInput").ap()
          for n, a in arrays.items()}
    io["out"] = nc.dram_tensor("out", (1, T, P), F32, kind="ExternalOutput").ap()
    build(nc, io)
    r = _run(nc, [{f"in_{n}": a for n, a in arrays.items()}], core_ids=[0])
    return r.results[0]["out"]
```

```python
import math
from contextlib import ExitStack

import concourse.bass as bass
import numpy as np
from concourse import mybir

F32 = mybir.dt.float32
F16 = mybir.dt.float16
BF16 = mybir.dt.bfloat16
I32 = mybir.dt.int32
U16 = mybir.dt.uint16
ALU = mybir.AluOpType
ACT = mybir.ActivationFunctionType
AX = mybir.AxisListType

P = 128
T = 2048
NT = T // P
EPS = 1e-5

W0 = 32
H0 = 16
D0 = P // H0
G0 = 4
HG = H0 // G0
NB = T // (2 * W0)
SC0 = float(D0) ** -0.5
VW = HG * D0 + 1

NE, NTRUE, RANK = 10, 8, 16
NZ = NTRUE * RANK + NE
LORA_SCALE = 2.0

H1 = 16
D1 = 64
NP = H1 // 2
HALF = 1024
CENTRE = T // 2
TW = 2 * T - P
ROW_M = 64
ROW_A = 96
NA = 6
M_UNIT = 64.0
M_UNIT_TWICE = float(np.array([M_UNIT] * 2, np.float16).view(np.float32)[0])

NORM_OF = (0, 1, 3, 4)

HID = 384
NH = HID // P
WSCALE = 1.0 / 127.0

POOL_SUMS = [1, 2, 4, 5, 6, 8, 9, 10, 12, 13, 14]
DVE_SUMS = [3, 7, 11, 15]
ND = len(DVE_SUMS)
SCALE_AFTER = 6


def bcast(ap, dim, n):
    a = ap.unsqueeze(dim)
    shape = list(a.shape)
    shape[dim] = n
    return a.broadcast_to(shape)


def prep_items():
    items = [("proj", i, c) for i in range(2) for c in range(T // 512)]
    items += [("value", c) for c in range(T // 512)]
    for h in range(2):
        for t in range(NT):
            items += [("max", h, t, c) for c in range(T // 512)]
            if h == 1 and t == 0:
                items.append(("mrow", 0))
    items.append(("mrow", 1))
    return items


MAX_FROM = 26
SLOT_TIME = 1.9
BACKLOG = 1.4
SLOTS = 4


def main_schedule():
    prep = prep_items()
    slots = [[] for _ in range(2 * NT * SLOTS)]
    for i in range(12):
        slots[SLOTS + 2 + i].append(prep[i])
    rest = prep[12:]

    for q in range(2):
        base = q * NT * SLOTS
        for k, item in ((2 * SLOTS + 2, ("den", 0)), (2 * SLOTS + 3, ("den", 1)), (4 * SLOTS + 1, ("recip",)),
                        (8 * SLOTS + 3, ("out", 0)), (9 * SLOTS + 1, ("out", 1))):
            slots[base + k].append(item)

    end = len(slots) - SLOTS
    open_ = [k for k in range(MAX_FROM, end) if k // SLOTS % NT or k % SLOTS < 2]
    backlog, at = 0.0, 0
    for k in range(MAX_FROM, end):
        J, part = k // SLOTS % NT, k % SLOTS
        backlog = max(0.0, backlog - SLOT_TIME)
        backlog += (J == 0 or J - 1 in DVE_SUMS) + 2 * (J == 1 and part < 2) + len(slots[k])
        if k not in open_:
            continue
        quota = math.ceil((len(rest) - 1) * min(1, (open_.index(k) + 1) / (len(open_) - 2)))
        placed = 0
        while at < quota and (placed < 2 and backlog <= BACKLOG or k == end - 1):
            item = rest[at]
            slots[k].append(item)
            backlog = max(0.0, backlog - 0.35) + 1
            if item[0] == "mrow":
                backlog += 2.5
            elif item[2:] == (0, 0):
                backlog += 2
            at += 1
            placed += 1
    slots[end + 1].append(rest[-1])
    return slots


def banked(item):
    return item[0] != "recip"


PREP = prep_items()
SCHED = main_schedule()
TAILS = [[x for x in s if x[0] in ("den", "recip", "out")] for s in SCHED]
FLAT, FLAT_TAILS = ([x for s in k for x in s if banked(x)] for k in (SCHED, TAILS))
NPREP = len(PREP)
NMAIN = len(FLAT)
NALL = NPREP + (NP - 1) * NMAIN + len(FLAT_TAILS)
assert NPREP % 2 == 0 and NMAIN % 2 == 0 and NALL % 2 == 0


def is_last(n):
    return isinstance(n, int) and n == NP - 1


def numbered(s, n):
    sched = TAILS if is_last(n) else SCHED
    g = sum(banked(x) for k in sched[:SLOTS * s] for x in k)
    out = []
    for k in sched[SLOTS * s:SLOTS * s + SLOTS]:
        out.append([])
        for x in k:
            out[-1].append((x, g))
            g += banked(x)
    return out


def build(nc, io):
    ctx = ExitStack()
    with ctx:
        def sb(name, shape, dt):
            return ctx.enter_context(nc.sbuf_tensor(name, shape, dt))

        def sem(name):
            return ctx.enter_context(nc.semaphore(name))

        ps = ctx.enter_context(nc.psum_tensor("ps", [P, 8, 512], F32))

        x = sb("x", [P, NT, P], F32)
        ident = sb("ident", [P, P], F32)
        stat = sb("stat", [P, 8, NT], F32)
        xT_hi = sb("xT_hi", [P, W0 + T], F16)
        xT_lo = sb("xT_lo", [P, W0 + T], F16)
        wide = sb("wide", [P, T], F32)

        QA = sb("QA", [P, 2, 2, T], F16)
        KA = sb("KA", [P, 2, 2, T], F16)
        QB = sb("QB", [P, 2, 2, T], F16)
        KL = sb("KL", [P, 2, 2, T], F16)
        KR = sb("KR", [P, 2, 2, T], F16)
        arena = sb("arena", [P, 16384], F32)
        A16 = arena[:, :].bitcast(F16)

        HI = A16[:, 0:4096].rearrange("p (i t) -> p i t", i=2)
        LO = A16[:, 4096:8192].rearrange("p (i t) -> p i t", i=2)
        V1 = arena[:, 4096:8192].rearrange("p (a j d) -> p a j d", a=2, j=NT)
        Pr = arena[:, 8192:12288].rearrange("p (h a q) -> p h a q", h=2, a=2)
        accP = arena[:, 12288:14336].rearrange("p (h q) -> p h q", h=2)
        accD = arena[:, 14336:16384].rearrange("p (h q) -> p h q", h=2)
        o_raw = sb("o_raw", [P, HALF], F32)
        o_nrm = sb("o_nrm", [P, HALF], F32)
        dist = sb("dist", [P, TW], F16)
        dist_h = sb("dist_h", [P, TW], F16)
        junk = sb("junk", [P, 2, 512], F16)
        diag = sb("diag", [P, 2, 2, 2, P], F16)
        relu_w = sb("relu_w", [P, P], F16)
        w1 = sb("w1", [P, 3, P], F32)
        w1_hi = sb("w1_hi", [P, 3, P], F16)
        w1_lo = sb("w1_lo", [P, 3, P], F16)
        wo1 = sb("wo1", [P, 2, P], F32)
        slope = sb("slope", [P, 2, 2], F32)
        mx2 = sb("mx2", [P, 2, NT, 4], F32)
        den_c = sb("den_c", [P, 2, HALF // P], F32)
        rec_c = sb("rec_c", [P, 2, HALF // P], F32)
        den_sb = rec_b = o_nrm
        rec_row = nc.dram_tensor("rec_row", (2, HALF), F32, kind="Internal").ap()
        nm = sb("nm", [P, 2, 2, NT], F32)
        bmask = sb("bmask", [P, NT], F32)
        tick = sb("tick", [P, 1], F32)
        ones1 = sb("ones1", [P, D1], F32)
        gb = sb("gb", [P, 2], F32)

        kT = A16[:, 0:2 * (W0 + T)].rearrange("p (a t) -> p a t", a=2)
        qT = A16[:, 4160:4160 + 2 * T].rearrange("p (a t) -> p a t", a=2)
        o1 = 8256
        nv = NB * G0 * 2 * VW
        v_hi = A16[:, o1:o1 + nv].rearrange("p (b g a w) -> p b g a w", b=NB, g=G0, a=2)
        v_lo = A16[:, o1 + nv:o1 + 2 * nv].rearrange("p (b g a w) -> p b g a w", b=NB, g=G0, a=2)
        R32 = QA[:, 0].rearrange("p h t -> p (h t)").bitcast(F32)
        R32b = QA[:, 1].rearrange("p h t -> p (h t)").bitcast(F32)
        RK = KA[:, 0].rearrange("p h t -> p (h t)")
        RK2 = KA[:, 1].rearrange("p h t -> p (h t)").bitcast(F32)
        sub_s = R32[:, 0:1024].rearrange("p (a n) -> p a n", a=2)
        exp_s = R32[:, 1024:2048].rearrange("p (a n) -> p a n", a=2)
        pT = RK[:, 0:2048].rearrange("p (a c n) -> p a c n", a=2, c=2)
        qm_lo = R32b[:, 0:1024].bitcast(F16).rearrange("p (c n) -> p c n", c=2)
        qm_hi = R32b[:, 1024:2048].bitcast(F16).rearrange("p (c n) -> p c n", c=2)
        om1 = RK2[:, 0:256]
        om = RK2[:, 256:768].rearrange("p (a n) -> p a n", a=2)
        oT = RK2[:, 768:896]
        mx0 = RK2[:, 896:904]
        rc0 = RK2[:, 904:912]

        QBh = QB[:, :, :, :].rearrange("p a h t -> p (a h t)")
        QBf = QBh.bitcast(F32)
        mask0 = QBf[:, 0:512].bitcast(BF16).rearrange("p (v n) -> p v n", v=2)
        ident_b = QBf[:, 512:576].bitcast(BF16)
        hmask = QBh[:, 1152:1152 + H0 * W0]
        gmask = QBf[:, 832:864]
        sel = QBf[:, 864:896]
        w0 = QBf[:, 896:1280]
        w0_hi = QBh[:, 2560:2944]
        w0_lo = QBh[:, 2944:3328]
        wo0 = QBf[:, 1664:1792]
        wz = QBf[:, 1792:1792 + NZ]
        wbase = QBf[:, 1936:2064]
        wlb = QBf[:, 2064:2192]
        bias0 = QBf[:, 2192:2320]
        rank10 = QBf[:, 2320:2330]

        ffT = arena[:, 0:2048]
        z = arena[:, 2048:2048 + NT * NZ].rearrange("p (t n) -> p t n", t=NT)
        zw = arena[:, 4352:6400].rearrange("p (t n) -> p t n", t=NT)
        zwT = arena[:, 6400:8448]
        rt = arena[:, 8448:8448 + 8 * NT * NE].rearrange("p (k t e) -> p k t e", k=8, t=NT)
        rs = arena[:, 10240:10240 + 8 * NT].rearrange("p (k t) -> p k t", k=8)

        wgi = arena[:, 0:HID].bitcast(I32)
        wui = arena[:, HID:2 * HID].bitcast(I32)
        wdi = arena[:, 2 * HID:3 * HID].bitcast(I32)
        wg = A16[:, 4096:4096 + HID]
        wu = A16[:, 4096 + HID:4096 + 2 * HID]
        wd = arena[:, 2560:2560 + HID].rearrange("p (k d) -> p k d", k=NH)
        silu = arena[:, 4096:4096 + 2 * 512].rearrange("p (a n) -> p a n", a=2)
        hid = arena[:, 6144:6144 + NH * T].rearrange("p (k t) -> p k t", k=NH)

        ldx = sem("ldx")
        ld0 = sem("ld0")
        ldc = sem("ldc")
        dv = sem("dv")
        ln_c, ln_sq, ln_v, ln_sd = sem("ln_c"), sem("ln_sq"), sem("ln_v"), sem("ln_sd")
        ln_x = sem("ln_x")
        tr = sem("tr")
        tr_ev = sem("tr_ev")
        gbt = sem("gbt")
        hi_ev = sem("hi_ev")
        w_split = sem("w_split")
        init = sem("init")
        set_up = sem("set_up")
        qk0, qk0_hi, qk0_ev = sem("qk0"), sem("qk0_hi"), sem("qk0_ev")
        v0, v0_hi, v0_ev = sem("v0"), sem("v0_hi"), sem("v0_ev")
        qmh, qml, s0, m0, sub0, e0 = (sem(n) for n in ("qmh", "qml", "s0", "m0", "sub0", "e0"))
        t0, hi0, lo0, pv0, rc_s, om1_s, om0 = (sem(n) for n in ("t0", "hi0", "lo0", "pv0", "rc_s", "om1_s", "om0"))
        sel0, ot0, y0, x0 = (sem(n) for n in ("sel0", "ot0", "y0", "x0"))
        z_mm, z_ev, r_exp, r_exp_in, zw_s, zt_mm, zt_ev, f_mm, xb_s = (
            sem(n) for n in ("z_mm", "z_ev", "r_exp", "r_exp_in", "zw_s", "zt_mm", "zt_ev", "f_mm", "xb_s"))
        ldrow = sem("ldrow")
        ldp = sem("ldp")
        ldt = sem("ldt")
        ldw = sem("ldw")
        w1s = sem("w1s")
        w1c = sem("w1c")
        mx_full = sem("mx_full")
        mx_free = [sem("mx_free0"), sem("mx_free1")]
        hi_done = sem("hi_done")
        asm = [sem("asm_a"), sem("asm_b")]
        asm_kq = sem("asm_kq")
        ts_done, nm1, nm_done = sem("ts_done"), sem("nm1"), sem("nm_done")
        qk_done, exp_done, pv_done, pv_evac = (sem(n) for n in ("qk_done", "exp_done", "pv_done", "pv_evac"))
        sum_pool, sum_dve, comb_done = sem("sum_pool"), sem("sum_dve"), sem("comb_done")
        o_done = sem("o_done")
        den_dma, rec_done, row_dma, rb_dma = (
            sem(n) for n in ("den_dma", "rec_done", "row_dma", "rb_dma"))
        yt_mm, x3_s = sem("yt_mm"), sem("x3_s")
        wcv, gu_mm, silu_s, h_s, dn_mm, x4_s, st = (
            sem(n) for n in ("wcv", "gu_mm", "silu_s", "h_s", "dn_mm", "x4_s", "st"))

        LD0 = 11
        block = ctx.enter_context(nc.Block())

        MX = [ps[:, 6, :], ps[:, 7, :]]
        S1 = [ps[:, 2 * h:2 * h + 2, :].rearrange("p b n -> p (b n)") for h in range(2)]
        PV = ps[:, 4:6, :].rearrange("p b n -> p (b n)")

        def await_bank(eng, b0, g):
            eng.wait_ge(mx_free[g % 2], b0 + (g // 2 + 1))

        def await_items(eng, b0, g):
            eng.wait_ge(mx_free[0], b0 + (g // 2 + 2))
            eng.wait_ge(mx_free[1], b0 + ((g + 1) // 2 + 1))

        @block.sync
        def _(sp):
            def await_values(*pairs):
                counts = [settled(sp, v) for _, v in pairs]
                sp.wait_ge(init, 3)
                for (s_, _), v in zip(pairs, counts):
                    sp.wait_ge(s_, v)

            def items(b0, g):
                return (mx_free[0], b0 + (g // 2 + 2)), (mx_free[1], b0 + ((g + 1) // 2 + 1))

            sp.dma_start(x[:, :, :], io["x"].rearrange("o (t p) d -> p (o t) d", p=P)).then_inc(ldx, 16)
            for dst, name in ((w0, "w_qkv"), (wo0, "w_out"), (ident, "ident"), (ident_b.bitcast(U16), "ident_b"),
                              (hmask, "hmask"), (gmask, "gmask"), (sel, "sel"), (wz, "wz"),
                              (wbase, "wbase"), (wlb, "wlb")):
                sp.dma_start(dst[:, :], io[name]).then_inc(ld0, 16)
            sp.dma_start(mask0.bitcast(U16), io["mask0"]).then_inc(ld0, 16)
            for dst, name in ((dist, "dist"), (relu_w, "relu_w"), (gb, "gb"), (bias0, "bias0"),
                              (rank10, "rank10"), (bmask, "bmask")):
                sp.dma_start(dst[:, :], io[name]).then_inc(ldc, 16)

            sp.wait_ge(init, 3)
            for a in range(2):
                for h in range(2):
                    sp.dma_start(QB[ROW_A:ROW_A + NA, a, h, :], io["pos_rows"]).then_inc(ldrow, 16)

            def load_w1(m):
                await_values((w1c, m * 2 + 1))
                sp.dma_start(w1[:, :, :], io["w1"][m]).then_inc(ldp, 16)

            def load_tables(m, a):
                if not (isinstance(m, int) and m == 0):
                    await_values((qk_done, m * (4 * NT) + (2 - 4 * NT)), (ts_done, m * 2))
                for h in range(2):
                    sp.dma_start(KL[ROW_A:ROW_A + NA, a, h, :], io["alibi_l"][m, h]).then_inc(ldt, 16)
                    sp.dma_start(KR[ROW_A:ROW_A + NA, a, h, :], io["alibi_r"][m, h]).then_inc(ldt, 16)
                    sp.dma_start(diag[:, a, h, :, :], io["diag"][m, h]).then_inc(ldt, 16)
                sp.dma_start(slope[:, a, :], io["slope"][m]).then_inc(ldt, 16)

            def load_wo(m, a):
                sp.dma_start(wo1[:, a, :], io["wo1"][m]).then_inc(ldw, 16)

            def assemble(m, a, b0, g):
                await_values((hi_done, m * 8 + 8), *items(b0, g))
                for h in range(2):
                    rows = slice(64 * h, 64 * h + 64)
                    sp.dma_start(QA[0:64, a, h, :], HI[rows, 0, :]).then_inc(asm[h], 16)
                    sp.dma_start(QA[64:128, a, h, :], LO[rows, 0, :]).then_inc(asm[h], 16)
                    sp.dma_start(KA[0:64, a, h, :], HI[rows, 1, :]).then_inc(asm[h], 16)
                    sp.dma_start(KA[64:128, a, h, :], HI[rows, 1, :]).then_inc(asm[h], 16)

            def assemble_second(a):
                for h in range(2):
                    rows = slice(64 * h, 64 * h + 64)
                    sp.dma_start(QB[0:64, a, h, :], HI[rows, 0, :]).then_inc(asm_kq, 16)
                    sp.dma_start(KL[0:64, a, h, :], LO[rows, 1, :]).then_inc(asm_kq, 16)
                    sp.dma_start(KR[0:64, a, h, :], LO[rows, 1, :]).then_inc(asm_kq, 16)

            def tail(b0, g):
                await_values(*items(b0, g))
                for h in range(2):
                    sp.dma_start(den_c[:, h, :], den_sb[64 * h:64 * h + 1, :]).then_inc(den_dma, 16)

            def tail_back(H):
                await_values((rec_done, H + 1))
                for h in range(2):
                    sp.dma_start(rec_row[h].rearrange("(p i) -> p i", p=P), rec_c[:, h, :]).then_inc(row_dma, 16)
                await_values((row_dma, H * 32 + 32))
                for h in range(2):
                    sp.dma_start(rec_b[64 * h:64 * h + 64, :],
                                 rec_row[h:h + 1, :].broadcast_to([64, HALF])).then_inc(rb_dma, 16)

            load_w1(0)
            load_tables(0, 0)
            load_wo(0, 0)
            assemble(0, 0, 0, 7)
            assemble_second(0)
            load_w1(1)
            def sync_main(it, a):
                n = it * 2 + a
                b0 = n * (NMAIN // 2) + NPREP // 2
                flat = FLAT_TAILS if is_last(n) else FLAT
                if not is_last(n):
                    load_tables(n + 1, 1 - a)
                tail(b0, flat.index(("den", 1)))
                if not is_last(n):
                    assemble(n + 1, 1 - a, b0, flat.index(("proj", 1, 3)))
                tail_back(n * 2)
                if not is_last(n):
                    assemble_second(1 - a)
                    await_values(*items(b0, flat.index(("out", 1))))
                    load_wo(n + 1, 1 - a)
                tail(b0, len(flat) - 1 - flat[::-1].index(("den", 1)))
                tail_back(n * 2 + 1)
                if not isinstance(n, int):
                    load_w1(n + 2)

            run_pairs(sp, sync_main)
            sp.wait_ge(ldp, 16 * NP)

            sp.wait_ge(yt_mm, 1)
            for sem_, per in ((asm[0], 64), (asm[1], 64), (asm_kq, 96)):
                sp.wait_ge(sem_, per * NP)
            for dst, name in ((wgi, "w_gate"), (wui, "w_up")):
                sp.dma_start(dst, io[name]).then_inc(wcv, 16)
            sp.dma_start(wdi.rearrange("p (k d) -> p k d", k=NH),
                         io["w_down"].rearrange("(k p) d -> p k d", p=P)).then_inc(wcv, 16)
            out_v = io["out"].rearrange("o (t p) d -> p (o t) d", p=P)
            for c in range(4):
                sp.wait_ge(x4_s, c + 1)
                sp.dma_start(out_v[:, 4 * c:4 * c + 4, :], x[:, 4 * c:4 * c + 4, :]).then_inc(st, 16)
            sp.wait_ge(st, 64)

        @block.tensor
        def _(pe):
            def transposes(k, src, bank0=0):
                for c in range(4):
                    pe.wait_ge(ln_x, 4 * NORM_OF[k] + c + 1)
                    for j in range(4):
                        last = nc.tensor.transpose(ps[:, bank0 + c, j * P:(j + 1) * P],
                                                   src[:, 4 * c + j, :], ident[:, :])
                    last.then_inc(tr, 1)

            def three_parts(out, a, b, start=True, stop=True):
                nc.tensor.matmul(out, a[0], b[0], start=start, stop=False)
                nc.tensor.matmul(out, a[1], b[0], start=False, stop=False)
                return nc.tensor.matmul(out, a[0], b[1], start=False, stop=stop)

            xn = wide[:, :].rearrange("p (t d) -> p t d", t=NT)
            pe.wait_ge(ld0, 16 * LD0)
            transposes(0, xn)
            pe.wait_ge(w_split, 2)
            for i in range(2):
                for c in range(4):
                    if i == 0:
                        pe.wait_ge(tr_ev, c + 1)
                    if i == 1:
                        pe.wait_ge(qk0_ev, c + 1)
                    cols = slice(W0 + 512 * c, W0 + 512 * c + 512)
                    wc = slice(P * i, P * i + P)
                    three_parts(ps[:, 4 + c, :], (w0_hi[:, wc], w0_lo[:, wc]),
                                (xT_hi[:, cols], xT_lo[:, cols])).then_inc(qk0, 1)
            pe.wait_ge(init, 1)
            wc = slice(2 * P, 3 * P)
            for g in range(NB // 4):
                if g >= 4:
                    pe.wait_ge(v0_ev, g - 3)
                for j in range(4):
                    b = 4 * g + j
                    win = [xp[:, 2 * W0 * b:2 * W0 * b + 3 * W0] for xp in (xT_hi, xT_lo)]
                    for blk in range(2):
                        o = ps[64 * blk:64 * blk + 64, g % 4, j * P:(j + 1) * P]
                        w = [v[:, W0 * blk:W0 * blk + 2 * W0] for v in win]
                        last = three_parts(o, w, (w0_hi[:, wc], w0_lo[:, wc]))
                last.then_inc(v0, 1)

            def attn0(k, on, a, first):
                if on[0]:
                    b = k
                    pe.wait_ge(qmh, b + 1)
                    pe.wait_ge(qml, b + 1)
                    if not first or a >= 2:
                        pe.wait_ge(sub0, b - 1)
                    bank = a % 2
                    nc.tensor.matmul(ps[:, bank, :], ident_b[:, :], mask0[:, 1 if (first and a == 0) else 0, :],
                                     start=True, stop=False, skip_group_check=True)
                    for blk in range(2):
                        col = b * (2 * W0) + W0 * blk
                        kh = kT[:, 0, bass.ds(col, 2 * W0)]
                        kl = kT[:, 1, bass.ds(col, 2 * W0)]
                        for g in range(G0):
                            o = ps[:, bank, g * P + 64 * blk:g * P + 64 * blk + 64]
                            qs = slice(blk * 512 + g * P, blk * 512 + g * P + P)
                            end = blk == 1 and g == G0 - 1
                            nc.tensor.matmul(o, qm_hi[:, bank, qs], kh, start=False, stop=False, skip_group_check=True)
                            nc.tensor.matmul(o, qm_lo[:, bank, qs], kh, start=False, stop=False, skip_group_check=True)
                            last = nc.tensor.matmul(o, qm_hi[:, bank, qs], kl, start=False, stop=end,
                                                    skip_group_check=True)
                    last.then_inc(s0, 1)
                if on[1]:
                    b = k - 1
                    par = (a + 1) % 2
                    pe.wait_ge(e0, b + 1)
                    if not first or a >= 3:
                        pe.wait_ge(lo0, b - 1)
                    for g in range(G0):
                        last = nc.tensor.transpose(ps[:, 2 + par, g * P:(g + 1) * P],
                                                   exp_s[:, par, g * P:(g + 1) * P], ident[:, :])
                    last.then_inc(t0, 1)
                if on[2]:
                    b = k - 2
                    par = a % 2
                    pe.wait_ge(lo0, b + 1)
                    if not first or a >= 4:
                        pe.wait_ge(om0, b - 1)
                    for g in range(G0):
                        o = ps[:, 4 + par, g * 2 * VW:(g + 1) * 2 * VW]
                        pp = [pT[:, par, i, g * P:(g + 1) * P] for i in range(2)]
                        if isinstance(b, int):
                            vv = [v[:, b, g, :, :] for v in (v_hi, v_lo)]
                        else:
                            vv = [v[:, bass.ds(b, 1), g, :, :] for v in (v_hi, v_lo)]
                        vv = [v.rearrange("p a w -> p (a w)") if isinstance(b, int)
                              else v.rearrange("p b a w -> p (b a w)") for v in vv]
                        last = three_parts(o, pp, vv)
                    last.then_inc(pv0, 1)
                if on[3]:
                    b = k - 3
                    par = (a + 1) % 2
                    pe.wait_ge(om0, b + 1)
                    if not (first and a == 3):
                        pe.wait_ge(ot0, b)
                    for blk in range(2):
                        last = nc.tensor.matmul(ps[:, 6, blk * W0:(blk + 1) * W0],
                                                om[:, par, blk * P:(blk + 1) * P], sel[:, :], start=True, stop=True)
                    last.then_inc(sel0, 1)
                if on[4] and a % 2 == 0:
                    tile = on[4][0]
                    pe.wait_ge(ot0, tile * 2 + 2)
                    if not on[4][1]:
                        pe.wait_ge(x0, tile)
                    nc.tensor.matmul(ps[:, 7, 0:P], oT[:, :], wo0[:, :], start=True, stop=True).then_inc(y0, 1)

            run_attn0(pe, attn0)

            transposes(1, xn)
            for c in range(8):
                pe.wait_ge(tr_ev, 4 + c // 2 + 1)
                if c >= 4:
                    pe.wait_ge(z_ev, c - 3)
                for j in range(2):
                    tt = 2 * c + j
                    last = nc.tensor.matmul(ps[:, 4 + c % 4, j * NZ:(j + 1) * NZ],
                                            ffT[:, tt * P:(tt + 1) * P], wz[:, :], start=True, stop=True)
                last.then_inc(z_mm, 1)
            pe.wait_ge(z_ev, 8)
            for tt in range(NT):
                nc.tensor.matmul(ps[:, 4 + tt // 4, tt % 4 * P:tt % 4 * P + P], ffT[:, tt * P:(tt + 1) * P], wbase[:, :],
                                 start=tt % 4 == 0, stop=False, skip_group_check=True)
            pe.wait_ge(zw_s, 1)
            for c in range(4):
                for j in range(4):
                    last = nc.tensor.transpose(ps[:, c, j * P:(j + 1) * P], zw[:, 4 * c + j, :], ident[:, :])
                last.then_inc(zt_mm, 1)
            for c in range(4):
                pe.wait_ge(zt_ev, c + 1)
                for j in range(4):
                    tt = 4 * c + j
                    o = ps[:, 4 + c, j * P:(j + 1) * P]
                    last = nc.tensor.matmul(o, zwT[:, tt * P:(tt + 1) * P], wlb[:, :], start=False, stop=j == 3,
                                            skip_group_check=True)
                last.then_inc(f_mm, 1)

            transposes(2, xn)
            pe.wait_ge(tr_ev, 12)

            def item(it_, a, b0, g, info):
                kind = it_[0]
                bank = MX[g % 2]
                if not banked(it_):
                    return
                if kind == "proj":
                    if it_[1:] == (0, 0):
                        pe.wait_ge(w1s, info["m"] * 2 + 2)
                    await_bank(pe, b0, g)
                    _, i, c = it_
                    cols = slice(W0 + 512 * c, W0 + 512 * c + 512)
                    last = three_parts(bank, (w1_hi[:, i, :], w1_lo[:, i, :]), (xT_hi[:, cols], xT_lo[:, cols]))
                elif kind == "value":
                    await_bank(pe, b0, g)
                    for j in range(4):
                        cols = slice(W0 + P * (4 * it_[1] + j), W0 + P * (4 * it_[1] + j) + P)
                        last = three_parts(bank[:, P * j:P * j + P], (xT_hi[:, cols], xT_lo[:, cols]),
                                           (w1_hi[:, 2, :], w1_lo[:, 2, :]))
                elif kind == "max":
                    _, h, tt, c = it_
                    if tt == 0 and c == 0:
                        pe.wait_ge(asm[h], info["m"] * 64 + 64)
                    await_bank(pe, b0, g)
                    last = nc.tensor.matmul(bank, QA[:, a, h, tt * P:(tt + 1) * P],
                                            KA[:, a, h, 512 * c:512 * c + 512], start=True, stop=True)
                elif kind == "mrow":
                    pe.wait_ge(nm_done, info["m"] * 2 + (it_[1] + 1))
                    await_bank(pe, b0, g)
                    last = nc.tensor.matmul(bank[ROW_M:ROW_M + NT, 0:P], nm[:, 1, it_[1], :], ident[:, :],
                                            start=True, stop=True)
                elif kind == "den":
                    pe.wait_ge(comb_done, info["H"] * 2 + 2)
                    await_bank(pe, b0, g)
                    cs = slice(512 * it_[1], 512 * it_[1] + 512)
                    nc.tensor.matmul(bank[0:64, :], ones1[:, :], accD[:, 0, cs], start=True, stop=True)
                    last = nc.tensor.matmul(bank[64:128, :], ones1[:, :], accD[:, 1, cs], start=True, stop=True)
                elif kind == "out":
                    if info["wo_load"] is not None:
                        pe.wait_ge(ldw, info["wo_load"] * 16 + 16)
                    pe.wait_ge(o_done, info["H"] + 1)
                    await_bank(pe, b0, g)
                    cs = slice(512 * it_[1], 512 * it_[1] + 512)
                    last = nc.tensor.matmul(bank, wo1[:, info["wo"], :], o_nrm[:, cs], start=True, stop=True)
                last.then_inc(mx_full, 1)

            def scores(a, h, Q, J):
                key = slice(J * P, J * P + P)
                for n in range(2):
                    q0 = HALF * Q + 512 * n
                    S = S1[h]
                    right = min(max(J - q0 // P, 0), 4)
                    on_diag = 0 <= J - q0 // P < 4
                    nc.tensor.matmul(S[:, 512 * n:512 * n + 512], KA[:, a, h, key], QA[:, a, h, q0:q0 + 512],
                                     start=True, stop=False, skip_group_check=True)
                    if right:
                        last = nc.tensor.matmul(S[:, 512 * n:512 * n + right * P], KR[:, a, h, key],
                                                QB[:, a, h, q0:q0 + right * P], start=False,
                                                stop=right == 4, skip_group_check=True)
                    if right < 4:
                        last = nc.tensor.matmul(S[:, 512 * n + right * P:512 * n + 512], KL[:, a, h, key],
                                                QB[:, a, h, q0 + right * P:q0 + 512], start=False,
                                                stop=not on_diag, skip_group_check=True)
                    if on_diag:
                        d = 512 * n + right * P
                        for part in range(2):
                            last = nc.tensor.matmul(S[:, d:d + P], relu_w[:, :], diag[:, a, h, part, :],
                                                    start=False, stop=part == 1, skip_group_check=True)
                return last

            def values(a, J, n):
                cs = slice(512 * n, 512 * n + 512)
                nc.tensor.matmul(PV[0:64, cs], V1[:, a, J, 0:64], Pr[:, 0, J % 2, cs],
                                 start=J == 0, stop=J == NT - 1)
                last = nc.tensor.matmul(PV[64:128, cs], V1[:, a, J, 64:128], Pr[:, 1, J % 2, cs],
                                        start=J == 0, stop=J == NT - 1)
                if n == 1:
                    last.then_inc(pv_done, 1)

            def tensor_main(it, a):
                n = it * 2 + a
                b0 = n * (NMAIN // 2) + NPREP // 2
                for s in range(2 * NT):
                    Q, J = divmod(s, NT)
                    H = it * 4 + (2 * a + Q)
                    G = H * NT + J
                    if s == 0:
                        await_items(pe, b0, -1)
                        pe.wait_ge(asm_kq, n * 96 + 96)
                        pe.wait_ge(ldt, n * 112 + 112)
                    todo = numbered(s, n)
                    info = {"m": n + 1, "H": H, "wo": (1 - a) if Q == 0 else a,
                            "wo_load": n if Q else None}
                    for h in range(2):
                        pe.wait_ge(exp_done, G * 2 + (h + 1))
                        scores(a, h, Q, J).then_inc(qk_done, 1)
                        for i_, g in todo[h]:
                            item(i_, 1 - a, b0, g, info)
                    for JJ in ([J - 1] if J else []) + ([J] if J == NT - 1 else []):
                        if JJ == 0:
                            pe.wait_ge(pv_evac, H + 1)
                        pe.wait_ge(exp_done, (H * NT + JJ) * 2 + 4)
                        for x_ in range(2):
                            values(a, JJ, x_)
                            if JJ < J:
                                for i_, g in todo[2 + x_]:
                                    item(i_, 1 - a, b0, g, info)

            for g, i_ in enumerate(PREP):
                if i_[0] != "max":
                    item(i_, 0, 0, g, {"m": 0})
                elif i_[3] == 0:
                    _, h, tt, _ = i_
                    if tt == 0:
                        pe.wait_ge(asm[h], 64)
                    await_items(pe, 0, g - 1 if PREP[g - 1][0] == "mrow" else g - 5)
                    for c in range(4):
                        last = nc.tensor.matmul(ps[:, 4 * (tt % 2) + c, :], QA[:, 0, h, tt * P:(tt + 1) * P],
                                                KA[:, 0, h, 512 * c:512 * c + 512], start=True, stop=True)
                    last.then_inc(mx_full, 4)
            pe.wait_ge(ldrow, 16 * 4)
            pe.wait_ge(init, 4)
            run_pairs(pe, tensor_main)
            b0 = NALL // 2
            info = {"H": 2 * NP, "wo": 1, "wo_load": None}
            for g, i_ in enumerate((("den", 0), ("den", 1), ("out", 0), ("out", 1))):
                item(i_, 0, b0, g, dict(info, H=2 * NP + (g == 3)))
            await_items(pe, b0, 3)
            for c in range(4):
                for j in range(4):
                    tt = 4 * c + j
                    last = nc.tensor.transpose(ps[:, c, j * P:(j + 1) * P], wide[:, tt * P:(tt + 1) * P], ident[:, :])
                last.then_inc(yt_mm, 1)

            transposes(3, xn)
            pe.wait_ge(w_split, 5)
            for c in range(4):
                pe.wait_ge(tr_ev, 12 + c + 1)
                cols = slice(W0 + 512 * c, W0 + 512 * c + 512)
                for k in range(NH):
                    u = NH * c + k
                    if u >= 2:
                        pe.wait_ge(h_s, u - 1)
                    for i, w in enumerate((wg, wu)):
                        o = ps[:, 4 + 2 * (u % 2) + i, :]
                        nc.tensor.matmul(o, w[:, k * P:(k + 1) * P], xT_hi[:, cols], start=True, stop=False)
                        last = nc.tensor.matmul(o, w[:, k * P:(k + 1) * P], xT_lo[:, cols], start=False, stop=True)
                    last.then_inc(gu_mm, 1)
                if c:
                    down(pe, nc, c - 1, ps, hid, wd, h_s, dn_mm)
            down(pe, nc, 3, ps, hid, wd, h_s, dn_mm)

        @block.scalar
        def _(act):
            def norm(k):
                for c in range(4):
                    cs = slice(512 * c, 512 * c + 512)
                    act.wait_ge(ln_c, 4 * k + c + 1)
                    nc.scalar.activation(wide[:, cs], xc_view[:, cs], ACT.Square).then_inc(ln_sq, 1)
                act.wait_ge(ln_v, k + 1)
                nc.scalar.activation(stat[:, 4, :], stat[:, 3, :], ACT.Sqrt).then_inc(ln_sd, 1)

            xc_view = QA[:, 0].rearrange("p h t -> p (h t)").bitcast(F32)

            norm(0)
            for c in range(4):
                act.wait_ge(tr, c + 1)
                nc.scalar.copy(xT_hi[:, W0 + 512 * c:W0 + 512 * c + 512], ps[:, c, :]).then_inc(hi_ev, 1)
            for i in range(2):
                dst = (qT[:, 0, :], kT[:, 0, W0:])[i]
                for c in range(4):
                    act.wait_ge(qk0, 4 * i + c + 1)
                    nc.scalar.copy(dst[:, 512 * c:512 * c + 512], ps[:, 4 + c, :]).then_inc(qk0_hi, 1)
            act.wait_ge(init, 2)
            for g in range(NB // 4):
                act.wait_ge(v0, g + 1)
                for blk in range(2):
                    rows = slice(64 * blk, 64 * blk + 64)
                    src = ps[rows, g % 4, :].rearrange("p (b g w) -> p (b g) w", b=4, g=G0)
                    dst = v_hi[rows, 4 * g:4 * g + 4, :, blk, 0:HG * D0].rearrange("p b g w -> p (b g) w")
                    last = nc.scalar.copy(dst, src)
                last.then_inc(v0_hi, 1)

            def attn0(k, on, a, first):
                if on[1]:
                    b = k - 1
                    par = (a + 1) % 2
                    act.wait_ge(t0, b + 1)
                    if not first or a >= 3:
                        act.wait_ge(pv0, b - 1)
                    nc.scalar.copy(pT[:, par, 0, :], ps[:, 2 + par, :]).then_inc(hi0, 1)
                if on[3]:
                    b = k - 3
                    par = (a + 1) % 2
                    act.wait_ge(sel0, b + 1)
                    tile, is_first = on[3]
                    if par == 0 and not is_first:
                        act.wait_ge(y0, tile)
                    nc.scalar.copy(oT[:, 64 * par:64 * par + 64], ps[:, 6, 0:64]).then_inc(ot0, 1)
                if on[0]:
                    b = k
                    act.wait_ge(sub0, b + 1)
                    if not first or a >= 2:
                        act.wait_ge(t0, b - 1)
                    nc.scalar.activation(exp_s[:, a % 2, :], sub_s[:, a % 2, :], ACT.Exp, scale=SC0).then_inc(e0, 1)

            run_attn0(act, attn0)

            norm(1)
            for c in range(4):
                act.wait_ge(tr, 4 + c + 1)
                nc.scalar.copy(ffT[:, 512 * c:512 * c + 512], ps[:, c, :]).then_inc(tr_ev, 1)
            for c in range(8):
                act.wait_ge(z_mm, c + 1)
                nc.scalar.copy(z[:, 2 * c:2 * c + 2, :].rearrange("p t n -> p (t n)"),
                               ps[:, 4 + c % 4, 0:2 * NZ]).then_inc(z_ev, 1)
            act.wait_ge(r_exp_in, 1)
            nc.scalar.activation(rt[:, 1].rearrange("p t e -> p (t e)"), rt[:, 0].rearrange("p t e -> p (t e)"),
                                 ACT.Exp).then_inc(r_exp, 1)
            for c in range(4):
                act.wait_ge(zt_mm, c + 1)
                nc.scalar.copy(zwT[:, 512 * c:512 * c + 512], ps[:, c, :]).then_inc(zt_ev, 1)

            norm(2)
            norm(3)
            for c in range(4):
                act.wait_ge(gbt, c + 1)
                nc.scalar.copy(xT_hi[:, W0 + 512 * c:W0 + 512 * c + 512],
                               ffT[:, 512 * c:512 * c + 512]).then_inc(hi_ev, 1)

            def item(it_, a, g0, g, m):
                kind = it_[0]
                bank = MX[g % 2]
                if kind == "proj":
                    _, i, c = it_
                    act.wait_ge(mx_full, g0 + 1 + g)
                    if i == 0 and c == 0 and not (isinstance(m, int) and m == 0):
                        act.wait_ge(asm[0], m * 64)
                        act.wait_ge(asm[1], m * 64)
                        act.wait_ge(asm_kq, m * 96)
                    nc.scalar.mul(HI[:, i, 512 * c:512 * c + 512], bank,
                                  0.125 if i == 0 else 1.0).then_inc(hi_done, 1)
                elif kind == "value":
                    act.wait_ge(mx_full, g0 + 1 + g)
                    c = it_[1]
                    nc.scalar.copy(V1[:, a, 4 * c:4 * c + 4, :].rearrange("p j d -> p (j d)"),
                                   bank).then_inc(mx_free[g % 2], 1)
                elif kind == "den":
                    act.wait_ge(mx_full, g0 + 1 + g)
                    cs = slice(512 * it_[1], 512 * it_[1] + 512)
                    nc.scalar.copy(den_sb[:, cs], bank).then_inc(mx_free[g % 2], 1)

            def scalar_main(it, a):
                n = it * 2 + a
                g0 = n * NMAIN + NPREP
                for s in range(2 * NT):
                    Q, J = divmod(s, NT)
                    H = it * 4 + (2 * a + Q)
                    G = H * NT + J
                    todo = numbered(s, n)
                    for h in range(2):
                        act.wait_ge(qk_done, G * 2 + (h + 2))
                        act.wait_ge(pv_done, G + 1)
                        old = (J - 2) % NT
                        Ho = H if J >= 2 else H - 1
                        if old in DVE_SUMS:
                            act.wait_ge(sum_dve, Ho * (2 * ND) + (2 * ND + 2 * DVE_SUMS.index(old) + h + 1))
                        else:
                            k = POOL_SUMS.index(max(old, 1))
                            act.wait_ge(sum_pool, Ho * (2 * len(POOL_SUMS)) + (2 * k + h + 3))
                        nc.scalar.activation(Pr[:, h, J % 2, :], S1[h], ACT.Exp).then_inc(exp_done, 1)
                        for i_, g in (todo[h] if h == 0 else todo[1] + todo[2] + todo[3]):
                            item(i_, 1 - a, g0, g, n + 1)
                    if J == NT - 1:
                        act.wait_ge(pv_done, G + 3)
                        act.wait_ge(o_done, H + 1)
                        nc.scalar.copy(o_raw[:, :], PV).then_inc(pv_evac, 1)

            for g, i_ in enumerate(PREP):
                item(i_, 0, 0, g, 0)
            run_pairs(act, scalar_main)

            norm(4)
            for c in range(4):
                act.wait_ge(tr, 12 + c + 1)
                nc.scalar.copy(xT_hi[:, W0 + 512 * c:W0 + 512 * c + 512], ps[:, c, :]).then_inc(hi_ev, 1)
            for u in range(4 * NH):
                act.wait_ge(gu_mm, u + 1)
                if u >= 2:
                    act.wait_ge(h_s, u - 1)
                nc.scalar.activation(silu[:, u % 2, :], ps[:, 4 + 2 * (u % 2), :], ACT.Silu,
                                     scale=WSCALE).then_inc(silu_s, 1)

        @block.vector
        def _(dve):
            chain = [0]

            def link(ins):
                chain[0] += 1
                ins.then_inc(dv, 1)
                dve.wait_ge(dv, chain[0])

            xcf = QA[:, 0].rearrange("p h t -> p (h t)").bitcast(F32)
            xc = xcf.rearrange("p (t d) -> p t d", t=NT)
            xn = wide[:, :].rearrange("p (t d) -> p t d", t=NT)

            def norm(k, src, dst):
                link(nc.vector.reduce_sum(stat[:, 0, :], src, AX.X))
                link(nc.vector.tensor_scalar(stat[:, 1, :], stat[:, 0, :], -1.0 / P, None, ALU.mult))
                for c in range(4):
                    tc_ = slice(4 * c, 4 * c + 4)
                    nc.vector.tensor_tensor(xc[:, tc_, :], src[:, tc_, :], bcast(stat[:, 1, tc_], 2, P),
                                            ALU.add).then_inc(ln_c, 1)
                for c in range(4):
                    tc_ = slice(4 * c, 4 * c + 4)
                    dve.wait_ge(ln_sq, 4 * k + c + 1)
                    last = nc.vector.reduce_sum(stat[:, 2, tc_], xn[:, tc_, :], AX.X)
                link(last)
                nc.vector.tensor_scalar(stat[:, 3, :], stat[:, 2, :], 1.0 / P, EPS, ALU.mult,
                                        ALU.add).then_inc(ln_v, 1)
                dve.wait_ge(ln_sd, k + 1)
                link(nc.vector.reciprocal(stat[:, 5, :], stat[:, 4, :]))
                for c in range(4):
                    tc_ = slice(4 * c, 4 * c + 4)
                    nc.vector.tensor_tensor(dst[:, tc_, :], xc[:, tc_, :], bcast(stat[:, 5, tc_], 2, P),
                                            ALU.mult).then_inc(ln_x, 1)

            dve.wait_ge(ldx, 16)
            norm(0, x[:, :, :], xn)
            dve.wait_ge(ld0, 16 * LD0)
            link(nc.vector.tensor_copy(w0_hi[:, :], w0[:, :]))
            nc.vector.tensor_tensor(w0_lo[:, :], w0[:, :], w0_hi[:, :], ALU.subtract).then_inc(w_split, 2)
            for c in range(4):
                dve.wait_ge(hi_ev, c + 1)
                cols = slice(W0 + 512 * c, W0 + 512 * c + 512)
                nc.vector.tensor_tensor(xT_lo[:, cols], ps[:, c, :], xT_hi[:, cols], ALU.subtract).then_inc(tr_ev, 1)
            for i in range(2):
                hi = (qT[:, 0, :], kT[:, 0, W0:])[i]
                lo = (qT[:, 1, :], kT[:, 1, W0:])[i]
                for c in range(4):
                    dve.wait_ge(qk0_hi, 4 * i + c + 1)
                    cs = slice(512 * c, 512 * c + 512)
                    nc.vector.tensor_tensor(lo[:, cs], ps[:, 4 + c, :], hi[:, cs], ALU.subtract).then_inc(qk0_ev, 1)
            for g in range(NB // 4):
                dve.wait_ge(v0_hi, g + 1)
                for blk in range(2):
                    rows = slice(64 * blk, 64 * blk + 64)
                    src = ps[rows, g % 4, :].rearrange("p (b g w) -> p (b g) w", b=4, g=G0)
                    cut = lambda v: v[rows, 4 * g:4 * g + 4, :, blk, 0:HG * D0].rearrange("p b g w -> p (b g) w")
                    last = nc.vector.tensor_tensor(cut(v_lo), src, cut(v_hi), ALU.subtract)
                last.then_inc(v0_ev, 1)
            dve.wait_ge(qk0_ev, 8)
            dve.wait_ge(v0_ev, NB // 4)

            hm = hmask[:, :].rearrange("p (h q) -> p h q", h=H0)

            def mask_q(b, par):
                for blk in range(2):
                    q = qT[:, 0, bass.ds(b * (2 * W0) + W0 * blk, W0)]
                    last = nc.vector.tensor_tensor(
                        qm_hi[:, par, blk * 512:blk * 512 + 512].rearrange("p (h q) -> p h q", h=H0),
                        bcast(q, 1, H0), hm, ALU.mult)
                last.then_inc(qmh, 1)

            def attn0(k, on, a, first):
                if on[0]:
                    b = k
                    par = a % 2
                    dve.wait_ge(s0, b + 1)
                    sc = ps[:, par, :].rearrange("p (n k) -> p n k", k=2 * W0)
                    if not (first and a == 0):
                        dve.wait_ge(sub0, b)
                    nc.vector.reduce_max(mx0, sc, AX.X).then_inc(m0, 1)
                    dve.wait_ge(m0, b + 1)
                    if not first or a >= 2:
                        dve.wait_ge(e0, b - 1)
                    nc.vector.tensor_tensor(sub_s[:, par, :].rearrange("p (n k) -> p n k", k=2 * W0), sc,
                                            bcast(mx0, 2, 2 * W0), ALU.subtract).then_inc(sub0, 1)
                if on[5]:
                    mask_q(k + 1, (a + 1) % 2)
                if on[1]:
                    b = k - 1
                    par = (a + 1) % 2
                    dve.wait_ge(hi0, b + 1)
                    if not first or a >= 3:
                        dve.wait_ge(pv0, b - 1)
                    nc.vector.tensor_tensor(pT[:, par, 1, :], ps[:, 2 + par, :], pT[:, par, 0, :],
                                            ALU.subtract).then_inc(lo0, 1)
                if on[2]:
                    b = k - 2
                    par = a % 2
                    dve.wait_ge(pv0, b + 1)
                    o = ps[:, 4 + par, 0:G0 * 2 * VW].rearrange("p (g a w) -> p a g w", g=G0, a=2)
                    if not (first and a == 2):
                        dve.wait_ge(om0, b)
                    rc = rc0.rearrange("p (a g) -> p a g", a=2)
                    nc.vector.reciprocal(rc, o[:, :, :, VW - 1]).then_inc(rc_s, 1)
                    t3 = om1.rearrange("p (a g w) -> p (a g) w", a=2, g=G0)
                    for blk in range(2):
                        last = nc.vector.tensor_tensor(t3[:, G0 * blk:G0 * blk + G0, :], o[:, blk, :, 0:VW - 1],
                                                       bcast(gmask[:, :], 1, G0), ALU.mult)
                    last.then_inc(om1_s, 1)
                if on[4] and a % 2 == 0:
                    tile, _ = on[4]
                    dve.wait_ge(y0, tile + 1)
                    xt = x[:, bass.ds(tile, 1), :].rearrange("p a d -> p (a d)")
                    nc.vector.tensor_tensor(xt, ps[:, 7, 0:P], xt, ALU.add).then_inc(x0, 1)

            mask_q(0, 0)
            run_attn0(dve, attn0)
            dve.wait_ge(x0, NT)

            norm(1, x[:, :, :], xn)
            dve.wait_ge(ldc, 16 * 6)
            dve.wait_ge(ln_x, 4 * 2)
            link(nc.vector.tensor_tensor(xc, x[:, :, :], bcast(bias0[:, :], 1, NT), ALU.add))
            dve.wait_ge(z_ev, 8)
            dve.wait_ge(ldc, 16 * 6)
            lg = z[:, :, NTRUE * RANK:NZ]
            link(nc.vector.reduce_max(rs[:, 0, :], lg, AX.X))
            nc.vector.tensor_tensor(rt[:, 0], lg, bcast(rs[:, 0, :], 2, NE), ALU.subtract).then_inc(r_exp_in, 1)
            dve.wait_ge(r_exp, 1)
            cur = rt[:, 1]
            for r in range(2):
                link(nc.vector.reduce_max(rs[:, 1, :], cur, AX.X))
                link(nc.vector.tensor_tensor(rt[:, 2], cur, bcast(rs[:, 1, :], 2, NE), ALU.is_equal))
                link(nc.vector.tensor_tensor(rt[:, 3], rt[:, 2], bcast(rank10[:, :], 1, NT), ALU.mult))
                link(nc.vector.reduce_max(rs[:, 2, :], rt[:, 3], AX.X))
                link(nc.vector.tensor_tensor(rt[:, 4 + r], rt[:, 3], bcast(rs[:, 2, :], 2, NE), ALU.is_equal))
                if r == 0:
                    link(nc.vector.tensor_tensor(rt[:, 6], cur, rt[:, 4], ALU.subtract))
                    link(nc.vector.tensor_tensor(rt[:, 7], rt[:, 6], rt[:, 4], ALU.subtract))
                    cur = rt[:, 7]
            link(nc.vector.tensor_tensor(rt[:, 2], rt[:, 4], rt[:, 5], ALU.add))
            link(nc.vector.tensor_tensor(rt[:, 3], rt[:, 2], rt[:, 1], ALU.mult))
            link(nc.vector.reduce_sum(rs[:, 3, :], rt[:, 3, :, 0:NTRUE], AX.X))
            link(nc.vector.tensor_scalar(rs[:, 4, :], rs[:, 3, :], 0.0, None, ALU.is_equal))
            link(nc.vector.tensor_tensor(rs[:, 5, :], rs[:, 3, :], rs[:, 4, :], ALU.add))
            link(nc.vector.reciprocal(rs[:, 6, :], rs[:, 5, :]))
            link(nc.vector.tensor_scalar(rs[:, 7, :], rs[:, 6, :], LORA_SCALE, None, ALU.mult))
            link(nc.vector.tensor_tensor(rt[:, 6], rt[:, 3], bcast(rs[:, 7, :], 2, NE), ALU.mult))
            for t8 in range(2):
                ts_ = slice(8 * t8, 8 * t8 + 8)
                last = nc.vector.tensor_tensor(
                    zw[:, ts_, :].rearrange("p t (e r) -> p t e r", e=NTRUE),
                    z[:, ts_, 0:NTRUE * RANK].rearrange("p t (e r) -> p t e r", e=NTRUE),
                    bcast(rt[:, 6, ts_, 0:NTRUE], 3, RANK), ALU.mult)
            last.then_inc(zw_s, 1)
            for c in range(4):
                dve.wait_ge(f_mm, c + 1)
                last = nc.vector.tensor_tensor(x[:, 4 * c:4 * c + 4, :].rearrange("p t d -> p (t d)"), ps[:, 4 + c, :],
                                               xc[:, 4 * c:4 * c + 4, :].rearrange("p t d -> p (t d)"), ALU.add)
            link(last)

            xn1 = ffT.rearrange("p (t d) -> p t d", t=NT)
            norm(2, x[:, :, :], xn1)
            dve.wait_ge(ln_x, 4 * 3)
            norm(3, xn1, xn)
            for c in range(4):
                dve.wait_ge(tr, 8 + c + 1)
                cs = slice(512 * c, 512 * c + 512)
                nc.vector.tensor_scalar(ffT[:, cs], ps[:, c, :], gb[:, 0:1], gb[:, 1:2], ALU.mult,
                                        ALU.add).then_inc(gbt, 1)
                dve.wait_ge(hi_ev, 4 + c + 1)
                cols = slice(W0 + 512 * c, W0 + 512 * c + 512)
                nc.vector.tensor_tensor(xT_lo[:, cols], ffT[:, cs], xT_hi[:, cols], ALU.subtract).then_inc(tr_ev, 1)
            dve.wait_ge(tr_ev, 12)

            def scale_distances(a, m, b0, h, g):
                await_items(dve, b0, g - 1)
                dve.wait_ge(ldc, 16 * 6)
                dve.wait_ge(ldt, m * 112 + 112)
                nc.vector.tensor_scalar(dist_h[:, :], dist[:, :], slope[:, a, h:h + 1], None,
                                        ALU.mult).then_inc(ts_done, 1)
                scaled = settled(dve, m * 2 + (h + 1))
                dve.wait_ge(ldc, 16 * 6)
                dve.wait_ge(ts_done, scaled)

            def maxima_done(m, b0, h, g, parts):
                await_items(dve, b0, g)
                nc.vector.reduce_max(nm[:, 0, h, :], mx2[:, h, :, 0:parts], AX.X).then_inc(nm1, 1)
                dve.wait_ge(nm1, m * 2 + (h + 1))
                nc.vector.tensor_scalar(nm[:, 1, h, :], nm[:, 0, h, :], -1.0 / M_UNIT, None,
                                        ALU.mult).then_inc(nm_done, 1)

            def item(it_, a, g0, b0, g, m, H, yhalf):
                kind = it_[0]
                bank = MX[g % 2]
                if kind == "proj":
                    _, i, c = it_
                    dve.wait_ge(hi_done, m * 8 + (4 * i + c + 1))
                    cs = slice(512 * c, 512 * c + 512)
                    nc.vector.scalar_tensor_tensor(out=LO[:, i, cs], in0=bank, scalar=0.125 if i == 0 else 1.0,
                                                   in1=HI[:, i, cs], op0=ALU.mult,
                                                   op1=ALU.subtract).then_inc(mx_free[g % 2], 1)
                elif kind == "max":
                    _, h, tt, c = it_
                    if tt == 0 and c == 0:
                        scale_distances(a, m, b0, h, g)
                    ready = settled(dve, g0 + 1 + g)
                    dve.wait_ge(ldc, 16 * 6)
                    dve.wait_ge(mx_full, ready)
                    c0 = T - P - P * tt + 512 * c
                    nc.vector.tensor_tensor_reduce(
                        out=junk[:, g % 2, :], in0=bank, in1=dist_h[:, c0:c0 + 512], scale=1.0, scalar=-3.0e38,
                        op0=ALU.add, op1=ALU.max, accum_out=mx2[:, h, tt, c:c + 1]).then_inc(mx_free[g % 2], 1)
                    if tt == NT - 1 and c == 3:
                        maxima_done(m, b0, h, g, 4)
                elif kind == "mrow":
                    h = it_[1]
                    rows = slice(ROW_M, ROW_M + NT)
                    dve.wait_ge(mx_full, g0 + 1 + g)
                    nc.vector.tensor_tensor(QB[rows, a, h, :].rearrange("p (t q) -> p t q", t=NT),
                                            bcast(bank[rows, 0:P], 1, NT), bcast(bmask[rows, :], 2, P),
                                            ALU.mult).then_inc(mx_free[g % 2], 1)
                elif kind == "recip":
                    dve.wait_ge(den_dma, H * 32 + 32)
                    nc.vector.reciprocal(rec_c[:, :, :], den_c[:, :, :]).then_inc(rec_done, 1)
                elif kind == "out":
                    dve.wait_ge(mx_full, g0 + 1 + g)
                    cs = slice(HALF * yhalf + 512 * it_[1], HALF * yhalf + 512 * it_[1] + 512)
                    nc.vector.tensor_tensor(wide[:, cs], bank, wide[:, cs], ALU.add).then_inc(mx_free[g % 2], 1)

            def vector_sum(H, J, h, part):
                k = DVE_SUMS.index(J)
                cs = slice(512 * part, 512 * part + 512)
                if part == 0:
                    dve.wait_ge(exp_done, (H * NT + J) * 2 + (h + 3))
                    if k:
                        dve.wait_ge(sum_dve, H * (2 * ND) + (2 * ND + 2 * k + h - 1))
                if k == 0:
                    last = nc.vector.tensor_copy(accD[:, h, cs], Pr[:, h, J % 2, cs])
                else:
                    last = nc.vector.tensor_tensor(accD[:, h, cs], accD[:, h, cs], Pr[:, h, J % 2, cs], ALU.add)
                if part:
                    last.then_inc(sum_dve, 1)

            def combine(H, h):
                dve.wait_ge(sum_pool, H * (2 * len(POOL_SUMS)) + (2 * len(POOL_SUMS) + 2))
                dve.wait_ge(sum_dve, H * (2 * ND) + (4 * ND))
                nc.vector.tensor_tensor(accD[:, h, :], accD[:, h, :], accP[:, h, :], ALU.add).then_inc(comb_done, 1)

            def vector_main(it, a):
                n = it * 2 + a
                g0 = n * NMAIN + NPREP
                b0 = n * (NMAIN // 2) + NPREP // 2
                for s in range(2 * NT):
                    Q, J = divmod(s, NT)
                    H = it * 4 + (2 * a + Q)
                    for k, todo in enumerate(numbered(s, n)):
                        for i_, g in todo:
                            item(i_, 1 - a, g0, b0, g, n + 1, H, 1 - Q)
                        if J == 0:
                            vector_sum(H - 1, NT - 1, k // 2, k % 2)
                        elif J - 1 in DVE_SUMS:
                            vector_sum(H, J - 1, k // 2, k % 2)
                        if J == 1 and k < 2:
                            combine(H - 1, k)

            for g, i_ in enumerate(PREP):
                if i_[0] != "max":
                    item(i_, 0, 0, 0, g, 0, 0, 0)
                elif i_[3] == 0:
                    _, h, tt, _ = i_
                    if tt == 0:
                        scale_distances(0, 0, 0, h, g)
                    dve.wait_ge(mx_full, g + 4)
                    await_items(dve, 0, g - 5)
                    for u in range(2):
                        c0 = T - P - P * tt + 1024 * u
                        bank0 = 4 * (tt % 2) + 2 * u
                        nc.vector.tensor_tensor_reduce(
                            out=(QA, KA)[tt % 2][:, 1, u, :].bitcast(F32),
                            in0=ps[:, bank0:bank0 + 2, :].rearrange("p b n -> p (b n)"),
                            in1=dist_h[:, c0:c0 + 1024], scale=1.0, scalar=-3.0e38,
                            op0=ALU.add, op1=ALU.max, accum_out=mx2[:, h, tt, u:u + 1]).then_inc(mx_free[u], 2)
                    if tt == NT - 1:
                        maxima_done(0, 0, h, g + 3, 2)
            dve.wait_ge(init, 4)
            run_pairs(dve, vector_main)
            g0 = NALL
            for k in range(4):
                vector_sum(2 * NP - 1, NT - 1, k // 2, k % 2)
            for h in range(2):
                combine(2 * NP - 1, h)
            dve.wait_ge(pv_evac, 2 * NP + 1)
            for g in range(2):
                dve.wait_ge(mx_full, g0 + 1 + g)
                cs = slice(512 * g, 512 * g + 512)
                nc.vector.reciprocal(rec_b[:, cs], MX[g]).then_inc(mx_free[g], 1)
                dve.wait_ge(mx_free[g], g0 // 2 + 2)
                nc.vector.tensor_tensor(o_nrm[:, cs], o_raw[:, cs], rec_b[:, cs], ALU.mult).then_inc(o_done, 1)
            for g in range(2):
                item(("out", g), 0, g0, g0 // 2, g + 2, 0, 2 * NP, 1)
            for c in range(4):
                dve.wait_ge(yt_mm, c + 1)
                xs = x[:, 4 * c:4 * c + 4, :].rearrange("p t d -> p (t d)")
                last = nc.vector.tensor_tensor(xs, ps[:, c, :], xs, ALU.add)
            link(last)

            for h in range(2):
                dve.wait_ge(asm[h], 64 * NP)
            dve.wait_ge(ldt, 112 * NP)
            norm(4, x[:, :, :], xn)
            dve.wait_ge(wcv, 48)
            for dst, src in ((wg, wgi), (wu, wui), (wd.rearrange("p k d -> p (k d)"), wdi)):
                nc.vector.tensor_copy(dst, src).then_inc(w_split, 1)
            for c in range(4):
                dve.wait_ge(hi_ev, 8 + c + 1)
                cols = slice(W0 + 512 * c, W0 + 512 * c + 512)
                nc.vector.tensor_tensor(xT_lo[:, cols], ps[:, c, :], xT_hi[:, cols], ALU.subtract).then_inc(tr_ev, 1)
            for c in range(4):
                for k in range(NH):
                    u = NH * c + k
                    dve.wait_ge(silu_s, u + 1)
                    nc.vector.scalar_tensor_tensor(out=hid[:, k, 512 * c:512 * c + 512],
                                                   in0=ps[:, 5 + 2 * (u % 2), :], scalar=WSCALE,
                                                   in1=silu[:, u % 2, :], op0=ALU.mult, op1=ALU.mult).then_inc(h_s, 1)
                if c:
                    residual(dve, nc, c - 1, ps, x, dn_mm, x4_s)
            residual(dve, nc, 3, ps, x, dn_mm, x4_s)

        @block.gpsimd
        def _(pool):
            nc.gpsimd.memset(xT_hi[:, 0:W0], 0.0)
            nc.gpsimd.memset(kT[:, :, 0:W0], 0.0)
            nc.gpsimd.memset(xT_lo[:, 0:W0], 0.0).then_inc(init, 1)
            pool.wait_ge(init, 1)
            nc.gpsimd.memset(v_hi.rearrange("p b g a w -> p (b g a w)"), 0.0)
            nc.gpsimd.memset(v_lo.rearrange("p b g a w -> p (b g a w)"), 0.0).then_inc(xb_s, 1)
            pool.wait_ge(xb_s, 1)
            nc.gpsimd.memset(v_hi[0:64, :, :, 0, VW - 1], 1.0).then_inc(xb_s, 1)
            pool.wait_ge(xb_s, 2)
            nc.gpsimd.memset(v_hi[64:128, :, :, 1, VW - 1], 1.0).then_inc(init, 1)
            pool.wait_ge(init, 2)

            hm = hmask[:, :].rearrange("p (h q) -> p h q", h=H0)
            pool.wait_ge(ld0, 16 * LD0)
            pool.wait_ge(qk0_ev, 4)

            def mask_q(b, par):
                for blk in range(2):
                    q = qT[:, 1, bass.ds(b * (2 * W0) + W0 * blk, W0)]
                    last = nc.gpsimd.tensor_tensor(
                        qm_lo[:, par, blk * 512:blk * 512 + 512].rearrange("p (h q) -> p h q", h=H0),
                        bcast(q, 1, H0), hm, ALU.mult)
                last.then_inc(qml, 1)

            def attn0(k, on, a, first):
                if on[5]:
                    if not first or a >= 1:
                        pool.wait_ge(s0, k)
                    mask_q(k + 1, (a + 1) % 2)
                if on[3]:
                    b = k - 3
                    pool.wait_ge(rc_s, b + 1)
                    pool.wait_ge(om1_s, b + 1)
                    if not first or a >= 5:
                        pool.wait_ge(sel0, b - 1)
                    nc.gpsimd.tensor_tensor(om[:, (a + 1) % 2, :].rearrange("p (n w) -> p n w", n=2 * G0),
                                            om1.rearrange("p (n w) -> p n w", n=2 * G0),
                                            bcast(rc0, 2, HG * D0), ALU.mult).then_inc(om0, 1)

            mask_q(0, 0)
            run_attn0(pool, attn0)

            flat = lambda K, rows: K[rows, :, :, :].rearrange("p a h t -> p (a h t)").bitcast(F32)
            pool.wait_ge(om0, NB)
            for K in (KL, KR):
                nc.gpsimd.memset(flat(K, slice(64, 128)), 0.0).then_inc(set_up, 1)
            pool.wait_ge(set_up, 2)
            for K in (KL, KR):
                nc.gpsimd.memset(flat(K, slice(ROW_M, ROW_M + NT)), M_UNIT_TWICE).then_inc(set_up, 1)
            pool.wait_ge(set_up, 4)
            pool.wait_ge(pv0, NB)
            nc.gpsimd.memset(arena[:, 12288:16384], 1.0)
            nc.gpsimd.memset(wo1[:, :, :], 0.0)
            nc.gpsimd.memset(ones1[:, :], 1.0)
            nc.gpsimd.memset(o_raw[:, :], 0.0).then_inc(pv_evac, 1)
            pool.wait_ge(pv_evac, 1)
            pool.wait_ge(f_mm, 4)
            nc.gpsimd.memset(flat(QB, slice(64, 128)), 0.0).then_inc(init, 1)
            pool.wait_ge(init, 3)

            def split(m):
                loaded = settled(pool, m * 16 + 16)
                pool.wait_ge(w1c, 1)
                pool.wait_ge(ldp, loaded)
                nc.gpsimd.tensor_copy(w1_hi[:, :, :], w1[:, :, :]).then_inc(w1s, 1)
                pool.wait_ge(w1s, m * 2 + 1)
                nc.gpsimd.tensor_tensor(w1_lo[:, :, :], w1[:, :, :], w1_hi[:, :, :], ALU.subtract).then_inc(w1s, 1)
                pool.wait_ge(w1s, m * 2 + 2)
                nc.gpsimd.memset(tick[:, :], 0.0).then_inc(w1c, 2)

            def pool_main(it, a):
                n = it * 2 + a
                if not is_last(n):
                    await_items(pool, n * (NMAIN // 2) + NPREP // 2, -1)
                    split(n + 1)
                for Q in range(2):
                    H = it * 4 + (2 * a + Q)
                    for k, J in enumerate(POOL_SUMS):
                        for h in range(2):
                            pool.wait_ge(exp_done, (H * NT + J) * 2 + (h + 3))
                            own = H * (2 * len(POOL_SUMS))
                            if k == 0:
                                pool.wait_ge(comb_done, H * 2 + (h + 1))
                                nc.gpsimd.tensor_tensor(accP[:, h, :], Pr[:, h, 0, :], Pr[:, h, 1, :],
                                                        ALU.add).then_inc(sum_pool, 1)
                            else:
                                pool.wait_ge(sum_pool, own + (2 * k + h + 1))
                                nc.gpsimd.tensor_tensor(accP[:, h, :], accP[:, h, :], Pr[:, h, J % 2, :],
                                                        ALU.add).then_inc(sum_pool, 1)
                        if J == SCALE_AFTER:
                            pool.wait_ge(rb_dma, H * 32 + 32)
                            pool.wait_ge(pv_evac, H + 1)
                            nc.gpsimd.tensor_tensor(o_nrm[:, :], o_raw[:, :], rec_b[:, :],
                                                    ALU.mult).then_inc(o_done, 1)

            nc.gpsimd.memset(tick[:, :], 0.0).then_inc(qk_done, 1)
            pool.wait_ge(qk_done, 1)
            for s_, v in ((pv_done, 2), (sum_pool, 2), (sum_dve, 2 * ND - 2), (mx_free[0], 1), (mx_free[1], 1),
                          (w1c, 1)):
                nc.gpsimd.memset(tick[:, :], 0.0).then_inc(s_, v)
                pool.wait_ge(s_, v)
            split(0)
            nc.gpsimd.memset(Pr[:, :, 1, :], 1.0).then_inc(set_up, 1)
            pool.wait_ge(set_up, 5)
            pool.wait_ge(tr, 12)
            nc.gpsimd.memset(wide[:, :], 0.0).then_inc(init, 1)
            pool.wait_ge(init, 4)
            nc.gpsimd.memset(tick[:, :], 0.0).then_inc(exp_done, 2)
            pool.wait_ge(exp_done, 2)
            run_pairs(pool, pool_main)


def settled(eng, value):
    if not isinstance(value, int):
        eng.compute_val(value)
    return value


def down(pe, nc, c, ps, hid, wd, h_s, dn_mm):
    pe.wait_ge(h_s, NH * (c + 1))
    for j in range(4):
        t = 4 * c + j
        for k in range(NH):
            last = nc.tensor.matmul(ps[:, c, j * P:(j + 1) * P], hid[:, k, t * P:(t + 1) * P], wd[:, k, :],
                                    start=k == 0, stop=k == NH - 1)
    last.then_inc(dn_mm, 1)


def residual(dve, nc, c, ps, x, dn_mm, x4_s):
    dve.wait_ge(dn_mm, c + 1)
    xs = x[:, 4 * c:4 * c + 4, :].rearrange("p t d -> p (t d)")
    nc.vector.scalar_tensor_tensor(out=xs, in0=ps[:, c, :], scalar=WSCALE, in1=xs, op0=ALU.mult,
                                   op1=ALU.add).then_inc(x4_s, 1)


def run_pairs(eng, main):
    with eng.Fori(0, NP // 2 - 1) as it:
        for a in range(2):
            main(it, a)
    for a in range(2):
        main(NP // 2 - 1, a)


def run_attn0(eng, step):
    last = 3
    steady = 6

    def on(k, base=None):
        flags = []
        for j in range(5):
            b = k - min(j, 3)
            live = 0 <= b < NB
            if base is not None:
                live = True
            if live and j >= 3:
                tile = b // 2 if base is None else base + (b // 2)
                flags.append((tile, base is None and tile == 0))
            else:
                flags.append(live)
        flags.append(base is not None or k + 1 < NB)
        return flags

    for k in range(steady):
        step(k, on(k), k, True)
    n = (NB - steady) // 2 - 1
    with eng.Fori(0, n) as i:
        for s in range(2):
            flags = on(steady + s, i)
            step(i * 2 + (steady + s), flags, (steady + s), False)
    for k in range(NB - 2, NB + last):
        step(k, on(k), k, False)


def constants():
    c = {}
    c["ident"] = np.eye(P, dtype=np.float32)
    c["ident_b"] = bf16_bits(np.eye(P, dtype=np.float32))
    d = np.arange(P)
    c["hmask"] = np.repeat((d[:, None] // D0 == np.arange(H0)[None, :]), W0, axis=1).astype(np.float16)
    c["gmask"] = (d[:, None] // W0 == np.arange(HG * D0)[None, :] // D0).astype(np.float32)
    c["sel"] = (d[:, None] % W0 == np.arange(W0)[None, :]).astype(np.float32)
    ti, tj = (d % W0)[:, None], np.arange(2 * W0)[None, :]
    band = (tj >= ti + 1) & (tj <= ti + W0)
    first = band & (tj >= W0)
    mask = np.zeros((P, 2, G0, 2, 2 * W0), np.float32)
    mask[:, :] = np.where(band, 0.0, -1e30)[:, None, None, None, :]
    mask[:, 1, :, 0, :] = np.where(first, 0.0, -1e30)[:, None, :]
    c["mask0"] = bf16_bits(mask.reshape(P, 2, 512))
    c["rank10"] = np.tile(NE - np.arange(NE, dtype=np.float32), (P, 1))
    col = np.arange(TW)
    c["dist"] = (-np.abs(d[:, None] - col[None, :] + (T - P))).astype(np.float16)
    c["relu_w"] = np.maximum(d[None, :] - d[:, None], 0).astype(np.float16)
    bm = np.zeros((P, NT), np.float32)
    bm[ROW_M:ROW_M + NT] = np.eye(NT)
    c["bmask"] = bm
    n_seq = np.arange(H1, 0, -1).astype(np.float32)
    slopes = (np.float32(2.0) ** (np.float32(-8.0) / n_seq)).astype(np.float32).astype(np.float64)

    def parts(v, n):
        out = []
        for _ in range(n):
            p = v.astype(np.float16).astype(np.float64)
            out.append(p)
            v = v - p
        return np.stack(out)

    pos = np.arange(T) - CENTRE
    rows = np.zeros((NA, T))
    rows[0:3] = pos / 1024.0
    rows[3:6] = 1.0
    c["pos_rows"] = rows.astype(np.float16)
    left = np.zeros((H1, NA, T))
    for h in range(H1):
        left[h, 0:3] = parts(-slopes[h:h + 1] * 1024.0, 3)
        left[h, 3:6] = parts(slopes[h] * pos, 3)
    c["alibi_l"] = left.reshape(NP, 2, NA, T).astype(np.float16)
    c["alibi_r"] = -c["alibi_l"]
    dg = np.zeros((H1, P, 2, P))
    for h in range(H1):
        for i, p in enumerate(parts(-2.0 * slopes[h:h + 1], 2)):
            dg[h, :, i, :] = np.eye(P) * p
    c["diag"] = dg.reshape(NP, 2, P, 2, P).astype(np.float16)
    c["slope"] = np.tile(slopes.astype(np.float32).reshape(NP, 1, 2), (1, P, 1))
    return c


def bf16_bits(a):
    return (np.ascontiguousarray(a, np.float32).view(np.uint32) >> 16).astype(np.uint16)


def layout(v):
    pairs = lambda w: w.reshape(P, NP, P).transpose(1, 0, 2)
    out = {
        "x": v["L0_attn_x"], "w_qkv": v["L0_attn_w_qkv"], "w_out": v["L0_attn_w_out"],
        "wz": np.concatenate([v["L0_ffn_lora_A"].reshape(NTRUE * RANK, P), v["L0_ffn_gate_w"]]).T,
        "wbase": v["L0_ffn_base_w"].T,
        "wlb": v["L0_ffn_lora_B"].transpose(0, 2, 1).reshape(NTRUE * RANK, P),
        "bias0": np.broadcast_to(v["L0_ffn_base_b"], (P, P)),
        "gb": np.stack([v["L1_attn_ln_gamma"], v["L1_attn_ln_beta"]], axis=1),
        "w1": np.stack([pairs(v["L1_attn_Wq"]), pairs(v["L1_attn_Wk"]), pairs(v["L1_attn_Wv"])], axis=2),
        "wo1": v["L1_attn_Wo"].reshape(NP, P, P),
        "w_gate": v["L1_ffn_w_gate"].T, "w_up": v["L1_ffn_w_up"].T, "w_down": v["L1_ffn_w_down"].T,
    }
    return {k: np.ascontiguousarray(a) for k, a in out.items()}


def kernel(**inputs):
    import concourse.bacc as _bacc
    from concourse.bass_utils import run_bass_kernel_spmd as _run

    nc = _bacc.Bacc("TRN2", target_bir_lowering=False, num_devices=1)
    arrays = layout({k: np.asarray(a) for k, a in inputs.items()})
    arrays.update(constants())
    io = {n: nc.dram_tensor(f"in_{n}", a.shape, mybir.dt.from_np(a.dtype), kind="ExternalInput").ap()
          for n, a in arrays.items()}
    io["out"] = nc.dram_tensor("out", (1, T, P), F32, kind="ExternalOutput").ap()
    build(nc, io)
    r = _run(nc, [{f"in_{n}": a for n, a in arrays.items()}], core_ids=[0])
    return r.results[0]["out"]
```
